# Optimizing a Trainium2 kernel written in Bass

```python
import numpy as np
import jax
import jax.numpy as jnp

def _softmax(x, axis=-1):
    return jax.nn.softmax(x, axis=axis)

def _gelu(x):
    return jax.nn.gelu(x, approximate=True)

def _silu(x):
    return jax.nn.silu(x)

def _sigmoid(x):
    return jax.nn.sigmoid(x)

def _layernorm(x, axis=-1, eps=1e-05):
    m = jnp.mean(x, axis=axis, keepdims=True)
    v = jnp.var(x, axis=axis, keepdims=True)
    return (x - m) / jnp.sqrt(v + eps)

def _scatter_add(tgt, idx, src, axis=0):
    return tgt.at[idx].add(src)

def _segment_sum(src, seg, n):
    return jax.ops.segment_sum(src, seg, n)
kernel_name = 'mk_gnn_preln_d4_gnn_r16_25f08c'

def setup_inputs(seed: int=0):
    np.random.seed(seed)
    _w = jnp.asarray

    def _rec_inputs():
        import jax
        import jax.numpy as jnp
        _gk = jax.random.key(seed)
        x = -0.0002117 + 1 * jax.random.normal(jax.random.fold_in(_gk, 1), (6250, 256), jnp.float32)
        src = jax.random.randint(jax.random.fold_in(_gk, 2), (100000,), 0, 6250, jnp.int32)
        dst = jax.random.randint(jax.random.fold_in(_gk, 3), (100000,), 0, 6250, jnp.int32)
        _o = jnp.argsort(dst, stable=True)
        src = src[_o]
        dst = dst[_o]
        edge_attr_128 = 9.41057e-06 + 1 * jax.random.normal(jax.random.fold_in(_gk, 12), (100000, 128), jnp.float32)
        edge_type_16 = jax.random.randint(jax.random.fold_in(_gk, 14), (100000,), 0, 16, jnp.int32)
        edge_weight = jax.random.uniform(jax.random.fold_in(_gk, 15), (100000,), jnp.float32, 0.0, 1)
        node_vec1 = jax.random.uniform(jax.random.fold_in(_gk, 16), (6250, 1), jnp.float32, 0.0, 0.999973)
        node_vec1_n2 = jax.random.uniform(jax.random.fold_in(_gk, 17), (6250, 1), jnp.float32, 0.0, 0.999973)
        return (x, src, dst, edge_attr_128, edge_type_16, edge_weight, node_vec1, node_vec1_n2)
    x, src, dst, edge_attr_128, edge_type_16, edge_weight, node_vec1, node_vec1_n2 = _rec_inputs()

    def _L0_gnn_setup():
        import jax, jax.numpy as jnp
        import numpy as np
        N_NODES = 6250
        N_EDGES = 200000
        D = 256
        key = jax.random.key(seed)
        k1, k2, k3, k4, k5, k6 = jax.random.split(key, 6)
        x = jax.random.normal(k1, (N_NODES, D), dtype=jnp.float32)
        edge_row = jax.random.randint(k2, (N_EDGES,), 0, N_NODES, dtype=jnp.int32)
        edge_col = jax.random.randint(k3, (N_EDGES,), 0, N_NODES, dtype=jnp.int32)
        edge_val = jax.random.uniform(k4, (N_EDGES,), dtype=jnp.float32)
        stdv = 1.0 / np.sqrt(D)
        weight = jax.random.uniform(k5, (D, D), dtype=jnp.float32, minval=-stdv, maxval=stdv)
        b = jax.random.uniform(k6, (D,), dtype=jnp.float32, minval=-stdv, maxval=stdv)
        return {'x': x, 'edge_row': edge_row, 'edge_col': edge_col, 'edge_val': edge_val, 'weight': weight, 'b': b}
    _L0_gnn_all = _L0_gnn_setup()
    _L0_gnn_in = {k: v for k, v in _L0_gnn_all.items() if k in ('weight', 'b')}
    del _L0_gnn_all

    def _L1_gnn_setup():
        import jax, jax.numpy as jnp
        import numpy as np
        NUM_NODES = 3125
        NUM_EDGES = 100000
        NODE_DIM = 256
        EDGE_DIM = 128
        MAX_IN_DEGREE = 512
        MAX_OUT_DEGREE = 512
        key = jax.random.key(seed)
        ks = jax.random.split(key, 12)
        x = jax.random.normal(ks[0], (NUM_NODES, NODE_DIM), dtype=jnp.float32)
        edge_index = jax.random.randint(ks[1], (2, NUM_EDGES), 0, NUM_NODES, dtype=jnp.int64 if jax.config.read('jax_enable_x64') else jnp.int32)
        edge_attr = jax.random.normal(ks[2], (NUM_EDGES, EDGE_DIM), dtype=jnp.float32)
        voronoi_values = jax.random.uniform(ks[3], (NUM_NODES, 1), dtype=jnp.float32)
        centralities = jax.random.uniform(ks[4], (NUM_NODES, 1), dtype=jnp.float32)
        z_in = jax.random.normal(ks[5], (MAX_IN_DEGREE, NODE_DIM), dtype=jnp.float32)
        z_out = jax.random.normal(ks[6], (MAX_OUT_DEGREE, NODE_DIM), dtype=jnp.float32)
        W_cent = jax.random.normal(ks[7], (1, NODE_DIM), dtype=jnp.float32) * 0.5
        b_cent = jnp.zeros((NODE_DIM,), dtype=jnp.float32)
        W_vor = jax.random.normal(ks[8], (1, NODE_DIM), dtype=jnp.float32) * 0.5
        b_vor = jnp.zeros((NODE_DIM,), dtype=jnp.float32)
        W_sum = jax.random.normal(ks[9], (EDGE_DIM, NODE_DIM), dtype=jnp.float32) * (1.0 / np.sqrt(EDGE_DIM))
        b_sum = jnp.zeros((NODE_DIM,), dtype=jnp.float32)
        return {'x': x, 'edge_index': edge_index, 'edge_attr': edge_attr, 'voronoi_values': voronoi_values, 'centralities': centralities, 'z_in': z_in, 'z_out': z_out, 'W_cent': W_cent, 'b_cent': b_cent, 'W_vor': W_vor, 'b_vor': b_vor, 'W_sum': W_sum, 'b_sum': b_sum}
    _L1_gnn_all = _L1_gnn_setup()
    _L1_gnn_in = {k: v for k, v in _L1_gnn_all.items() if k in ('z_in', 'z_out', 'W_cent', 'b_cent', 'W_vor', 'b_vor', 'W_sum', 'b_sum')}
    del _L1_gnn_all

    def _L2_gnn_setup():
        import jax, jax.numpy as jnp
        import numpy as np
        N = 625
        E = 20000
        D = 256
        EPS = 1e-05

        def layer_norm(x, g, b):
            mu = jnp.mean(x, axis=-1, keepdims=True)
            var = jnp.mean(jnp.square(x - mu), axis=-1, keepdims=True)
            return (x - mu) * jax.lax.rsqrt(var + EPS) * g + b

        def linear(x, w, b):
            return x @ w + b
        key = jax.random.key(seed)
        ks = jax.random.split(key, 20)
        s = 1.0 / np.sqrt(D)
        inp = {'x': jax.random.normal(ks[0], (N, D), jnp.float32), 'edge_index': jax.random.randint(ks[1], (2, E), 0, N, jnp.int64), 'edge_weight': jax.random.normal(ks[2], (E,), jnp.float32), 'wq': jax.random.normal(ks[3], (D, D), jnp.float32) * s, 'bq': jnp.zeros((D,), jnp.float32), 'wk': jax.random.normal(ks[4], (D, D), jnp.float32) * s, 'bk': jnp.zeros((D,), jnp.float32), 'wv': jax.random.normal(ks[5], (D, D), jnp.float32) * s, 'bv': jnp.zeros((D,), jnp.float32), 'ws': jax.random.normal(ks[6], (D, D), jnp.float32) * s, 'bs': jnp.zeros((D,), jnp.float32), 'we': jax.random.normal(ks[7], (1, 1), jnp.float32), 'be': jnp.zeros((1,), jnp.float32), 'g1': jnp.ones((D,), jnp.float32), 'b1': jnp.zeros((D,), jnp.float32), 'g2': jnp.ones((D,), jnp.float32), 'b2': jnp.zeros((D,), jnp.float32), 'w_ff1': jax.random.normal(ks[8], (D, 2 * D), jnp.float32) * s, 'b_ff1': jnp.zeros((2 * D,), jnp.float32), 'w_ff2': jax.random.normal(ks[9], (2 * D, D), jnp.float32) * (1.0 / np.sqrt(2 * D)), 'b_ff2': jnp.zeros((D,), jnp.float32)}
        return inp
    _L2_gnn_all = _L2_gnn_setup()
    _L2_gnn_in = {k: v for k, v in _L2_gnn_all.items() if k in ('wq', 'bq', 'wk', 'bk', 'wv', 'bv', 'ws', 'bs', 'we', 'be', 'g1', 'b1', 'g2', 'b2', 'w_ff1', 'b_ff1', 'w_ff2', 'b_ff2')}
    del _L2_gnn_all

    def _L3_gnn_setup():
        import jax, jax.numpy as jnp
        import numpy as np
        N_NODES = 3125
        N_EDGES = 50000
        HDIM = 256
        NUMRELS = 16

        def _gru_cell(x, h, w_ih, w_hh, b_ih, b_hh):
            gi = x @ w_ih.T + b_ih
            gh = h @ w_hh.T + b_hh
            i_r, i_z, i_n = jnp.split(gi, 3, axis=-1)
            h_r, h_z, h_n = jnp.split(gh, 3, axis=-1)
            r = jax.nn.sigmoid(i_r + h_r)
            z = jax.nn.sigmoid(i_z + h_z)
            n = jnp.tanh(i_n + r * h_n)
            return (1.0 - z) * n + z * h
        key = jax.random.key(seed)
        ks = jax.random.split(key, 9)
        h = jax.random.normal(ks[0], (N_NODES, HDIM), dtype=jnp.float32)
        relvectors = jax.random.normal(ks[1], (NUMRELS, HDIM), dtype=jnp.float32)
        s = 1.0 / np.sqrt(HDIM)
        w_ih = jax.random.uniform(ks[2], (3 * HDIM, HDIM), minval=-s, maxval=s, dtype=jnp.float32)
        w_hh = jax.random.uniform(ks[3], (3 * HDIM, HDIM), minval=-s, maxval=s, dtype=jnp.float32)
        b_ih = jax.random.uniform(ks[4], (3 * HDIM,), minval=-s, maxval=s, dtype=jnp.float32)
        b_hh = jax.random.uniform(ks[5], (3 * HDIM,), minval=-s, maxval=s, dtype=jnp.float32)
        edge_src = jax.random.randint(ks[6], (N_EDGES,), 0, N_NODES, dtype=jnp.int32)
        edge_dst = jax.random.randint(ks[7], (N_EDGES,), 0, N_NODES, dtype=jnp.int32)
        edge_rel = jax.random.randint(ks[8], (N_EDGES,), 0, NUMRELS, dtype=jnp.int32)
        return {'h': h, 'relvectors': relvectors, 'w_ih': w_ih, 'w_hh': w_hh, 'b_ih': b_ih, 'b_hh': b_hh, 'edge_src': edge_src, 'edge_dst': edge_dst, 'edge_rel': edge_rel}
    _L3_gnn_all = _L3_gnn_setup()
    _L3_gnn_in = {k: v for k, v in _L3_gnn_all.items() if k in ('relvectors', 'w_ih', 'w_hh', 'b_ih', 'b_hh')}
    del _L3_gnn_all
    return {'x': x, 'src': src, 'dst': dst, 'edge_attr_128': edge_attr_128, 'edge_type_16': edge_type_16, 'edge_weight': edge_weight, 'node_vec1': node_vec1, 'node_vec1_n2': node_vec1_n2, 'L0_gnn_weight': _L0_gnn_in['weight'], 'L0_gnn_b': _L0_gnn_in['b'], 'L1_gnn_z_in': _L1_gnn_in['z_in'], 'L1_gnn_z_out': _L1_gnn_in['z_out'], 'L1_gnn_W_cent': _L1_gnn_in['W_cent'], 'L1_gnn_b_cent': _L1_gnn_in['b_cent'], 'L1_gnn_W_vor': _L1_gnn_in['W_vor'], 'L1_gnn_b_vor': _L1_gnn_in['b_vor'], 'L1_gnn_W_sum': _L1_gnn_in['W_sum'], 'L1_gnn_b_sum': _L1_gnn_in['b_sum'], 'L2_gnn_wq': _L2_gnn_in['wq'], 'L2_gnn_bq': _L2_gnn_in['bq'], 'L2_gnn_wk': _L2_gnn_in['wk'], 'L2_gnn_bk': _L2_gnn_in['bk'], 'L2_gnn_wv': _L2_gnn_in['wv'], 'L2_gnn_bv': _L2_gnn_in['bv'], 'L2_gnn_ws': _L2_gnn_in['ws'], 'L2_gnn_bs': _L2_gnn_in['bs'], 'L2_gnn_we': _L2_gnn_in['we'], 'L2_gnn_be': _L2_gnn_in['be'], 'L2_gnn_g1': _L2_gnn_in['g1'], 'L2_gnn_b1': _L2_gnn_in['b1'], 'L2_gnn_g2': _L2_gnn_in['g2'], 'L2_gnn_b2': _L2_gnn_in['b2'], 'L2_gnn_w_ff1': _L2_gnn_in['w_ff1'], 'L2_gnn_b_ff1': _L2_gnn_in['b_ff1'], 'L2_gnn_w_ff2': _L2_gnn_in['w_ff2'], 'L2_gnn_b_ff2': _L2_gnn_in['b_ff2'], 'L3_gnn_relvectors': _L3_gnn_in['relvectors'], 'L3_gnn_w_ih': _L3_gnn_in['w_ih'], 'L3_gnn_w_hh': _L3_gnn_in['w_hh'], 'L3_gnn_b_ih': _L3_gnn_in['b_ih'], 'L3_gnn_b_hh': _L3_gnn_in['b_hh']}

def reference(x, src, dst, edge_attr_128, edge_type_16, edge_weight, node_vec1, node_vec1_n2, L0_gnn_weight, L0_gnn_b, L1_gnn_z_in, L1_gnn_z_out, L1_gnn_W_cent, L1_gnn_b_cent, L1_gnn_W_vor, L1_gnn_b_vor, L1_gnn_W_sum, L1_gnn_b_sum, L2_gnn_wq, L2_gnn_bq, L2_gnn_wk, L2_gnn_bk, L2_gnn_wv, L2_gnn_bv, L2_gnn_ws, L2_gnn_bs, L2_gnn_we, L2_gnn_be, L2_gnn_g1, L2_gnn_b1, L2_gnn_g2, L2_gnn_b2, L2_gnn_w_ff1, L2_gnn_b_ff1, L2_gnn_w_ff2, L2_gnn_b_ff2, L3_gnn_relvectors, L3_gnn_w_ih, L3_gnn_w_hh, L3_gnn_b_ih, L3_gnn_b_hh):
    import jax
    import jax.numpy as jnp

    def _L0_gnn_ref(x, edge_row, edge_col, edge_val, weight, b):
        import jax, jax.numpy as jnp
        import numpy as np
        N_NODES = 6250
        N_EDGES = 200000
        D = 256
        support = x @ weight
        msgs = support[edge_col] * edge_val[:, None]
        out = jax.ops.segment_sum(msgs, edge_row, num_segments=N_NODES)
        return out + b

    def _L1_gnn_ref(x, edge_index, edge_attr, voronoi_values, centralities, z_in, z_out, W_cent, b_cent, W_vor, b_vor, W_sum, b_sum):
        import jax, jax.numpy as jnp
        import numpy as np
        NUM_NODES = 3125
        NUM_EDGES = 100000
        NODE_DIM = 256
        EDGE_DIM = 128
        MAX_IN_DEGREE = 512
        MAX_OUT_DEGREE = 512
        num_nodes = x.shape[0]
        src = edge_index[0]
        dst = edge_index[1]
        ones = jnp.ones_like(src, dtype=jnp.int32)
        in_deg = jnp.minimum(jax.ops.segment_sum(ones, dst, num_segments=num_nodes), MAX_IN_DEGREE - 1)
        out_deg = jnp.minimum(jax.ops.segment_sum(ones, src, num_segments=num_nodes), MAX_OUT_DEGREE - 1)
        edge_proj = edge_attr @ W_sum + b_sum
        sum3d = jax.ops.segment_sum(edge_proj, src, num_segments=num_nodes)
        cent_term = jax.nn.sigmoid(centralities @ W_cent + b_cent)
        vor_term = jax.nn.sigmoid(voronoi_values @ W_vor + b_vor)
        return x + z_in[in_deg] + z_out[out_deg] + cent_term + vor_term + sum3d

    def _L2_gnn_ref(x, edge_index, edge_weight, wq, bq, wk, bk, wv, bv, ws, bs, we, be, g1, b1, g2, b2, w_ff1, b_ff1, w_ff2, b_ff2):
        import jax, jax.numpy as jnp
        import numpy as np
        N = 625
        E = 20000
        D = 256
        EPS = 1e-05

        def layer_norm(x, g, b):
            mu = jnp.mean(x, axis=-1, keepdims=True)
            var = jnp.mean(jnp.square(x - mu), axis=-1, keepdims=True)
            return (x - mu) * jax.lax.rsqrt(var + EPS) * g + b

        def linear(x, w, b):
            return x @ w + b
        n = x.shape[0]
        scale = x.shape[-1] ** (-0.5)
        q = linear(x, wq, bq)
        k = linear(x, wk, bk)
        v = linear(x, wv, bv)
        src, dst = (edge_index[0], edge_index[1])
        scores = jnp.sum(q[dst] * k[src], axis=-1) * scale
        scores = scores + (edge_weight[:, None] @ we + be)[:, 0]
        seg_max = jax.ops.segment_max(scores, dst, num_segments=n)
        exp_s = jnp.exp(scores - seg_max[dst])
        denom = jax.ops.segment_sum(exp_s, dst, num_segments=n)
        attn = exp_s / jnp.maximum(denom[dst], 1e-12)
        message = v[src] * attn[:, None]
        out = jax.ops.segment_sum(message, dst, num_segments=n)
        x = layer_norm(x + out + linear(x, ws, bs), g1, b1)
        ffn = linear(jax.nn.gelu(linear(x, w_ff1, b_ff1)), w_ff2, b_ff2)
        x = layer_norm(x + ffn, g2, b2)
        return x

    def _L3_gnn_ref(h, relvectors, w_ih, w_hh, b_ih, b_hh, edge_src, edge_dst, edge_rel):
        import jax, jax.numpy as jnp
        import numpy as np
        N_NODES = 3125
        N_EDGES = 50000
        HDIM = 256
        NUMRELS = 16

        def _gru_cell(x, h, w_ih, w_hh, b_ih, b_hh):
            gi = x @ w_ih.T + b_ih
            gh = h @ w_hh.T + b_hh
            i_r, i_z, i_n = jnp.split(gi, 3, axis=-1)
            h_r, h_z, h_n = jnp.split(gh, 3, axis=-1)
            r = jax.nn.sigmoid(i_r + h_r)
            z = jax.nn.sigmoid(i_z + h_z)
            n = jnp.tanh(i_n + r * h_n)
            return (1.0 - z) * n + z * h
        msg = h[edge_src] + relvectors[edge_rel]
        red = jax.ops.segment_sum(msg, edge_dst, num_segments=h.shape[0])
        return _gru_cell(red, h, w_ih, w_hh, b_ih, b_hh)
    edge_index = jnp.stack([src, dst])
    h = jnp.maximum(_layernorm(x, axis=-1), 0.0)
    x = x + _L0_gnn_ref(h, src, dst, edge_weight, L0_gnn_weight, L0_gnn_b)
    h = jnp.maximum(_layernorm(x, axis=-1), 0.0)
    x = x + _L1_gnn_ref(h, edge_index, edge_attr_128, node_vec1, node_vec1_n2, L1_gnn_z_in, L1_gnn_z_out, L1_gnn_W_cent, L1_gnn_b_cent, L1_gnn_W_vor, L1_gnn_b_vor, L1_gnn_W_sum, L1_gnn_b_sum)
    h = jnp.maximum(_layernorm(x, axis=-1), 0.0)
    x = x + _L2_gnn_ref(h, edge_index, edge_weight, L2_gnn_wq, L2_gnn_bq, L2_gnn_wk, L2_gnn_bk, L2_gnn_wv, L2_gnn_bv, L2_gnn_ws, L2_gnn_bs, L2_gnn_we, L2_gnn_be, L2_gnn_g1, L2_gnn_b1, L2_gnn_g2, L2_gnn_b2, L2_gnn_w_ff1, L2_gnn_b_ff1, L2_gnn_w_ff2, L2_gnn_b_ff2)
    h = jnp.maximum(_layernorm(x, axis=-1), 0.0)
    x = x + _L3_gnn_ref(h, L3_gnn_relvectors, L3_gnn_w_ih, L3_gnn_w_hh, L3_gnn_b_ih, L3_gnn_b_hh, src, dst, edge_type_16)
    return x

_drawn_inputs = setup_inputs


def setup_inputs(seed=0):
    import zlib

    import numpy as np

    out = dict(_drawn_inputs(seed))
    spreads = {'L1_gnn_b_cent': (0.0, 2.0),
     'L1_gnn_b_vor': (0.0, 2.0),
     'L1_gnn_b_sum': (0.0, 0.1),
     'L2_gnn_bq': (0.0, 2.0),
     'L2_gnn_bk': (0.0, 2.0),
     'L2_gnn_bv': (0.0, 0.511),
     'L2_gnn_bs': (0.0, 0.509),
     'L2_gnn_g1': (1.0, 0.555),
     'L2_gnn_b1': (0.0, 0.507),
     'L2_gnn_g2': (1.0, 0.2),
     'L2_gnn_b2': (0.0, 0.541),
     'L2_gnn_b_ff1': (0.0, 0.8),
     'L2_gnn_b_ff2': (0.0, 0.544)}
    factors = {'node_vec1': 8.0,
     'node_vec1_n2': 8.0,
     'L0_gnn_b': 6.45,
     'L1_gnn_W_cent': 4.295,
     'L1_gnn_W_vor': 4.652,
     'L2_gnn_wq': 7.212,
     'L2_gnn_wk': 7.116,
     'L3_gnn_w_hh': 4.542,
     'L3_gnn_b_ih': 43.1,
     'L3_gnn_b_hh': 59.767}
    for name, (base, spread) in spreads.items():
        noise = np.random.default_rng([zlib.crc32(name.encode()), seed]).standard_normal(out[name].shape)
        drawn = base * np.exp(spread * noise) if base else spread * noise
        out[name] = jnp.asarray(drawn.astype(out[name].dtype))
    for name, factor in factors.items():
        out[name] = (out[name] * factor).astype(out[name].dtype)
    return out
```

```python
from contextlib import ExitStack

import concourse.bass as bass
from concourse import mybir

F32 = mybir.dt.float32
BF16 = mybir.dt.bfloat16
I32 = mybir.dt.int32
U16 = mybir.dt.uint16
ALU = mybir.AluOpType
ACT = mybir.ActivationFunctionType
AX = mybir.AxisListType
SP_E, PE_E, DVE_E = mybir.EngineType.SP, mybir.EngineType.PE, mybir.EngineType.DVE

P = 128
NODES, D = 6250, 256
EDGES, ED = 100000, 128
BLOCKS = -(-NODES // P)
NODES_PAD = BLOCKS * P
LAST_ROWS = NODES - (BLOCKS - 1) * P
EP = 125
STEPS = EDGES // EP
UNROLL = 8
TILES = -(-(-(-EDGES // P) + BLOCKS) // (2 * UNROLL)) * 2 * UNROLL
TURNS = TILES // UNROLL
PAD = 2 * UNROLL
CHUNKS = -(-TILES // P)
TABLE = CHUNKS * P
BANK = 2048
REC = ED + 4
ONE, SRC, DST, WGT = ED, ED + 1, ED + 2, ED + 3
NW = D + ED + 1
DW = D + 16
TURN_BLOCKS = 7
RELS = 16
BLOCK_RANGE = "a tile's block is a count of blocks (1 to BLOCKS) less one, whatever the graph"
DEG_MAX = 511
EPS = 1e-5
DC = D // P


class Counter:

    def __init__(self, eng, sem, n=0):
        self.eng, self.sem, self.n = eng, sem, n

    def mark(self, ins):
        ins.then_inc(self.sem, 1)
        self.n = self.n + 1
        return ins

    def wait(self):
        self.eng.wait_ge(self.sem, self.n)

    def link(self, ins):
        self.mark(ins)
        self.wait()


def own_wait(eng, sem, value):
    eng.wait_ge(sem, value)
    eng.nop(nofuse=True)


def in_turns(eng, count, unroll, *steps, begin=None):
    turns = count // unroll
    assert turns * unroll == count and turns > 2
    begin = begin or (lambda i, k: None)

    for k in range(unroll):
        begin(k, k)
        for lag, step in steps:
            if k >= lag:
                step(k - lag, k - lag, True, 0)
    with eng.Fori(1, turns) as g:
        for k in range(unroll):
            begin(g * unroll + k, k)
            for lag, step in steps:
                step(g * unroll + (k - lag), (k - lag) % unroll, False, g if k >= lag else g - 1)
    for k in range(max(lag for lag, _ in steps)):
        begin(count + k, k)
        for lag, step in steps:
            if k < lag:
                i = count + k - lag
                step(i, i % unroll, False, i // unroll)


def before(k):
    return 2 if k >= 2 else (1, 3)[k]


def row_stats(nc, d, stats, t):
    s = stats
    d.mark(nc.vector.tensor_tensor(t["msum"][:], s[:, :, 1], s[:, :, 4], ALU.add))
    d.mark(nc.vector.tensor_tensor(t["mdif"][:], s[:, :, 1], s[:, :, 4], ALU.subtract))
    d.link(nc.vector.tensor_tensor(t["m2"][:], s[:, :, 2], s[:, :, 5], ALU.add))
    d.link(nc.vector.scalar_tensor_tensor(out=t["mdif"][:], in0=t["mdif"][:], scalar=0.25, in1=t["mdif"][:],
                                          op0=ALU.mult, op1=ALU.mult))
    d.link(nc.vector.scalar_tensor_tensor(out=t["m2"][:], in0=t["m2"][:], scalar=1.0 / D, in1=t["mdif"][:],
                                          op0=ALU.mult, op1=ALU.add))
    return nc.vector.tensor_scalar(t["vare"][:], t["m2"][:], EPS, None, ALU.add)


def build(nc, A, OUT):
    with ExitStack() as whole:
        def sem(name):
            return nc.alloc_semaphore(name=name)

        def sb(ctx, name, shape, dt=F32):
            return ctx.enter_context(nc.sbuf_tensor(name, shape, dt))

        def ps(ctx, name, shape, dt=F32):
            bank = ctx.enter_context(nc.psum_tensor(name, [P, BANK // mybir.dt.size(dt)], dt))
            n = 1
            for s in shape[1:]:
                n *= s
            if len(shape) == 2:
                return bank[0:shape[0], 0:n]
            return bank[0:shape[0], 0:n].rearrange("p (a b) -> p a b", a=shape[1])

        def dram(name, shape, dt=F32):
            return nc.dram_tensor(name, shape, dt, kind="Internal").ap()

        h0_rows = dram("h0_rows", (NODES_PAD, D))
        src_records = dram("src_records", (EDGES + P, REC))
        by_dst = {n: dram(f"by_dst_{n}", (EDGES + P, 1), F32 if n == "wgt" else I32)
                  for n in ("src", "dst", "wgt", "typ")}
        table_rows = {n: dram(f"table_{n}", (TABLE, 1), I32) for n in ("sb", "ss", "db")}

        c = {}
        c["iota"] = sb(whole, "iota", [P, P])
        c["pidx"] = sb(whole, "pidx", [P, 1])
        c["ident"] = sb(whole, "ident", [P, P])
        c["ones"] = sb(whole, "ones", [P, P])
        c["indeg"] = sb(whole, "indeg", [P, BLOCKS])
        c["dloc"] = sb(whole, "dloc", [P, TILES])
        c["dsrc"] = sb(whole, "dsrc", [P, TILES])
        c["dwgt"] = sb(whole, "dwgt", [P, TILES])
        c["dtyp"] = sb(whole, "dtyp", [P, TILES])
        c["dblk"] = sb(whole, "dblk", [1, TILES + 2 * PAD], I32)
        env = dict(nc=nc, A=A, OUT=OUT, c=c, sb=sb, ps=ps, sem=sem, h0_rows=h0_rows, dram=dram,
                   src_records=src_records, by_dst=by_dst, table_rows=table_rows)
        env["x_rows"] = dram("x_rows", (NODES_PAD, D))
        env["h2_rows"] = dram("h2_rows", (NODES_PAD, D))
        env["h3_rows"] = dram("h3_rows", (NODES_PAD, D))
        prepare(env)
        with ExitStack() as mid:
            env["nodes"] = sb(mid, "nodes", [P, BLOCKS, NW])
            source_sums(env)
            layers_0_and_1(env)
            env["sums"] = sb(mid, "sums", [P, BLOCKS, DW])
            attention(env)
            layer_2(env)
            relation_sums(env)
            layer_3(env)


def prepare(env):
    nc, A, c, sb, ps, sem = (env[k] for k in ("nc", "A", "c", "sb", "ps", "sem"))
    by_dst, table_rows, src_records = env["by_dst"], env["table_rows"], env["src_records"]
    HALF = 8
    SEG = STEPS // 4
    SB = TURN_BLOCKS
    PAIRS = (BLOCKS - 1) // 2
    FIRST_PAIR = 12
    REC_TURNS = STEPS // (2 * HALF)
    with nc.cleanup_on_exit(), ExitStack() as ctx:
        X = sb(ctx, "X", [P, BLOCKS, D])
        H = sb(ctx, "H0", [P, BLOCKS, D])
        key = {s: sb(ctx, f"key_{s}", [EP, STEPS], I32) for s in ("src", "dst")}
        typ = sb(ctx, "typ", [EP, STEPS], I32)
        wgt = sb(ctx, "wgt", [EP, STEPS])
        pos = {s: sb(ctx, f"pos_{s}", [EP, STEPS]) for s in ("src", "dst")}
        hi_i = sb(ctx, "hi_i", [EP, STEPS], I32)
        hi = sb(ctx, "hi", [EP, STEPS], BF16)
        hi_d = sb(ctx, "hi_d", [EP, STEPS], BF16)
        lo_d = sb(ctx, "lo_d", [EP, STEPS])
        eq = sb(ctx, "eq", [EP, SB, SEG], U16)
        cum_seg = sb(ctx, "cum_seg", [EP, SB, SEG])
        eq_f = sb(ctx, "eq_f", [EP, 2, STEPS], BF16)
        cum = sb(ctx, "cum", [EP, STEPS])
        ones_row = sb(ctx, "ones_row", [EP, SEG], BF16)
        meta = sb(ctx, "meta", [EP, STEPS, 4])
        rec = sb(ctx, "rec", [EP, 2 * HALF, REC])
        pos_slot = sb(ctx, "pos_slot", [EP, 2 * HALF], I32)
        word_slot = sb(ctx, "word_slot", [EP, 4, 4], I32)
        pos_one = sb(ctx, "pos_one", [EP, 4], I32)
        tail = sb(ctx, "tail", [P, REC])
        tail_i = sb(ctx, "tail_i", [P, 2], I32)
        iota_i = sb(ctx, "iota_i", [P, P], I32)
        pidx_i = sb(ctx, "pidx_i", [P, 1], I32)
        tile_i = sb(ctx, "tile_i", [P, CHUNKS], I32)
        tile_f = sb(ctx, "tile_f", [P, CHUNKS])
        upper = sb(ctx, "upper", [P, P])
        iota_b = sb(ctx, "iota_b", [P, P], BF16)
        cnt = sb(ctx, "cnt", [EP, BLOCKS])
        total = sb(ctx, "total", [P, BLOCKS])
        first = sb(ctx, "first", [P, BLOCKS])
        base = sb(ctx, "base", [EP, BLOCKS])
        nt_i = sb(ctx, "nt_i", [P, BLOCKS], I32)
        nt = sb(ctx, "nt", [P, BLOCKS])
        tfirst = sb(ctx, "tfirst", [P, BLOCKS])
        shift = sb(ctx, "shift", [P, BLOCKS])
        dshift = sb(ctx, "dshift", [P, BLOCKS])
        reached = sb(ctx, "reached", [P, CHUNKS, BLOCKS])
        weighed = sb(ctx, "weighed", [P, CHUNKS, BLOCKS])
        blk_f = sb(ctx, "blk_f", [P, CHUNKS])
        start_f = sb(ctx, "start_f", [P, CHUNKS])
        blk_i = {s: sb(ctx, f"blk_i_{s}", [P, CHUNKS], I32) for s in ("src", "dst")}
        start_i = {s: sb(ctx, f"start_i_{s}", [P, CHUNKS], I32) for s in ("src", "dst")}
        stats = sb(ctx, "stats", [P, BLOCKS, 6])
        rs = {n: sb(ctx, n, [P, BLOCKS]) for n in ("msum", "mdif", "m2", "vare")}
        vare = rs["vare"]
        half = sb(ctx, "half", [P, BLOCKS])
        rstd = sb(ctx, "rstd", [P, BLOCKS])
        nmr = sb(ctx, "nmr", [P, BLOCKS])
        oh_lo = sb(ctx, "oh_lo", [EP, 8, P], BF16)
        oh_hi = sb(ctx, "oh_hi", [EP, 8, BLOCKS], BF16)
        pair = sb(ctx, "pair", [EP - 1, 2], I32)
        pair_hi = sb(ctx, "pair_hi", [EP - 1, 2], I32)
        pair_f = sb(ctx, "pair_f", [EP - 1, 2])
        falls = sb(ctx, "falls", [P, 2])
        fall_sum = sb(ctx, "fall_sum", [P, 1])
        fall_i = sb(ctx, "fall_i", [1, 1], I32)
        windows = sb(ctx, "windows", [P, 4, P], I32)
        windows_f = sb(ctx, "windows_f", [P, 4, P])
        dblk_i = sb(ctx, "dblk_i", [P, TILES], I32)

        p_total = ps(ctx, "p_total", [P, BLOCKS])
        p_base = ps(ctx, "p_base", [P, BLOCKS])
        p_deg = ps(ctx, "p_deg", [P, BLOCKS])
        p_fall = ps(ctx, "p_fall", [P, 1])
        p_win = ps(ctx, "p_win", [P, 4, P])

        loaded_x, loaded_src, loaded_rest = sem("loaded_x"), sem("loaded_src"), sem("loaded_rest")
        iotas, consts = sem("iotas"), sem("consts")
        dve, stats_ready, rstd_ready = sem("prep_dve"), sem("stats_ready"), sem("rstd_ready")
        h0_ready, h0_stored = sem("h0_ready"), sem("h0_stored")
        counted, ranked = sem("counted"), sem("ranked")
        ranked_steps, meta_ready = sem("ranked_steps"), sem("meta_ready")
        rec_loaded = [sem(f"rec_loaded{h}") for h in range(2)]
        rec_ready = sem("rec_ready")
        rec_stored = [sem(f"rec_stored{h}") for h in range(2)]
        hot_ready, hot_used = sem("hot_ready"), sem("hot_used")
        tail_ready, tail_stored = sem("tail_ready"), sem("tail_stored")
        fall_ready, fall_summed, fall_known = sem("fall_ready"), sem("fall_summed"), sem("fall_known")
        dst_ordered, slots_copied = sem("dst_ordered"), sem("slots_copied")
        win_loaded, win_cast, win_turned = sem("win_loaded"), sem("win_cast"), sem("win_turned")
        win_out = sem("win_out")
        tables_ready, tables_stored, dblk_loaded = sem("tables_ready"), sem("tables_stored"), sem("dblk_loaded")
        act = sem("prep_act")
        block_counted, matched, scanned, carried, placed = (
            sem(n) for n in ("block_counted", "matched", "scanned", "carried", "placed"))
        rel_pad = sem("x_pad")

        def grid(ap):
            return ap.rearrange("(p t) -> p t", t=STEPS)

        nfull = (BLOCKS - 1) * P

        with nc.Block() as block:
            @block.sync
            def _(sp):
                sp.dma_start(key["src"][:], grid(A["src"])).then_inc(loaded_src, 16)
                sp.dma_start(key["dst"][:], grid(A["dst"])).then_inc(loaded_rest, 16)
                sp.dma_start(wgt[:], grid(A["edge_weight"])).then_inc(loaded_rest, 16)
                sp.dma_start(typ[:], grid(A["edge_type_16"])).then_inc(loaded_rest, 16)
                sp.dma_start(pair[:], A["dst"][STEPS - 1:STEPS - 1 + (EP - 1) * STEPS]
                             .rearrange("(p t) -> p t", t=STEPS)[:, 0:2]).then_inc(loaded_rest, 16)
                attr = A["edge_attr_128"].rearrange("(p t) d -> p t d", t=STEPS)

                def load(turn, h):
                    sp.dma_start(rec[:, h * HALF:(h + 1) * HALF, 0:ED],
                                 attr[:, bass.ds(turn * 2 * HALF + h * HALF, HALF), :]
                                 ).then_inc(rec_loaded[h], 16)

                for h in range(2):
                    load(0, h)
                sp.wait_ge(rel_pad, 1)
                sp.dma_start(X[:, 0:BLOCKS - 1, :],
                             A["x"][0:nfull, :].rearrange("(i p) d -> p i d", p=P)).then_inc(loaded_x, 16)
                sp.dma_start(X[0:LAST_ROWS, BLOCKS - 1, :], A["x"][nfull:NODES, :]).then_inc(loaded_x, 16)
                with sp.Fori(1, REC_TURNS) as turn:
                    for h in range(2):
                        sp.wait_ge(rec_stored[h], turn * (16 * HALF))
                        load(turn, h)
                sp.wait_ge(h0_ready, BLOCKS)
                sp.dma_start(env["h0_rows"].rearrange("(i p) d -> p i d", p=P), H[:]).then_inc(h0_stored, 16)
                sp.wait_ge(tail_ready, 2)
                sp.dma_start(src_records[EDGES:EDGES + P, :], tail[:]).then_inc(tail_stored, 16)
                for n, col in (("src", 1), ("dst", 0), ("wgt", 1), ("typ", 1)):
                    t = tail_i[:, col:col + 1]
                    if n == "wgt":
                        t = t.bitcast(F32)
                    sp.dma_start(by_dst[n][EDGES:EDGES + P, :], t).then_inc(tail_stored, 16)
                sp.wait_ge(tables_ready, 2)
                for n, t in (("sb", blk_i["src"]), ("ss", start_i["src"]), ("db", blk_i["dst"])):
                    sp.dma_start(table_rows[n].rearrange("(c p) o -> p (c o)", p=P), t[:],
                                 allow_slow_non_contiguous=True).then_inc(tables_stored, 16)
                sp.wait_ge(tables_stored, 48)
                row = table_rows["db"][0:TILES, :].rearrange("t o -> o t")
                sp.dma_start(c["dblk"][:, PAD:PAD + TILES], row).then_inc(dblk_loaded, 16)
                sp.dma_start(dblk_i[:], row.broadcast_to([P, TILES])).then_inc(dblk_loaded, 16)
                sp.wait_ge(h0_stored, 16)
                sp.wait_ge(tail_stored, 80)
                sp.wait_ge(dblk_loaded, 32)

            @block.gpsimd
            def _(gp):
                nc.gpsimd.iota(iota_i[:], [[1, P]], base=0, channel_multiplier=0).then_inc(iotas, 1)
                nc.gpsimd.iota(pidx_i[:], [[0, 1]], base=0, channel_multiplier=1).then_inc(iotas, 1)
                nc.gpsimd.iota(tile_i[:], [[P, CHUNKS]], base=0, channel_multiplier=1).then_inc(iotas, 1)
                nc.gpsimd.memset(half[:], -0.5).then_inc(iotas, 1)
                nc.gpsimd.memset(tail[:], 0.0).then_inc(iotas, 1)
                nc.gpsimd.memset(c["dblk"][:], 0)
                gp.wait_ge(iotas, 5)
                nc.gpsimd.memset(tail[:, SRC:SRC + 1], -1.0).then_inc(tail_ready, 1)
                nc.gpsimd.memset(tail_i[:, 0:1], -1).then_inc(iotas, 1)
                nc.gpsimd.memset(tail_i[:, 1:2], 0).then_inc(iotas, 1)
                gp.wait_ge(iotas, 7)
                nc.gpsimd.memset(ones_row[:], 1.0).then_inc(tail_ready, 1)
                gp.wait_ge(loaded_rest, 64)
                nc.gpsimd.memset(meta[:, :, 0], 1.0).then_inc(meta_ready, 1)
                nc.gpsimd.tensor_copy(meta[:, :, 1], key["src"][:]).then_inc(meta_ready, 1)
                nc.gpsimd.tensor_copy(meta[:, :, 2], key["dst"][:]).then_inc(meta_ready, 1)
                nc.gpsimd.tensor_copy(meta[:, :, 3], wgt[:]).then_inc(meta_ready, 1)

                def scatter(turn, h):
                    own_wait(gp, rec_ready, turn * 2 + h + 1)
                    for k in range(h * HALF, (h + 1) * HALF):
                        gp.indirect_dma_start(out=src_records,
                                              out_offset=bass.IndirectOffsetOnAxis(ap=pos_slot[:, k:k + 1], axis=0),
                                              in_=rec[:, k, :], in_offset=None).then_inc(rec_stored[h], 16)

                def scatters(turns):
                    with gp.Fori(*turns) as turn:
                        for h in range(2):
                            scatter(turn, h)

                scatters((0, FIRST_PAIR))
                gp.wait_ge(stats_ready, 1)
                nc.gpsimd.tensor_tensor(rstd[:], vare[:], half[:], ALU.pow).then_inc(rstd_ready, 1)
                scatters((FIRST_PAIR, REC_TURNS))
                for h in range(2):
                    gp.wait_ge(rec_stored[h], STEPS // (2 * HALF) * 16 * HALF)

                gp.wait_ge(fall_known, 1)
                gp.wait_ge(ranked_steps, 2 * STEPS)
                falling = gp.alloc_register("falling")
                gp.load(falling, fall_i[0:1, 0:1])
                with gp.If_ne(falling, 0):
                    with gp.Fori(0, STEPS // 4) as turn:
                        for n, field in enumerate((key["src"], key["dst"], wgt, typ)):
                            f = field[:, bass.ds(turn * 4, 4)]
                            if n == 2:
                                f = f.bitcast(I32)
                            nc.gpsimd.tensor_copy(word_slot[:, n, :], f).then_inc(slots_copied, 1)
                        nc.gpsimd.tensor_copy(pos_one[:], pos["dst"][:, bass.ds(turn * 4, 4)]).then_inc(slots_copied, 1)
                        own_wait(gp, slots_copied, turn * 5 + 5)
                        for k in range(4):
                            for n, name in enumerate(("src", "dst", "wgt", "typ")):
                                w = word_slot[:, n, k:k + 1]
                                if name == "wgt":
                                    w = w.bitcast(F32)
                                gp.indirect_dma_start(out=by_dst[name],
                                                      out_offset=bass.IndirectOffsetOnAxis(ap=pos_one[:, k:k + 1], axis=0),
                                                      in_=w, in_offset=None).then_inc(dst_ordered, 16)
                        gp.wait_ge(dst_ordered, turn * 256 + 256)
                with gp.Else():
                    for n, name in (("src", "src"), ("dst", "dst"), ("wgt", "edge_weight"), ("typ", "edge_type_16")):
                        gp.dma_start(by_dst[n][0:EDGES, :].rearrange("(a b) o -> a (b o)", a=32),
                                     A[name].rearrange("(a b) -> a b", a=32)).then_inc(dst_ordered, 16)
                    gp.wait_ge(dst_ordered, 64)
                gp.wait_ge(tail_stored, 80)
                for ch in range(CHUNKS):
                    if ch:
                        gp.wait_ge(win_cast, ch)
                    for n, name in enumerate(("src", "dst", "wgt", "typ")):
                        w = windows[:, n, :]
                        if name == "wgt":
                            w = w.bitcast(F32)
                        gp.indirect_dma_start(out=w, out_offset=None, in_=by_dst[name],
                                              in_offset=bass.IndirectOffsetOnAxis(ap=start_i["dst"][:, ch:ch + 1], axis=0)
                                              ).then_inc(win_loaded, 16)

            @block.scalar
            def _(ac):
                def complete(turn):
                    for h in range(2):
                        step = turn * 2 * HALF + h * HALF
                        ks = slice(h * HALF, (h + 1) * HALF)
                        ac.wait_ge(rec_loaded[h], turn * 16 + 16)
                        ac.wait_ge(ranked_steps, step + HALF)
                        nc.scalar.activation(pos_slot[:, ks], pos["src"][:, bass.ds(step, HALF)], ACT.Copy).then_inc(act, 1)
                        nc.scalar.activation(rec[:, ks, ED:REC], meta[:, bass.ds(step, HALF), :], ACT.Copy).then_inc(act, 1)
                        ac.wait_ge(act, turn * 4 + h * 2 + 2)
                        ac.nop().then_inc(rec_ready, 1)

                def normalise(i):
                    nc.scalar.activation(H[:, bass.ds(i, 1), :], X[:, bass.ds(i, 1), :], ACT.Relu,
                                         bias=nmr[:, bass.ds(i, 1)], scale=rstd[:, bass.ds(i, 1)]).then_inc(h0_ready, 1)

                ac.wait_ge(meta_ready, 4)
                with ac.Fori(0, FIRST_PAIR) as turn:
                    complete(turn)
                ac.wait_ge(rstd_ready, 2)
                ac.wait_ge(loaded_x, 32)
                with ac.Fori(0, PAIRS) as pair_i:
                    complete(pair_i + FIRST_PAIR)
                    normalise(pair_i * 2)
                    normalise(pair_i * 2 + 1)
                normalise(BLOCKS - 1)
                with ac.Fori(FIRST_PAIR + PAIRS, REC_TURNS) as turn:
                    complete(turn)

            @block.tensor
            def _(pe):
                for n in range(2):
                    pe.wait_ge(counted, n + 1)
                    pe.wait_ge(consts, 1)
                    nc.tensor.matmul(p_total[:], c["ones"][0:EP, :], cnt[:], start=True, stop=True)
                    nc.tensor.matmul(p_base[:], upper[0:EP, :], cnt[:], start=True, stop=True).then_inc(ranked, 1)
                pe.wait_ge(fall_ready, 1)
                nc.tensor.matmul(p_fall[:], c["ones"][:], fall_sum[:], start=True, stop=True).then_inc(fall_summed, 1)

                def degrees(turn, opening):
                    for k in range(8):
                        pe.wait_ge(hot_ready, turn * 8 + k + 1)
                        nc.tensor.matmul(p_deg[:], oh_lo[:, k, :], oh_hi[:, k, :], start=opening and k == 0,
                                         stop=True, skip_group_check=True).then_inc(hot_used, 1)

                degrees(0, True)
                with pe.Fori(1, STEPS // 8) as turn:
                    degrees(turn, False)
                for ch in range(CHUNKS):
                    pe.wait_ge(win_cast, ch + 1)
                    if ch:
                        pe.wait_ge(win_out, ch)
                    for n in range(4):
                        last = nc.tensor.transpose(p_win[:, n, :], windows_f[:, n, :], c["ident"][:])
                    last.then_inc(win_turned, 1)

            @block.vector
            def _(ve):
                d = Counter(ve, dve)
                nc.vector.memset(X[:, BLOCKS - 1, :], 0.0).then_inc(rel_pad, 1)
                d.mark(nc.vector.memset(c["ones"][:], 1.0))
                ve.wait_ge(iotas, 5)
                d.mark(nc.vector.tensor_copy(c["iota"][:], iota_i[:]))
                d.mark(nc.vector.tensor_copy(c["pidx"][:], pidx_i[:]))
                d.link(nc.vector.tensor_copy(tile_f[:], tile_i[:]))
                d.mark(nc.vector.tensor_copy(iota_b[:], c["iota"][:]))
                d.mark(nc.vector.tensor_scalar(c["ident"][:], c["iota"][:], c["pidx"][:, 0:1], None, ALU.is_equal))
                d.link(nc.vector.tensor_scalar(upper[:], c["iota"][:], c["pidx"][:, 0:1], None, ALU.is_gt))
                nc.vector.memset(fall_sum[:], 0.0).then_inc(consts, 1)

                def rank(side, hi_t):
                    if side == "dst":
                        ve.wait_ge(loaded_rest, 64)
                    else:
                        ve.wait_ge(loaded_src, 16)
                    d.link(nc.vector.tensor_scalar(hi_i[:], key[side][:], 7, None, ALU.arith_shift_right))
                    d.link(nc.vector.tensor_copy(hi_t[:], hi_i[:]))
                    nth = 0 if side == "src" else 1

                    def count_block(i, k, opening, g):
                        if not opening or k >= 2:
                            ve.wait_ge(block_counted, i - before(k) + (nth * BLOCKS + 1))
                        nc.vector.tensor_scalar(eq_f[:, k % 2, :], hi_t[:], c["iota"][0:EP, bass.ds(i, 1)], None, ALU.is_equal,
                                                op1=ALU.add, accum_out=cnt[:, bass.ds(i, 1)]).then_inc(block_counted, 1)

                    in_turns(ve, BLOCKS, SB, (0, count_block))
                    ve.wait_ge(block_counted, (nth + 1) * BLOCKS)
                    ve.nop().then_inc(counted, 1)
                    ve.wait_ge(ranked, 1 if side == "src" else 2)
                    d.link(nc.vector.tensor_copy(total[:], p_total[:]))
                    d.link(nc.vector.tensor_tensor_scan(first[:], total[:], total[:], 0.0, ALU.add, ALU.bypass))
                    d.link(nc.vector.tensor_tensor(first[:], first[:], total[:], ALU.subtract))
                    d.link(nc.vector.scalar_tensor_tensor(out=base[:], in0=p_base[0:EP, :], scalar=-1.0,
                                                          in1=first[0:EP, :], op0=ALU.add, op1=ALU.add))
                    for seg in range(STEPS // SEG):
                        cols = slice(seg * SEG, (seg + 1) * SEG)
                        n = (nth * (STEPS // SEG) + seg) * BLOCKS

                        def match(i, k, opening, g):
                            nc.vector.tensor_scalar(eq[:, k, :], hi_t[:, cols], c["iota"][0:EP, bass.ds(i, 1)], None,
                                                    ALU.is_equal).then_inc(matched, 1)

                        def count_up(i, k, opening, g):
                            ve.wait_ge(matched, i + (n + 1))
                            nc.vector.tensor_tensor_scan(cum_seg[:, k, :], ones_row[:], eq[:, k, :], base[:, bass.ds(i, 1)],
                                                         ALU.mult, ALU.add).then_inc(scanned, 1)

                        def place(i, k, opening, g):
                            ve.wait_ge(scanned, i + (n + 1))
                            own_wait(ve, placed, i + n)
                            nc.vector.copy_predicated(pos[side][:, cols], eq[:, k, :], cum_seg[:, k, :]).then_inc(placed, 1)

                        def carry(i, k, opening, g):
                            nc.vector.tensor_scalar(base[:, bass.ds(i, 1)], cum_seg[:, k, SEG - 1:SEG], 0.0, None,
                                                    ALU.add).then_inc(carried, 1)

                        in_turns(ve, BLOCKS, SB, (2, place), (2, carry), (1, count_up), (0, match))
                        ve.wait_ge(placed, n + BLOCKS)
                        ve.wait_ge(carried, n + BLOCKS)
                        ve.nop().then_inc(ranked_steps, SEG)

                def table(side):
                    d.link(nc.vector.tensor_scalar(nt[:], total[:], float(P - 1), None, ALU.add))
                    d.link(nc.vector.tensor_copy(nt_i[:], nt[:]))
                    d.link(nc.vector.tensor_scalar(nt_i[:], nt_i[:], 7, None, ALU.arith_shift_right))
                    d.link(nc.vector.tensor_copy(nt[:], nt_i[:]))
                    d.link(nc.vector.tensor_tensor_scan(tfirst[:], nt[:], nt[:], 0.0, ALU.add, ALU.bypass))
                    d.link(nc.vector.tensor_tensor(tfirst[:], tfirst[:], nt[:], ALU.subtract))
                    d.link(nc.vector.scalar_tensor_tensor(out=shift[:], in0=tfirst[:], scalar=-float(P),
                                                          in1=first[:], op0=ALU.mult, op1=ALU.add))
                    d.mark(nc.vector.tensor_copy(dshift[:, 0:1], shift[:, 0:1]))
                    d.link(nc.vector.tensor_tensor(dshift[:, 1:BLOCKS], shift[:, 1:BLOCKS],
                                                   shift[:, 0:BLOCKS - 1], ALU.subtract))
                    for ch in range(CHUNKS):
                        d.mark(nc.vector.tensor_scalar(reached[:, ch, :], tfirst[:], tile_f[:, ch:ch + 1], None, ALU.is_le))
                    d.wait()
                    for ch in range(CHUNKS):
                        d.mark(nc.vector.tensor_tensor(weighed[:, ch, :], reached[:, ch, :], dshift[:], ALU.mult))
                    d.mark(nc.vector.tensor_reduce(blk_f[:], reached[:], AX.X, ALU.add))
                    d.wait()
                    d.link(nc.vector.tensor_reduce(start_f[:], weighed[:], AX.X, ALU.add))
                    d.link(nc.vector.scalar_tensor_tensor(out=start_f[:], in0=tile_f[:], scalar=float(P),
                                                          in1=start_f[:], op0=ALU.mult, op1=ALU.add))
                    d.link(nc.vector.tensor_scalar(start_f[:], start_f[:], float(EDGES), None, ALU.min))
                    d.link(nc.vector.tensor_scalar(blk_f[:], blk_f[:], -1.0, None, ALU.add))
                    d.mark(nc.vector.tensor_copy(start_i[side][:], start_f[:]))
                    d.link(nc.vector.tensor_copy(blk_i[side][:], blk_f[:]))
                    ve.nop().then_inc(tables_ready, 1)

                ve.wait_ge(tail_ready, 2)
                rank("src", hi)

                ve.wait_ge(loaded_x, 32)
                n0 = d.n
                with ve.Fori(0, BLOCKS) as i:
                    nc.vector.bn_stats(stats[:, bass.ds(i, 1), :], X[:, bass.ds(i, 1), :]).then_inc(dve, 1)
                nc.vector.memset(falls[:], 0.0).then_inc(dve, 1)
                d.n = n0 + BLOCKS + 1
                d.wait()
                row_stats(nc, d, stats, rs).then_inc(stats_ready, 1)
                ve.wait_ge(rstd_ready, 1)
                nc.vector.scalar_tensor_tensor(out=nmr[:], in0=rs["msum"][:], scalar=-0.5, in1=rstd[:],
                                               op0=ALU.mult, op1=ALU.mult).then_inc(rstd_ready, 1)

                table("src")
                rank("dst", hi_d)
                table("dst")

                d.mark(nc.vector.tensor_tensor(cum[:, 0:STEPS - 1], hi_i[:, 0:STEPS - 1], hi_i[:, 1:STEPS], ALU.is_gt))
                d.link(nc.vector.tensor_scalar(pair_hi[:], pair[:], 7, None, ALU.arith_shift_right))
                d.mark(nc.vector.tensor_reduce(falls[0:EP, 0:1], cum[:, 0:STEPS - 1], AX.X, ALU.max))
                d.link(nc.vector.tensor_copy(pair_f[:], pair_hi[:]))
                d.link(nc.vector.tensor_tensor(falls[0:EP - 1, 1:2], pair_f[:, 0:1], pair_f[:, 1:2], ALU.is_gt))
                nc.vector.tensor_tensor(fall_sum[:], falls[:, 0:1], falls[:, 1:2], ALU.add).then_inc(fall_ready, 1)
                ve.wait_ge(fall_summed, 1)
                nc.vector.tensor_copy(fall_i[:], p_fall[0:1, :]).then_inc(fall_known, 1)

                d.link(nc.vector.tensor_scalar(hi_i[:], key["dst"][:], P - 1, None, ALU.bitwise_and))
                d.link(nc.vector.tensor_copy(lo_d[:], hi_i[:]))
                d.link(nc.vector.tensor_copy(cum[:], hi_d[:]))

                def hots(turn, opening):
                    for k in range(8):
                        if not opening:
                            ve.wait_ge(hot_used, turn * 8 + (k - 7))
                        nc.vector.tensor_scalar(oh_hi[:, k, :], iota_b[0:EP, 0:BLOCKS], cum[:, bass.ds(turn * 8 + k, 1)],
                                                None, ALU.is_equal)
                        nc.vector.tensor_scalar(oh_lo[:, k, :], iota_b[0:EP, :], lo_d[:, bass.ds(turn * 8 + k, 1)],
                                                None, ALU.is_equal).then_inc(hot_ready, 1)

                hots(0, True)
                with ve.Fori(1, STEPS // 8) as turn:
                    hots(turn, False)
                ve.wait_ge(hot_used, STEPS)
                nc.vector.tensor_copy(c["indeg"][:], p_deg[:])

                for ch in range(CHUNKS):
                    ve.wait_ge(win_loaded, 64 * (ch + 1))
                    if ch:
                        ve.wait_ge(win_turned, ch)
                    for n in (0, 1, 3):
                        nc.vector.tensor_copy(windows_f[:, n, :], windows[:, n, :])
                    nc.vector.tensor_copy(windows_f[:, 2, :], windows[:, 2, :].bitcast(F32)).then_inc(win_cast, 1)
                    ve.wait_ge(win_turned, ch + 1)
                    w = min(P, TILES - ch * P)
                    ts = slice(ch * P, ch * P + w)
                    for n, t in enumerate(("dsrc", "dloc", "dwgt", "dtyp")):
                        last = nc.vector.tensor_copy(c[t][:, ts], p_win[:, n, 0:w])
                    last.then_inc(win_out, 1)
                ve.wait_ge(dblk_loaded, 32)
                ve.wait_ge(win_out, CHUNKS)
                d.link(nc.vector.tensor_copy(cum[:], cum[:]))
                nc.vector.scalar_tensor_tensor(out=c["dloc"][:], in0=dblk_i[:], scalar=-float(P), in1=c["dloc"][:],
                                               op0=ALU.mult, op1=ALU.add)


def source_sums(env):
    nc, c, sb, ps, sem = (env[k] for k in ("nc", "c", "sb", "ps", "sem"))
    acc = env["nodes"]
    R = UNROLL
    LAG = 2
    with nc.cleanup_on_exit(), ExitStack() as ctx:
        rec = sb(ctx, "s_rec", [P, R, REC])
        row = sb(ctx, "s_row", [P, R, D])
        idx = sb(ctx, "s_idx", [P, R], I32)
        loc = sb(ctx, "s_loc", [P, R])
        hot = sb(ctx, "s_hot", [P, R, P])
        hotw = sb(ctx, "s_hotw", [P, R, P])
        blk = sb(ctx, "s_blk", [1, TILES], I32)
        start = sb(ctx, "s_start", [1, TILES], I32)
        blk_all = sb(ctx, "s_blk_all", [P, TILES], I32)
        nbase = sb(ctx, "s_nbase", [P, TILES])
        sums = [ps(ctx, f"s_sums{k}", [P, 512]) for k in range(4)]

        tables, cleared = sem("s_tables"), sem("s_cleared")
        rec_in = [sem(f"s_rec_in{k}") for k in range(R)]
        row_in = [sem(f"s_row_in{k}") for k in range(R)]
        idx_ready, loc_ready, hot_ready = sem("s_idx_ready"), sem("s_loc_ready"), sem("s_hot_ready")
        summed, added = sem("s_summed"), sem("s_added")

        with nc.Block() as block:
            @block.sync
            def _(sp):
                sp.dma_start(blk[:], env["table_rows"]["sb"][0:TILES, :].rearrange("t o -> o t")).then_inc(tables, 16)
                sp.dma_start(start[:], env["table_rows"]["ss"][0:TILES, :].rearrange("t o -> o t")).then_inc(tables, 16)
                sp.dma_start(blk_all[:], env["table_rows"]["sb"][0:TILES, :].rearrange("t o -> o t")
                             .broadcast_to([P, TILES])).then_inc(tables, 16)
                sp.wait_ge(tables, 48)

                def turn(g, opening):
                    _, firsts = nc.values_load_multi_w_load_instructions(
                        start[0:1, bass.ds(g * R, R)], engines=(SP_E,), min_val=0, max_val=EDGES)
                    for k in range(R):
                        if not opening:
                            sp.wait_ge(summed, g * R + (k - R + 1))
                        sp.dma_start(rec[:, k, :], env["src_records"][bass.ds(firsts[k], P), :]).then_inc(rec_in[k], 16)

                turn(0, True)
                with sp.Fori(1, TURNS) as g:
                    turn(g, False)

            @block.scalar
            def _(ac):
                ac.wait_ge(cleared, 2)
                with ac.Fori(0, TURNS) as g:
                    for k in range(R):
                        ac.wait_ge(rec_in[k], g * 16 + 16)
                        nc.scalar.activation(idx[:, k:k + 1], rec[:, k, DST:DST + 1], ACT.Copy).then_inc(idx_ready, 1)
                        nc.scalar.activation(loc[:, k:k + 1], rec[:, k, SRC:SRC + 1], ACT.Identity,
                                             bias=nbase[:, bass.ds(g * R + k, 1)]).then_inc(loc_ready, 1)

            @block.gpsimd
            def _(gp):
                with gp.Fori(0, TURNS) as g:
                    for k in range(R):
                        own_wait(gp, idx_ready, g * R + k + 1)
                        gp.indirect_dma_start(out=row[:, k, :], out_offset=None, in_=env["h0_rows"],
                                              in_offset=bass.IndirectOffsetOnAxis(ap=idx[:, k:k + 1], axis=0)
                                              ).then_inc(row_in[k], 16)

            @block.tensor
            def _(pe):
                def turn(g, opening):
                    for k in range(R):
                        pe.wait_ge(hot_ready, g * (2 * R) + 2 * k + 2)
                        pe.wait_ge(row_in[k], g * 16 + 16)
                        if not opening or k >= 4:
                            pe.wait_ge(added, g * R + (k - 4 + 1))
                        nc.tensor.matmul(sums[k % 4][:, 0:D], hotw[:, k, :], row[:, k, :], start=True, stop=True)
                        nc.tensor.matmul(sums[k % 4][:, D:NW], hot[:, k, :], rec[:, k, 0:ED + 1],
                                         start=True, stop=True).then_inc(summed, 1)

                turn(0, True)
                with pe.Fori(1, TURNS) as g:
                    turn(g, False)

            @block.vector
            def _(ve):
                nc.vector.memset(acc[:], 0.0).then_inc(cleared, 1)
                ve.wait_ge(tables, 48)
                nc.vector.tensor_scalar(nbase[:], blk_all[:], -float(P), None, ALU.mult).then_inc(cleared, 1)
                ve.wait_ge(cleared, 2)

                def hots(g, k):
                    ve.wait_ge(loc_ready, g * R + k + 1)
                    nc.vector.tensor_scalar(hot[:, k, :], c["iota"][:], loc[:, k:k + 1], None,
                                            ALU.is_equal).then_inc(hot_ready, 1)
                    nc.vector.tensor_scalar(hotw[:, k, :], c["iota"][:], loc[:, k:k + 1], rec[:, k, WGT:WGT + 1],
                                            ALU.is_equal, ALU.mult).then_inc(hot_ready, 1)

                def add(t, k, b):
                    ve.wait_ge(summed, t + 1)
                    ve.wait_ge(added, t)
                    s = acc[:, bass.ds(b, 1), :]
                    nc.vector.tensor_tensor(s, s, sums[k % 4][:, 0:NW].rearrange("p (a b) -> p a b", a=1),
                                            ALU.add).then_inc(added, 1)

                def turn(g, opening):
                    lo = 0 if opening else g * R - LAG
                    n = R - LAG if opening else R
                    _, blocks = nc.values_load_multi_w_load_instructions(
                        blk[0:1, bass.ds(lo, n)], engines=(DVE_E,), min_val=0, max_val=BLOCKS - 1,
                            skip_runtime_bounds_check_because=BLOCK_RANGE)
                    for k in range(R):
                        hots(g, k)
                        if not opening or k >= LAG:
                            add(g * R + (k - LAG), (k - LAG) % R, blocks[k - LAG if opening else k])

                turn(0, True)
                with ve.Fori(1, TURNS) as g:
                    turn(g, False)
                _, blocks = nc.values_load_multi_w_load_instructions(
                    blk[0:1, TILES - LAG:TILES], engines=(DVE_E,), min_val=0, max_val=BLOCKS - 1,
                            skip_runtime_bounds_check_because=BLOCK_RANGE)
                for k in range(LAG):
                    add(TILES - LAG + k, R - LAG + k, blocks[k])


def rows_view(ap, i, n=1):
    return ap[bass.ds(i * P, n * P), :].rearrange("(i p) d -> p i d", p=P)


def layers_0_and_1(env):
    nc, A, c, sb, ps, sem = (env[k] for k in ("nc", "A", "c", "sb", "ps", "sem"))
    acc = env["nodes"]
    TB = TURN_BLOCKS
    SCALE = float(D) ** -0.5
    with nc.cleanup_on_exit(), ExitStack() as ctx:
        w0 = sb(ctx, "w0", [P, DC, D])
        wsum = sb(ctx, "wsum", [P, D])
        wq = sb(ctx, "wq", [P, DC, D])
        wk = sb(ctx, "wk", [P, DC, D])
        wqT = sb(ctx, "wqT", [P, DC, D])
        wkT = sb(ctx, "wkT", [P, DC, D + 1])
        bq = sb(ctx, "bq", [P, DC])
        bqs = sb(ctx, "bqs", [P, DC, P])
        qk = sb(ctx, "qk", [P, DC, D + 1])
        qkb = sb(ctx, "qkb", [P, D + 1])
        b0 = sb(ctx, "b0", [P, D])
        bsum = sb(ctx, "bsum", [P, D])
        gate = sb(ctx, "gate", [2, 2, D])
        nodes = sb(ctx, "node_vecs", [2, 2, TB * P])
        deg_f = sb(ctx, "deg_f", [P, 2, BLOCKS])
        deg = sb(ctx, "deg", [P, 2, BLOCKS], I32)
        deg_slot = sb(ctx, "deg_slot", [P, 2, TB], I32)
        xin = sb(ctx, "xin", [P, TB, D])
        z = sb(ctx, "z", [P, TB, 2, D])
        turned = sb(ctx, "turned", [P, 2, DC, P])
        staged = sb(ctx, "staged", [P, 2, D])
        sig = sb(ctx, "sig", [P, 2, 2 * D])
        h1 = sb(ctx, "h1", [P, 2, D])
        h2 = sb(ctx, "h2", [P, TB, D])
        stats = sb(ctx, "n_stats", [P, BLOCKS, 6])
        rs = {n: sb(ctx, "n_" + n, [P, BLOCKS]) for n in ("msum", "mdif", "m2", "vare")}
        half, rstd, nmr = (sb(ctx, n, [P, BLOCKS]) for n in ("n_half", "n_rstd", "n_nmr"))
        p_t = [ps(ctx, f"p_t{k}", [P, DC, P]) for k in range(2)]
        p_o = [ps(ctx, f"p_o{k}", [P, 512]) for k in range(2)]
        p_g = [ps(ctx, f"p_g{k}", [P, 512]) for k in range(2)]

        bq_ready = sem("bq_ready")
        loaded, prep, prep_t = sem("n_loaded"), sem("n_prep"), sem("n_prep_t")
        x_in = [sem(f"n_x_in{k}") for k in range(TB)]
        x_used = sem("n_x_used")
        sums_staged, attr_staged = sem("sums_staged"), sem("attr_staged")
        sums_turned, sums_copied, sums_w, x1_ready = sem("sums_turned"), sem("sums_copied"), sem("sums_w"), sem("x1_ready")
        stats_ready, rstd_ready = sem("n_stats_ready"), sem("n_rstd_ready")
        vec_ones, vec_in = sem("vec_ones"), sem("vec_in")
        z_in = [sem(f"z_in{k}") for k in range(TB)]
        z_slot, deg_ready = sem("z_slot"), sem("deg_ready")
        h1_ready, gates_in, gates_ready = sem("h1_ready"), sem("gates_in"), sem("gates_ready")
        attr_turned, attr_copied, attr_w = sem("attr_turned"), sem("attr_copied"), sem("attr_w")
        x2_ready, x2_stored, h2_ready = sem("x2_ready"), [sem(f"x2_stored{k}") for k in range(TB)], sem("h2_ready")
        h2_stored = [sem(f"h2_stored{k}") for k in range(TB)]
        h2_turned, h2_copied, h2_qk, q_ready = sem("h2_turned"), sem("h2_copied"), sem("h2_qk"), sem("q_ready")
        dv = sem("n_dve")
        LOADS = 12

        def row(name):
            return A[name].rearrange("(a d) -> a d", a=1)

        def kchunks(ap):
            return ap.rearrange("(k p) d -> p k d", p=P)

        def blk(i):
            return bass.ds(i, 1)

        def flat(t):
            return t.rearrange("p a d -> p (a d)")

        with nc.Block() as block:
            @block.sync
            def _(sp):
                for t, a in ((wq, kchunks(A["L2_gnn_wq"])), (wk, kchunks(A["L2_gnn_wk"])),
                             (w0, kchunks(A["L0_gnn_weight"]))):
                    sp.dma_start(t[:], a).then_inc(loaded, 16)
                sp.dma_start(wsum[:], A["L1_gnn_W_sum"]).then_inc(loaded, 16)
                sp.dma_start(bq[:], A["L2_gnn_bq"].rearrange("(k p) -> p k", p=P),
                             allow_slow_non_contiguous=True).then_inc(loaded, 16)
                sp.dma_start(wkT[:, :, D], A["L2_gnn_bk"].rearrange("(k p) -> p k", p=P),
                             allow_slow_non_contiguous=True).then_inc(loaded, 16)
                sp.dma_start(b0[:], row("L0_gnn_b").broadcast_to([P, D])).then_inc(loaded, 16)
                sp.dma_start(bsum[:], row("L1_gnn_b_sum").broadcast_to([P, D])).then_inc(loaded, 16)
                for n, (w, b) in enumerate((("L1_gnn_W_cent", "L1_gnn_b_cent"), ("L1_gnn_W_vor", "L1_gnn_b_vor"))):
                    sp.dma_start(gate[0:1, n, :], A[w]).then_inc(loaded, 16)
                    sp.dma_start(gate[1:2, n, :], row(b)).then_inc(loaded, 16)

                for k in range(TB):
                    sp.dma_start(xin[:, k:k + 1, :], rows_view(A["x"], k)).then_inc(x_in[k], 16)
                with sp.Fori(1, BLOCKS // TB - 1) as g:
                    for k in range(TB):
                        sp.wait_ge(x_used, g * TB + (k - TB + 1))
                        sp.dma_start(xin[:, k:k + 1, :], rows_view(A["x"], g * TB + k)).then_inc(x_in[k], 16)
                for k in range(TB):
                    i = BLOCKS - TB + k
                    n = min(P, NODES - i * P)
                    sp.wait_ge(x_used, i - TB + 1)
                    sp.dma_start(xin[0:n, k, :], A["x"][i * P:i * P + n, :]).then_inc(x_in[k], 16)

                def vectors(g, first, n):
                    for m, name in enumerate(("node_vec1_n2", "node_vec1")):
                        sp.dma_start(nodes[0:1, m, 0:n], A[name][bass.ds(first, n), :].rearrange("t o -> o t")
                                     ).then_inc(vec_in, 16)

                sp.wait_ge(vec_ones, 1)
                vectors(0, 0, TB * P)
                with sp.Fori(1, BLOCKS // TB - 1) as g:
                    own_wait(sp, gates_in, g * TB)
                    vectors(g, g * (TB * P), TB * P)
                last = (BLOCKS - TB) * P
                sp.wait_ge(gates_in, BLOCKS - TB)
                vectors(None, last, NODES - last)

                def store_x2(i, k, opening, g):
                    if not opening:
                        own_wait(sp, x2_stored[k], g * 16)
                    own_wait(sp, x2_ready, i + 1)
                    sp.dma_start(rows_view(env["x_rows"], i), acc[:, blk(i), 0:D]).then_inc(x2_stored[k], 16)

                in_turns(sp, BLOCKS, TB, (0, store_x2))
                with sp.Fori(0, BLOCKS // TB) as g:
                    for k in range(TB):
                        own_wait(sp, h2_ready, g * TB + k + 1)
                        sp.dma_start(rows_view(env["h2_rows"], g * TB + k), h2[:, k:k + 1, :]).then_inc(h2_stored[k], 16)
                for k in range(TB):
                    sp.wait_ge(x2_stored[k], 16 * BLOCKS // TB)
                    sp.wait_ge(h2_stored[k], 16 * BLOCKS // TB)

            @block.gpsimd
            def _(gp):
                nc.gpsimd.memset(nodes[:], 1.0).then_inc(vec_ones, 1)
                nc.gpsimd.memset(half[:], -0.5).then_inc(rstd_ready, 1)
                gp.wait_ge(deg_ready, 1)

                def gather(i, k, opening, g):
                    if not opening:
                        own_wait(gp, x2_ready, i - TB + 1)
                    nc.gpsimd.tensor_copy(deg_slot[:, :, k:k + 1], deg[:, :, blk(i)]).then_inc(z_slot, 1)
                    own_wait(gp, z_slot, i + 1)
                    for n, name in enumerate(("L1_gnn_z_in", "L1_gnn_z_out")):
                        gp.indirect_dma_start(out=z[:, k, n, :], out_offset=None, in_=A[name],
                                              in_offset=bass.IndirectOffsetOnAxis(ap=deg_slot[:, n, k:k + 1], axis=0)
                                              ).then_inc(z_in[k], 16)

                def rsqrt(n):
                    gp.wait_ge(stats_ready, n)
                    gp.wait_ge(rstd_ready, 2 * n - 1)
                    nc.gpsimd.tensor_tensor(rstd[:], rs["vare"][:], half[:], ALU.pow).then_inc(rstd_ready, 1)

                for k in range(TB):
                    gather(k, k, True, 0)
                rsqrt(1)
                with gp.Fori(1, BLOCKS // TB) as g:
                    for k in range(TB):
                        gather(g * TB + k, k, False, g)
                rsqrt(2)

            @block.tensor
            def _(pe):
                pe.wait_ge(loaded, 16 * LOADS)
                for n, (t, k) in enumerate((t, k) for t in (wq, wk) for k in range(DC)):
                    if n >= 2:
                        pe.wait_ge(prep, n - 1)
                    for j in range(DC):
                        last = nc.tensor.transpose(p_t[n % 2][:, j, :], t[:, k, j * P:(j + 1) * P], c["ident"][:])
                    last.then_inc(prep_t, 1)
                pe.wait_ge(prep, 4)
                pe.wait_ge(bq_ready, 1)
                for k in range(DC):
                    for j in range(DC):
                        last = nc.tensor.matmul(p_o[k][:, 0:D + 1], wqT[:, j, k * P:(k + 1) * P], wkT[:, j, :],
                                                start=j == 0, stop=j == DC - 1)
                    last.then_inc(prep_t, 1)
                for j in range(DC):
                    last = nc.tensor.matmul(p_g[0][:, 0:D + 1], bqs[:, j, :], wkT[:, j, :], start=j == 0, stop=j == DC - 1)
                last.then_inc(prep_t, 1)
                pe.wait_ge(prep, 7)

                def turn_sums(i, k, opening, g):
                    pe.wait_ge(sums_staged, i + 1)
                    if not opening or k >= 2:
                        pe.wait_ge(sums_copied, i - before(k) + 1)
                    for j in range(DC):
                        last = nc.tensor.transpose(p_t[k % 2][:, j, :], staged[:, k % 2, j * P:(j + 1) * P], c["ident"][:])
                    last.then_inc(sums_turned, 1)

                def sums_times_w(i, k, opening, g):
                    pe.wait_ge(sums_copied, i + 1)
                    if not opening or k >= 2:
                        pe.wait_ge(x1_ready, i - before(k) + 1)
                    for j in range(DC):
                        last = nc.tensor.matmul(p_o[k % 2][:, 0:D], turned[:, k % 2, j, :], w0[:, j, :],
                                                start=j == 0, stop=j == DC - 1)
                    last.then_inc(sums_w, 1)

                in_turns(pe, BLOCKS, TB, (1, sums_times_w), (0, turn_sums))

                def turn_attr(i, k, opening, g):
                    pe.wait_ge(attr_staged, i + 1)
                    if not opening or k >= 2:
                        pe.wait_ge(attr_copied, i - before(k) + 1)
                    nc.tensor.transpose(p_t[k % 2][:, 0, :], staged[:, k % 2, 0:ED], c["ident"][:]).then_inc(attr_turned, 1)

                def gate_arguments(i, k, opening, g):
                    if k == 0:
                        pe.wait_ge(vec_in, g * 32 + 32)
                    if not opening or k >= 2:
                        pe.wait_ge(gates_ready, i - before(k) + 1)
                    for n in range(2):
                        last = nc.tensor.matmul(p_g[k % 2][:, n * D:(n + 1) * D], nodes[:, n, k * P:(k + 1) * P],
                                                gate[:, n, :], start=True, stop=True)
                    last.then_inc(gates_in, 1)

                def attr_times_w(i, k, opening, g):
                    pe.wait_ge(attr_copied, i + 1)
                    if not opening or k >= 2:
                        pe.wait_ge(x2_ready, i - before(k) + 1)
                    nc.tensor.matmul(p_o[k % 2][:, 0:D], turned[:, k % 2, 0, :], wsum[:],
                                     start=True, stop=True).then_inc(attr_w, 1)

                in_turns(pe, BLOCKS, TB, (1, attr_times_w), (0, turn_attr), (0, gate_arguments))

                def turn_h2(i, k, opening, g):
                    pe.wait_ge(h2_ready, i + 1)
                    if not opening or k >= 2:
                        pe.wait_ge(h2_copied, i - before(k) + 1)
                    for j in range(DC):
                        last = nc.tensor.transpose(p_t[k % 2][:, j, :], h2[:, k, j * P:(j + 1) * P], c["ident"][:])
                    last.then_inc(h2_turned, 1)

                def h2_times_qk(i, k, opening, g):
                    pe.wait_ge(h2_copied, i + 1)
                    if not opening or k >= 2:
                        pe.wait_ge(q_ready, i - before(k) + 1)
                    for j in range(DC):
                        last = nc.tensor.matmul(p_o[k % 2][:, 0:D + 1], turned[:, k % 2, j, :], qk[:, j, :],
                                                start=j == 0, stop=j == DC - 1)
                    last.then_inc(h2_qk, 1)

                in_turns(pe, BLOCKS, TB, (1, h2_times_qk), (0, turn_h2))

            @block.scalar
            def _(ac):
                for n in range(2 * DC):
                    ac.wait_ge(prep_t, n + 1)
                    t, k = (wqT, wkT)[n // DC], n % DC
                    nc.scalar.activation(t[:, :, k * P:(k + 1) * P], p_t[n % 2][:], ACT.Copy).then_inc(prep, 1)
                ac.wait_ge(prep_t, 2 * DC + 3)
                for k in range(DC):
                    nc.scalar.activation(qk[:, k, :], p_o[k][:, 0:D + 1], ACT.Copy, scale=SCALE).then_inc(prep, 1)
                nc.scalar.activation(qkb[:], p_g[0][:, 0:D + 1], ACT.Copy, scale=SCALE).then_inc(prep, 1)

                def stage_sums(i, k, opening, g):
                    if not opening or k >= 2:
                        ac.wait_ge(sums_turned, i - before(k) + 1)
                    nc.scalar.activation(staged[:, k % 2, :], flat(acc[:, blk(i), 0:D]), ACT.Copy).then_inc(sums_staged, 1)

                def copy_sums(i, k, opening, g):
                    ac.wait_ge(sums_turned, i + 1)
                    if not opening or k >= 2:
                        ac.wait_ge(sums_w, i - before(k) + 1)
                    nc.scalar.activation(turned[:, k % 2, :, :], p_t[k % 2][:], ACT.Copy).then_inc(sums_copied, 1)

                in_turns(ac, BLOCKS, TB, (1, copy_sums), (0, stage_sums))
                ac.wait_ge(rstd_ready, 3)

                def norm_x1(i, k, opening, g):
                    if not opening or k >= 2:
                        ac.wait_ge(x2_ready, i - before(k) + 1)
                    nc.scalar.activation(h1[:, k % 2, :], flat(acc[:, blk(i), 0:D]), ACT.Relu, bias=nmr[:, blk(i)],
                                         scale=rstd[:, blk(i)]).then_inc(h1_ready, 1)

                def gates(i, k, opening, g):
                    ac.wait_ge(gates_in, i + 1)
                    nc.scalar.activation(sig[:, k % 2, :], p_g[k % 2][:], ACT.Sigmoid).then_inc(gates_ready, 1)

                def stage_attr(i, k, opening, g):
                    if opening and k < 2:
                        ac.wait_ge(sums_turned, BLOCKS)
                    else:
                        ac.wait_ge(attr_turned, i - before(k) + 1)
                    nc.scalar.activation(staged[:, k % 2, 0:ED], flat(acc[:, blk(i), D:D + ED]), ACT.Copy).then_inc(attr_staged, 1)

                def copy_attr(i, k, opening, g):
                    ac.wait_ge(attr_turned, i + 1)
                    if not opening or k >= 2:
                        ac.wait_ge(attr_w, i - before(k) + 1)
                    nc.scalar.activation(turned[:, k % 2, 0, :], p_t[k % 2][:, 0, :], ACT.Copy).then_inc(attr_copied, 1)

                in_turns(ac, BLOCKS, TB, (1, copy_attr), (0, stage_attr), (0, norm_x1), (0, gates))
                ac.wait_ge(rstd_ready, 5)

                def norm_x2(i, k, opening, g):
                    if not opening:
                        ac.wait_ge(h2_turned, i - TB + 1)
                        ac.wait_ge(h2_stored[k], g * 16)
                    nc.scalar.activation(h2[:, k, :], flat(acc[:, blk(i), 0:D]), ACT.Relu, bias=nmr[:, blk(i)],
                                         scale=rstd[:, blk(i)]).then_inc(h2_ready, 1)

                def copy_h2(i, k, opening, g):
                    ac.wait_ge(h2_turned, i + 1)
                    if not opening or k >= 2:
                        ac.wait_ge(h2_qk, i - before(k) + 1)
                    nc.scalar.activation(turned[:, k % 2, :, :], p_t[k % 2][:], ACT.Copy).then_inc(h2_copied, 1)

                in_turns(ac, BLOCKS, TB, (1, copy_h2), (0, norm_x2))

            @block.vector
            def _(ve):
                d = Counter(ve, dv)
                ve.wait_ge(loaded, 16 * LOADS)
                for j in range(DC):
                    last = nc.vector.tensor_scalar(bqs[:, j, :], c["ones"][:], bq[:, j:j + 1], None, ALU.mult)
                last.then_inc(bq_ready, 1)
                for n, t in enumerate((c["indeg"][:], acc[:, :, NW - 1])):
                    d.mark(nc.vector.tensor_scalar(deg_f[:, n, :], t, float(DEG_MAX), None, ALU.min))
                d.wait()
                nc.vector.tensor_copy(deg[:], deg_f[:]).then_inc(deg_ready, 1)

                n0 = d.n

                def add_bias(i, k, opening, g):
                    ve.wait_ge(x_in[k], g * 16 + 16)
                    nc.vector.tensor_tensor(xin[:, k, :], xin[:, k, :], b0[:], ALU.add).then_inc(dv, 1)

                def make_x1(i, k, opening, g):
                    ve.wait_ge(dv, i + (n0 + 1))
                    ve.wait_ge(sums_w, i + 1)
                    nc.vector.tensor_tensor(flat(acc[:, blk(i), 0:D]), p_o[k % 2][:, 0:D], xin[:, k, :], ALU.add).then_inc(x1_ready, 1)

                def x1_stats(i, k, opening, g):
                    ve.wait_ge(x1_ready, i + 1)
                    nc.vector.bn_stats(flat(stats[:, blk(i), :]), flat(acc[:, blk(i), 0:D])).then_inc(x_used, 1)

                in_turns(ve, BLOCKS, TB, (2, x1_stats), (1, make_x1), (0, add_bias))
                d.n = n0 + BLOCKS
                ve.wait_ge(x_used, BLOCKS)
                row_stats(nc, d, stats, rs).then_inc(stats_ready, 1)
                ve.wait_ge(rstd_ready, 2)
                nc.vector.scalar_tensor_tensor(out=nmr[:], in0=rs["msum"][:], scalar=-0.5, in1=rstd[:],
                                               op0=ALU.mult, op1=ALU.mult).then_inc(rstd_ready, 1)

                n1 = d.n
                STEPS2 = 6

                def make_x2(i, k, opening, g):
                    a = flat(acc[:, blk(i), 0:D])
                    done = i * STEPS2 + n1

                    def add(n, t):
                        nc.vector.tensor_tensor(a, a, t, ALU.add).then_inc(dv, 1)
                        ve.wait_ge(dv, done + n)

                    ve.wait_ge(h1_ready, i + 1)
                    add(1, h1[:, k % 2, :])
                    nc.vector.scalar_tensor_tensor(out=a, in0=bsum[:], scalar=flat(acc[:, blk(i), NW - 1:NW]), in1=a,
                                                   op0=ALU.mult, op1=ALU.add).then_inc(dv, 1)
                    ve.wait_ge(dv, done + 2)
                    ve.wait_ge(z_in[k], g * 32 + 32)
                    add(3, z[:, k, 0, :])
                    add(4, z[:, k, 1, :])
                    ve.wait_ge(gates_ready, i + 1)
                    add(5, sig[:, k % 2, 0:D])
                    add(6, sig[:, k % 2, D:2 * D])
                    ve.wait_ge(attr_w, i + 1)
                    nc.vector.tensor_tensor(a, a, p_o[k % 2][:, 0:D], ALU.add).then_inc(x2_ready, 1)

                def x2_stats(i, k, opening, g):
                    ve.wait_ge(x2_ready, i + 1)
                    nc.vector.bn_stats(flat(stats[:, blk(i), :]), flat(acc[:, blk(i), 0:D]))

                in_turns(ve, BLOCKS, TB, (1, x2_stats), (0, make_x2))
                d.n = n1 + BLOCKS * STEPS2
                d.link(nc.vector.tensor_copy(rs["m2"][:], rs["m2"][:]))
                row_stats(nc, d, stats, rs).then_inc(stats_ready, 1)
                ve.wait_ge(rstd_ready, 4)
                nc.vector.scalar_tensor_tensor(out=nmr[:], in0=rs["msum"][:], scalar=-0.5, in1=rstd[:],
                                               op0=ALU.mult, op1=ALU.mult).then_inc(rstd_ready, 1)

                def make_q(i, k, opening, g):
                    ve.wait_ge(h2_qk, i + 1)
                    ve.wait_ge(x2_stored[k], g * 16 + 16)
                    nc.vector.tensor_tensor(flat(acc[:, blk(i), 0:D + 1]), p_o[k % 2][:, 0:D + 1], qkb[:],
                                            ALU.add).then_inc(q_ready, 1)

                in_turns(ve, BLOCKS, TB, (0, make_q))


def attention(env):
    nc, A, c, sb, ps, sem = (env[k] for k in ("nc", "A", "c", "sb", "ps", "sem"))
    query, acc = env["nodes"], env["sums"]
    R = 2 * UNROLL
    H = UNROLL
    FAR = 2.0 ** 110
    LOWEST = -1e30
    FAR_T, HOT_T, ASK, DOT, MASK, MASK_T, MAX, LOOK, EXP, SUM, ADD = range(1, 12)
    AHEAD = 4
    with nc.cleanup_on_exit(), ExitStack() as ctx:
        idx = sb(ctx, "a_idx", [P, R], I32)
        row = sb(ctx, "a_row", [P, R, D + 1])
        far = sb(ctx, "a_far", [P, H, P])
        hotT = sb(ctx, "a_hotT", [P, H, P])
        prod = sb(ctx, "a_prod", [P, 2, D + 1])
        dot = sb(ctx, "a_dot", [P, H])
        score = sb(ctx, "a_score", [P, H])
        masked = sb(ctx, "a_masked", [P, H, P])
        part = sb(ctx, "a_part", [P, H, P])
        tmax = sb(ctx, "a_tmax", [P, H])
        mnew = sb(ctx, "a_mnew", [P, H])
        drop = sb(ctx, "a_drop", [P, H])
        fade = sb(ctx, "a_fade", [P, H])
        mneg = sb(ctx, "a_mneg", [P, H])
        m = sb(ctx, "a_m", [P, BLOCKS])
        ew = sb(ctx, "a_ew", [P, TILES])
        web = sb(ctx, "a_web", [P, 2])
        p_hot = ps(ctx, "a_p_hot", [P, P])
        p_q = [ps(ctx, f"a_p_q{k}", [P, D + 1]) for k in range(2)]
        p_m = [ps(ctx, f"a_p_m{k}", [P, P]) for k in range(2)]
        p_l = ps(ctx, "a_p_l", [P, 1])
        p_s = [ps(ctx, f"a_p_s{k}", [P, D + 1]) for k in range(2)]

        names = ("loaded", "ones", "begun", "idx_ready", "far_ready", "hot_turned", "hotT_ready", "asked",
                 "dotted", "scored", "masked", "mask_turned", "maxed", "mnew", "dropped", "m_kept", "faded",
                 "looked_up", "m_negated", "part_ready", "summed", "added")
        S = {n: sem("a_" + n) for n in names}
        row_in = [sem(f"a_row_in{k}") for k in range(R)]

        with nc.Block() as block:
            @block.sync
            def _(sp):
                sp.dma_start(web[:, 0:1], A["L2_gnn_we"].broadcast_to([P, 1])).then_inc(S["loaded"], 16)
                sp.dma_start(web[:, 1:2], A["L2_gnn_be"].rearrange("(a b) -> a b", a=1).broadcast_to([P, 1])
                             ).then_inc(S["loaded"], 16)
                sp.wait_ge(S["loaded"], 32)

            @block.gpsimd
            def _(gp):
                nc.gpsimd.memset(row[:], 1.0).then_inc(S["ones"], 1)
                gp.wait_ge(S["ones"], 1)

                def gather(i, k, opening, g):
                    if k % 4 == 0:
                        own_wait(gp, S["idx_ready"], g * (R // 4) + (k // 4 + 1))
                    if not opening:
                        own_wait(gp, S["summed"], i - R + 1)
                    gp.indirect_dma_start(out=row[:, k, 0:D], out_offset=None, in_=env["h2_rows"],
                                          in_offset=bass.IndirectOffsetOnAxis(ap=idx[:, k:k + 1], axis=0)
                                          ).then_inc(row_in[k], 16)

                in_turns(gp, TILES, R, (0, gather))

            @block.scalar
            def _(ac):
                def indices(i, k, opening, g):
                    if k % 4:
                        return
                    if not opening:
                        for j in range(k, k + 4):
                            ac.wait_ge(row_in[j], g * 16)
                    nc.scalar.activation(idx[:, k:k + 4], c["dsrc"][:, bass.ds(i, 4)], ACT.Copy).then_inc(S["idx_ready"], 1)

                def copy_hot(i, k, opening, g):
                    ac.wait_ge(S["hot_turned"], i + 1)
                    nc.scalar.activation(hotT[:, k % H, :], p_hot, ACT.Relu, bias=c["ones"][:, 0:1]).then_inc(S["hotT_ready"], 1)

                def mask(i, k, opening, g):
                    ac.wait_ge(S["scored"], i + 1)
                    nc.scalar.activation(masked[:, k % H, :], far[:, k % H, :], ACT.Identity,
                                         bias=score[:, k % H:k % H + 1]).then_inc(S["masked"], 1)

                def exponents(i, k, opening, g):
                    ac.wait_ge(S["dropped"], i + 1)
                    nc.scalar.activation(fade[:, k % H:k % H + 1], drop[:, k % H:k % H + 1], ACT.Exp).then_inc(S["faded"], 1)
                    ac.wait_ge(S["looked_up"], i + 1)
                    nc.scalar.activation(mneg[:, k % H:k % H + 1], p_l, ACT.Copy, scale=-1.0).then_inc(S["m_negated"], 1)
                    ac.wait_ge(S["m_negated"], i + 1)
                    ac.wait_ge(S["masked"], i + 1)
                    nc.scalar.activation(part[:, k % H, :], masked[:, k % H, :], ACT.Exp,
                                         bias=mneg[:, k % H:k % H + 1]).then_inc(S["part_ready"], 1)

                in_turns(ac, TILES, R, (AHEAD + HOT_T, copy_hot), (AHEAD + EXP, exponents), (AHEAD + MASK, mask), (0, indices))

            @block.tensor
            def _(pe):
                blocks = []

                def load_blocks(i, k):
                    if k == 0:
                        _, blocks[:] = nc.values_load_multi_w_load_instructions(
                            c["dblk"][0:1, bass.ds(i + (PAD - ASK), R)],
                            engines=(PE_E,), min_val=0, max_val=BLOCKS - 1,
                            skip_runtime_bounds_check_because=BLOCK_RANGE)

                def turn_far(i, k, opening, g):
                    pe.wait_ge(S["far_ready"], i + 1)
                    if not opening or k >= 1:
                        pe.wait_ge(S["hotT_ready"], i)
                    nc.tensor.transpose(p_hot, far[:, k % H, :], c["ident"][:]).then_inc(S["hot_turned"], 1)

                def ask(i, k, opening, g):
                    pe.wait_ge(S["hotT_ready"], i + 1)
                    if not opening or k >= 2:
                        pe.wait_ge(S["dotted"], i - 1)
                    b = blocks[(k + ASK) % R]
                    nc.tensor.matmul(p_q[k % 2], hotT[:, k % H, :], query[:, bass.ds(b, 1), 0:D + 1].rearrange("p a d -> p (a d)"),
                                     start=True, stop=True).then_inc(S["asked"], 1)

                def turn_masked(i, k, opening, g):
                    pe.wait_ge(S["masked"], i + 1)
                    if not opening or k >= 2:
                        pe.wait_ge(S["maxed"], i - 1)
                    nc.tensor.transpose(p_m[k % 2], masked[:, k % H, :], c["ident"][:]).then_inc(S["mask_turned"], 1)

                def look_up(i, k, opening, g):
                    pe.wait_ge(S["mnew"], i + 1)
                    if not opening or k >= 1:
                        pe.wait_ge(S["m_negated"], i)
                    nc.tensor.matmul(p_l, hotT[:, k % H, :], mnew[:, k % H:k % H + 1], start=True, stop=True).then_inc(S["looked_up"], 1)

                def sum_rows(i, k, opening, g):
                    pe.wait_ge(S["part_ready"], i + 1)
                    pe.wait_ge(row_in[k], g * 16 + 16)
                    if not opening or k >= 2:
                        pe.wait_ge(S["added"], i - 1)
                    nc.tensor.matmul(p_s[k % 2], part[:, k % H, :], row[:, k, :], start=True, stop=True).then_inc(S["summed"], 1)

                in_turns(pe, TILES, R, (SUM, sum_rows), (ASK, ask), (MASK_T, turn_masked),
                         (LOOK, look_up), (FAR_T, turn_far), begin=load_blocks)

            @block.vector
            def _(ve):
                nc.vector.memset(acc[:], 0.0).then_inc(S["begun"], 1)
                nc.vector.memset(m[:], LOWEST).then_inc(S["begun"], 1)
                ve.wait_ge(S["loaded"], 32)
                nc.vector.tensor_scalar(ew[:], c["dwgt"][:], web[:, 0:1], web[:, 1:2], ALU.mult, ALU.add).then_inc(S["begun"], 1)
                ve.wait_ge(S["begun"], 3)
                blocks = []

                def load_blocks(i, k):
                    if k == 0:
                        _, blocks[:] = nc.values_load_multi_w_load_instructions(
                            c["dblk"][0:1, bass.ds(i + (PAD - ADD), R + ADD - MAX)],
                            engines=(DVE_E,), min_val=0, max_val=BLOCKS - 1,
                            skip_runtime_bounds_check_because=BLOCK_RANGE)

                def make_far(i, k, opening, g):
                    nc.vector.tensor_scalar(far[:, k % H, :], c["iota"][:], c["dloc"][:, bass.ds(i, 1)], -FAR,
                                            ALU.not_equal, ALU.mult).then_inc(S["far_ready"], 1)

                def dots(i, k, opening, g):
                    ve.wait_ge(S["asked"], i + 1)
                    ve.wait_ge(row_in[k], g * 16 + 16)
                    nc.vector.tensor_tensor_reduce(out=prod[:, k % 2, :], in0=p_q[k % 2], in1=row[:, k, :], scale=1.0,
                                                   scalar=0.0, op0=ALU.mult, op1=ALU.add,
                                                   accum_out=dot[:, k % H:k % H + 1]).then_inc(S["dotted"], 1)

                def scores(i, k, opening, g):
                    ve.wait_ge(S["dotted"], i + 1)
                    nc.vector.tensor_tensor(score[:, k % H:k % H + 1], dot[:, k % H:k % H + 1], ew[:, bass.ds(i, 1)], ALU.add).then_inc(S["scored"], 1)

                def tile_maximum(i, k, opening, g):
                    ve.wait_ge(S["mask_turned"], i + 1)
                    nc.vector.reduce_max(tmax[:, k % H:k % H + 1], p_m[k % 2], AX.X).then_inc(S["maxed"], 1)

                def new_maximum(i, k, opening, g):
                    b = bass.ds(blocks[(k + MAX) % R + ADD - MAX], 1)
                    ve.wait_ge(S["maxed"], i + 1)
                    ve.wait_ge(S["m_kept"], i)
                    nc.vector.tensor_tensor(mnew[:, k % H:k % H + 1], m[:, b], tmax[:, k % H:k % H + 1], ALU.max).then_inc(S["mnew"], 1)

                def maximum_drop(i, k, opening, g):
                    b = bass.ds(blocks[(k + MAX) % R + ADD - MAX], 1)
                    ve.wait_ge(S["mnew"], i + 1)
                    nc.vector.tensor_tensor(drop[:, k % H:k % H + 1], m[:, b], mnew[:, k % H:k % H + 1], ALU.subtract).then_inc(S["dropped"], 1)

                def keep_maximum(i, k, opening, g):
                    b = bass.ds(blocks[(k + MAX) % R + ADD - MAX], 1)
                    ve.wait_ge(S["dropped"], i + 1)
                    nc.vector.tensor_tensor(m[:, b], m[:, b], tmax[:, k % H:k % H + 1], ALU.max).then_inc(S["m_kept"], 1)

                def add(i, k, opening, g):
                    b = blocks[(k + ADD) % R]
                    ve.wait_ge(S["summed"], i + 1)
                    ve.wait_ge(S["faded"], i + 1)
                    ve.wait_ge(S["added"], i)
                    s = acc[:, bass.ds(b, 1), 0:D + 1].rearrange("p a d -> p (a d)")
                    nc.vector.scalar_tensor_tensor(out=s, in0=s, scalar=fade[:, k % H:k % H + 1], in1=p_s[k % 2],
                                                   op0=ALU.mult, op1=ALU.add).then_inc(S["added"], 1)

                in_turns(ve, TILES, R, (MAX, tile_maximum), (ADD, add), (MAX, new_maximum),
                         (DOT, dots), (MAX, maximum_drop), (0, make_far), (DOT, scores), (MAX, keep_maximum),
                         begin=load_blocks)


def relation_sums(env):
    nc, c, sb, ps, sem = (env[k] for k in ("nc", "c", "sb", "ps", "sem"))
    acc = env["sums"]
    R = UNROLL
    LAG = 2
    with nc.cleanup_on_exit(), ExitStack() as ctx:
        idx = sb(ctx, "r_idx", [P, R], I32)
        row = sb(ctx, "r_row", [P, R, DW])
        hot = sb(ctx, "r_hot", [P, R, P])
        p_s = [ps(ctx, f"r_p_s{k}", [P, DW]) for k in range(4)]
        idx_ready, hot_ready, summed, added, cleared = (sem("r_" + n) for n in ("idx_ready", "hot_ready", "summed", "added", "cleared"))
        row_in = [sem(f"r_row_in{k}") for k in range(R)]

        with nc.Block() as block:
            @block.gpsimd
            def _(gp):
                def gather(i, k, opening, g):
                    if k % 4 == 0:
                        own_wait(gp, idx_ready, g * (R // 4) + (k // 4 + 1))
                    if not opening:
                        own_wait(gp, summed, i - R + 1)
                    gp.indirect_dma_start(out=row[:, k, 0:D], out_offset=None, in_=env["h3_rows"],
                                          in_offset=bass.IndirectOffsetOnAxis(ap=idx[:, k:k + 1], axis=0)
                                          ).then_inc(row_in[k], 16)

                in_turns(gp, TILES, R, (0, gather))

            @block.scalar
            def _(ac):
                def indices(i, k, opening, g):
                    if k % 4:
                        return
                    if not opening:
                        for j in range(k, k + 4):
                            ac.wait_ge(row_in[j], g * 16)
                    nc.scalar.activation(idx[:, k:k + 4], c["dsrc"][:, bass.ds(i, 4)], ACT.Copy).then_inc(idx_ready, 1)

                in_turns(ac, TILES, R, (0, indices))

            @block.tensor
            def _(pe):
                def sum_rows(i, k, opening, g):
                    pe.wait_ge(hot_ready, i * 2 + 2)
                    pe.wait_ge(row_in[k], g * 16 + 16)
                    if not opening or k >= 4:
                        pe.wait_ge(added, i - 3)
                    nc.tensor.matmul(p_s[k % 4], hot[:, k, :], row[:, k, :], start=True, stop=True).then_inc(summed, 1)

                in_turns(pe, TILES, R, (0, sum_rows))

            @block.vector
            def _(ve):
                nc.vector.memset(acc[:], 0.0).then_inc(cleared, 1)
                ve.wait_ge(cleared, 1)
                blocks = []

                def load_blocks(i, k):
                    if k == 0:
                        _, blocks[:] = nc.values_load_multi_w_load_instructions(
                            c["dblk"][0:1, bass.ds(i + (PAD - LAG), R + LAG)], engines=(DVE_E,), min_val=0, max_val=BLOCKS - 1,
                            skip_runtime_bounds_check_because=BLOCK_RANGE)

                def hots(i, k, opening, g):
                    if not opening:
                        ve.wait_ge(summed, i - R + 1)
                    nc.vector.tensor_scalar(hot[:, k, :], c["iota"][:], c["dloc"][:, bass.ds(i, 1)], None,
                                            ALU.is_equal).then_inc(hot_ready, 1)
                    nc.vector.tensor_scalar(row[:, k, D:DW], c["iota"][:, 0:RELS], c["dtyp"][:, bass.ds(i, 1)], None,
                                            ALU.is_equal).then_inc(hot_ready, 1)

                def add(i, k, opening, g):
                    b = blocks[LAG + (k + LAG) % R - LAG]
                    ve.wait_ge(summed, i + 1)
                    ve.wait_ge(added, i)
                    s = acc[:, bass.ds(b, 1), :].rearrange("p a d -> p (a d)")
                    nc.vector.tensor_tensor(s, s, p_s[k % 4], ALU.add).then_inc(added, 1)

                in_turns(ve, TILES, R, (LAG, add), (0, hots), begin=load_blocks)


def layer_2(env):
    nc, A, c, sb, ps, sem = (env[k] for k in ("nc", "A", "c", "sb", "ps", "sem"))
    sums = env["sums"]
    val = env["nodes"]
    TB = TURN_BLOCKS
    F = 2 * D
    FC = F // P
    with nc.cleanup_on_exit(), ExitStack() as ctx:
        wv = sb(ctx, "e_wv", [P, DC, D])
        ws = sb(ctx, "e_ws", [P, DC, D])
        w1 = sb(ctx, "e_w1", [P, DC, F])
        w2 = sb(ctx, "e_w2", [P, FC, D])
        b_ff1 = sb(ctx, "b_ff1_cols", [P, FC])
        vec = {n: sb(ctx, "e_" + n, [P, D]) for n in ("bv", "bs", "g1", "b1", "g2", "b2", "b_ff2")}
        xin = sb(ctx, "e_xin", [P, TB, D])
        staged = sb(ctx, "e_staged", [P, 2, D])
        turned = sb(ctx, "e_turned", [P, 2, 2 * DC, P])
        norm = sb(ctx, "e_norm", [P, 2, D])
        y = sb(ctx, "e_y", [P, TB, D])
        hid = sb(ctx, "e_hid", [P, 2, FC, P])
        stats = sb(ctx, "e_stats", [P, BLOCKS, 6])
        rs = {n: sb(ctx, "e_" + n, [P, BLOCKS]) for n in ("msum", "mdif", "m2", "vare")}
        half, rstd, nmr, inv, coef = (sb(ctx, "e_" + n, [P, BLOCKS]) for n in ("half", "rstd", "nmr", "inv", "coef"))
        p_t = [ps(ctx, f"e_p_t{k}", [P, 2 * DC, P]) for k in range(2)]
        p_o = [ps(ctx, f"e_p_o{k}", [P, D]) for k in range(2)]
        p_f = [ps(ctx, f"e_p_f{k}", [P, FC, P]) for k in range(2)]

        names = ("loaded", "inv_ready", "staged", "turned", "copied", "projected", "res1", "res1_done", "bias1",
                 "stats_ready", "rstd_ready", "norm1", "y_ready", "y_turned", "y_copied", "hid_in", "hid_ready",
                 "ffn", "bias2", "res2_done", "norm2", "x3_ready", "h3_ready", "dv")
        S = {n: sem("e_" + n) for n in names}
        h2_in = [sem(f"e_h2_in{k}") for k in range(TB)]
        x2_in = [sem(f"e_x2_in{k}") for k in range(TB)]
        h3_stored = [sem(f"e_h3_stored{k}") for k in range(TB)]
        LOADS = 5 + len(vec)

        def row(name):
            return A[name].rearrange("(a d) -> a d", a=1)

        def kchunks(ap):
            return ap.rearrange("(k p) d -> p k d", p=P)

        def blk(i):
            return bass.ds(i, 1)

        def flat(t):
            return t.rearrange("p a d -> p (a d)")

        with nc.Block() as block:
            @block.sync
            def _(sp):
                for t, n in ((wv, "L2_gnn_wv"), (ws, "L2_gnn_ws"), (w1, "L2_gnn_w_ff1"), (w2, "L2_gnn_w_ff2")):
                    sp.dma_start(t[:], kchunks(A[n])).then_inc(S["loaded"], 16)
                sp.dma_start(b_ff1[:], A["L2_gnn_b_ff1"].rearrange("(k p) -> p k", p=P),
                             allow_slow_non_contiguous=True).then_inc(S["loaded"], 16)
                for n, t in vec.items():
                    sp.dma_start(t[:], row("L2_gnn_" + n).broadcast_to([P, D])).then_inc(S["loaded"], 16)

                def load_h2(i, k, opening, g):
                    if not opening:
                        own_wait(sp, S["res1_done"], i - TB + 1)
                    sp.dma_start(xin[:, k:k + 1, :], rows_view(env["h2_rows"], i)).then_inc(h2_in[k], 16)

                in_turns(sp, BLOCKS, TB, (0, load_h2))

                def load_x2(i, k, opening, g):
                    if opening:
                        own_wait(sp, S["res1_done"], BLOCKS - TB + k + 1)
                    else:
                        own_wait(sp, S["x3_ready"], i - TB + 1)
                    sp.dma_start(xin[:, k:k + 1, :], rows_view(env["x_rows"], i)).then_inc(x2_in[k], 16)

                in_turns(sp, BLOCKS, TB, (0, load_x2))

                def store_h3(i, k, opening, g):
                    own_wait(sp, S["h3_ready"], i + 1)
                    sp.dma_start(rows_view(env["h3_rows"], i), y[:, k:k + 1, :]).then_inc(h3_stored[k], 16)

                in_turns(sp, BLOCKS, TB, (0, store_h3))
                for k in range(TB):
                    sp.wait_ge(h3_stored[k], 16 * BLOCKS // TB)

            @block.gpsimd
            def _(gp):
                nc.gpsimd.memset(half[:], -0.5).then_inc(S["rstd_ready"], 1)
                gp.wait_ge(S["loaded"], 16 * LOADS)

                def add_bs(i, k, opening, g):
                    own_wait(gp, h2_in[k], g * 16 + 16)
                    if not opening or k >= 2:
                        own_wait(gp, S["res1_done"], i - before(k) + 1)
                    nc.gpsimd.tensor_tensor(norm[:, k % 2, :], xin[:, k, :], vec["bs"][:], ALU.add).then_inc(S["bias1"], 1)

                in_turns(gp, BLOCKS, TB, (0, add_bs))

                def rsqrt(n):
                    gp.wait_ge(S["stats_ready"], n)
                    gp.wait_ge(S["rstd_ready"], 2 * n - 1)
                    nc.gpsimd.tensor_tensor(rstd[:], rs["vare"][:], half[:], ALU.pow).then_inc(S["rstd_ready"], 1)

                for n in range(3):
                    rsqrt(n + 1)

            @block.tensor
            def _(pe):
                pe.wait_ge(S["loaded"], 16 * LOADS)

                def turn_rows(i, k, opening, g):
                    pe.wait_ge(S["staged"], i + 1)
                    pe.wait_ge(h2_in[k], g * 16 + 16)
                    if not opening or k >= 2:
                        pe.wait_ge(S["copied"], i - before(k) + 1)
                    for j in range(DC):
                        nc.tensor.transpose(p_t[k % 2][:, j, :], staged[:, k % 2, j * P:(j + 1) * P], c["ident"][:])
                        last = nc.tensor.transpose(p_t[k % 2][:, DC + j, :], xin[:, k, j * P:(j + 1) * P], c["ident"][:])
                    last.then_inc(S["turned"], 1)

                def project(i, k, opening, g):
                    pe.wait_ge(S["copied"], i + 1)
                    if not opening or k >= 2:
                        pe.wait_ge(S["res1"], i - before(k) + 1)
                    for n, w in enumerate((wv, ws)):
                        for j in range(DC):
                            last = nc.tensor.matmul(p_o[k % 2], turned[:, k % 2, n * DC + j, :], w[:, j, :],
                                                    start=n + j == 0, stop=n + j == DC)
                    last.then_inc(S["projected"], 1)

                in_turns(pe, BLOCKS, TB, (1, project), (0, turn_rows))

                def turn_y(i, k, opening, g):
                    pe.wait_ge(S["y_ready"], i + 1)
                    if not opening or k >= 2:
                        pe.wait_ge(S["y_copied"], i - before(k) + 1)
                    for j in range(DC):
                        last = nc.tensor.transpose(p_t[k % 2][:, j, :], y[:, k, j * P:(j + 1) * P], c["ident"][:])
                    last.then_inc(S["y_turned"], 1)

                def ffn_in(i, k, opening, g):
                    pe.wait_ge(S["y_copied"], i + 1)
                    if not opening or k >= 2:
                        pe.wait_ge(S["hid_ready"], (i - before(k) + 1) * FC)
                    for f in range(FC):
                        for j in range(DC):
                            last = nc.tensor.matmul(p_f[k % 2][:, f, :], w1[:, j, f * P:(f + 1) * P],
                                                    turned[:, k % 2, j, :], start=j == 0, stop=j == DC - 1)
                    last.then_inc(S["hid_in"], 1)

                def ffn_out(i, k, opening, g):
                    pe.wait_ge(S["hid_ready"], (i + 1) * FC)
                    if not opening or k >= 2:
                        pe.wait_ge(S["res2_done"], i - before(k) + 1)
                    for f in range(FC):
                        last = nc.tensor.matmul(p_o[k % 2], hid[:, k % 2, f, :], w2[:, f, :], start=f == 0, stop=f == FC - 1)
                    last.then_inc(S["ffn"], 1)

                in_turns(pe, BLOCKS, TB, (2, ffn_out), (1, ffn_in), (0, turn_y))

            @block.scalar
            def _(ac):
                ac.wait_ge(S["inv_ready"], 2)

                def stage(i, k, opening, g):
                    if not opening or k >= 2:
                        ac.wait_ge(S["turned"], i - before(k) + 1)
                    nc.scalar.activation(staged[:, k % 2, :], flat(sums[:, blk(i), 0:D]), ACT.Copy,
                                         scale=inv[:, blk(i)]).then_inc(S["staged"], 1)

                def copy_rows(i, k, opening, g):
                    ac.wait_ge(S["turned"], i + 1)
                    if not opening or k >= 2:
                        ac.wait_ge(S["projected"], i - before(k) + 1)
                    nc.scalar.activation(turned[:, k % 2, :, :], p_t[k % 2], ACT.Copy).then_inc(S["copied"], 1)

                in_turns(ac, BLOCKS, TB, (1, copy_rows), (0, stage))
                ac.wait_ge(S["rstd_ready"], 3)

                def normalise(done, out):
                    def step(i, k, opening, g):
                        if not opening or k >= 2:
                            ac.wait_ge(S[done], i - before(k) + 1)
                        nc.scalar.activation(norm[:, k % 2, :], flat(val[:, blk(i), 0:D]), ACT.Identity,
                                             bias=nmr[:, blk(i)], scale=rstd[:, blk(i)]).then_inc(S[out], 1)
                    return step

                def copy_y(i, k, opening, g):
                    ac.wait_ge(S["y_turned"], i + 1)
                    if not opening or k >= 2:
                        ac.wait_ge(S["hid_in"], i - before(k) + 1)
                    nc.scalar.activation(turned[:, k % 2, 0:DC, :], p_t[k % 2][:, 0:DC, :], ACT.Copy).then_inc(S["y_copied"], 1)

                def hidden(i, k, opening, g):
                    ac.wait_ge(S["hid_in"], i + 1)
                    if not opening or k >= 2:
                        ac.wait_ge(S["ffn"], i - before(k) + 1)
                    for f in range(FC):
                        nc.scalar.activation(hid[:, k % 2, f, :], p_f[k % 2][:, f, :], ACT.Gelu_apprx_tanh,
                                             bias=b_ff1[:, f:f + 1]).then_inc(S["hid_ready"], 1)

                in_turns(ac, BLOCKS, TB, (2, hidden), (1, copy_y), (0, normalise("y_ready", "norm1")))
                ac.wait_ge(S["rstd_ready"], 5)
                in_turns(ac, BLOCKS, TB, (0, normalise("x3_ready", "norm2")))
                ac.wait_ge(S["rstd_ready"], 7)

                def norm_x3(i, k, opening, g):
                    if not opening:
                        ac.wait_ge(h3_stored[k], g * 16)
                    nc.scalar.activation(y[:, k, :], flat(val[:, blk(i), 0:D]), ACT.Relu, bias=nmr[:, blk(i)],
                                         scale=rstd[:, blk(i)]).then_inc(S["h3_ready"], 1)

                in_turns(ac, BLOCKS, TB, (0, norm_x3))

            @block.vector
            def _(ve):
                d = Counter(ve, S["dv"])
                d.link(nc.vector.tensor_scalar(coef[:], sums[:, :, D], 1e-12, None, ALU.max))
                nc.vector.reciprocal(inv[:], coef[:]).then_inc(S["inv_ready"], 1)
                ve.wait_ge(S["inv_ready"], 1)
                nc.vector.tensor_tensor(coef[:], sums[:, :, D], inv[:], ALU.mult).then_inc(S["inv_ready"], 1)
                ve.wait_ge(S["inv_ready"], 2)
                ve.wait_ge(S["loaded"], 16 * LOADS)

                def residual1(i, k, opening, g):
                    v = flat(val[:, blk(i), 0:D])
                    ve.wait_ge(S["projected"], i + 1)
                    ve.wait_ge(S["bias1"], i + 1)
                    nc.vector.tensor_tensor(v, p_o[k % 2], norm[:, k % 2, :], ALU.add).then_inc(S["res1"], 1)
                    ve.wait_ge(S["res1"], i + 1)
                    nc.vector.scalar_tensor_tensor(out=v, in0=vec["bv"][:], scalar=coef[:, blk(i)], in1=v,
                                                   op0=ALU.mult, op1=ALU.add).then_inc(S["res1_done"], 1)

                def stats1(i, k, opening, g):
                    ve.wait_ge(S["res1_done"], i + 1)
                    nc.vector.bn_stats(flat(stats[:, blk(i), :]), flat(val[:, blk(i), 0:D]))

                def whole_stats(n):
                    d.link(nc.vector.memset(rs["m2"][:], 0.0))
                    row_stats(nc, d, stats, rs).then_inc(S["stats_ready"], 1)
                    ve.wait_ge(S["rstd_ready"], 2 * n)
                    nc.vector.scalar_tensor_tensor(out=nmr[:], in0=rs["msum"][:], scalar=-0.5, in1=rstd[:],
                                                   op0=ALU.mult, op1=ALU.mult).then_inc(S["rstd_ready"], 1)

                in_turns(ve, BLOCKS, TB, (1, stats1), (0, residual1))
                whole_stats(1)

                def make_y(n1):
                    def step(i, k, opening, g):
                        ve.wait_ge(S["norm1"], i + 1)
                        nc.vector.tensor_tensor(y[:, k, :], norm[:, k % 2, :], vec["g1"][:], ALU.mult).then_inc(S["dv"], 1)
                        ve.wait_ge(S["dv"], i + (n1 + 1))
                        nc.vector.tensor_tensor(y[:, k, :], y[:, k, :], vec["b1"][:], ALU.add).then_inc(S["y_ready"], 1)
                    return step

                def residual2(i, k, opening, g):
                    v = flat(val[:, blk(i), 0:D])
                    ve.wait_ge(S["y_ready"], i + 1)
                    nc.vector.tensor_tensor(v, y[:, k, :], vec["b_ff2"][:], ALU.add).then_inc(S["bias2"], 1)
                    ve.wait_ge(S["bias2"], i + 1)
                    ve.wait_ge(S["ffn"], i + 1)
                    nc.vector.tensor_tensor(v, v, p_o[k % 2], ALU.add).then_inc(S["res2_done"], 1)

                def stats2(i, k, opening, g):
                    ve.wait_ge(S["res2_done"], i + 1)
                    nc.vector.bn_stats(flat(stats[:, blk(i), :]), flat(val[:, blk(i), 0:D]))

                in_turns(ve, BLOCKS, TB, (4, stats2), (3, residual2), (0, make_y(d.n)))
                d.n += BLOCKS
                whole_stats(2)

                def make_x3(n2):
                    def step(i, k, opening, g):
                        v = flat(val[:, blk(i), 0:D])
                        ve.wait_ge(S["norm2"], i + 1)
                        nc.vector.tensor_tensor(v, norm[:, k % 2, :], vec["g2"][:], ALU.mult).then_inc(S["dv"], 1)
                        ve.wait_ge(S["dv"], i * 2 + (n2 + 1))
                        nc.vector.tensor_tensor(v, v, vec["b2"][:], ALU.add).then_inc(S["dv"], 1)
                        ve.wait_ge(S["dv"], i * 2 + (n2 + 2))
                        ve.wait_ge(x2_in[k], g * 16 + 16)
                        nc.vector.tensor_tensor(v, v, xin[:, k, :], ALU.add).then_inc(S["x3_ready"], 1)
                    return step

                def stats3(i, k, opening, g):
                    ve.wait_ge(S["x3_ready"], i + 1)
                    nc.vector.bn_stats(flat(stats[:, blk(i), :]), flat(val[:, blk(i), 0:D]))

                in_turns(ve, BLOCKS, TB, (1, stats3), (0, make_x3(d.n)))
                d.n += 2 * BLOCKS
                whole_stats(3)


def layer_3(env):
    nc, A, c, sb, ps, sem = (env[k] for k in ("nc", "A", "c", "sb", "ps", "sem"))
    sums, x3, out = env["sums"], env["nodes"], env["OUT"]
    TB = TURN_BLOCKS
    G = 3 * D
    RW = RELS + 1
    with nc.cleanup_on_exit(), ExitStack() as ctx:
        wraw = {n: sb(ctx, f"g_w_{n}_raw", [P, G // P, D]) for n in ("ih", "hh")}
        wT = {n: sb(ctx, f"g_w_{n}", [P, DC, G]) for n in ("ih", "hh")}
        rel = sb(ctx, "g_rel", [RELS, D])
        relT = sb(ctx, "g_relT", [P, DC, RELS])
        relw = sb(ctx, "g_relw", [RW, G])
        b_ih, b_hh = sb(ctx, "g_b_ih", [1, G]), sb(ctx, "g_b_hh", [1, G])
        b_hn = sb(ctx, "g_b_hn", [P, D])
        hin = sb(ctx, "g_hin", [P, TB, D])
        staged = sb(ctx, "g_staged", [P, 2, DW])
        turned = sb(ctx, "g_turned", [P, 2, 2 * DC, P])
        typT = sb(ctx, "g_typT", [RW, 2, P])
        rz = sb(ctx, "g_rz", [P, 2, 2 * D])
        cand = sb(ctx, "g_cand", [P, 2, D])
        new = sb(ctx, "g_new", [P, 2, D])
        step_h = sb(ctx, "g_step", [P, 2, D])
        p_t = [ps(ctx, f"g_p_t{k}", [P, 2 * DC, P]) for k in range(2)]
        p_y = ps(ctx, "g_p_y", [RELS, P])
        p_rz = [ps(ctx, f"g_p_rz{k}", [P, 2 * D]) for k in range(2)]
        p_n = [ps(ctx, f"g_p_n{k}", [P, 2 * D]) for k in range(2)]

        names = ("loaded", "ones", "w_turned", "w_copied", "bias", "bias_in", "staged", "turned", "copied",
                 "rz_in", "n_in", "rz_ready", "cand1", "cand2", "cand_in", "new_ready", "s1", "s2", "s3", "done")
        S = {n: sem("g_" + n) for n in names}
        h_in = [sem(f"g_h_in{k}") for k in range(TB)]
        stored = [sem(f"g_stored{k}") for k in range(TB)]

        def blk(i):
            return bass.ds(i, 1)

        def flat(t):
            return t.rearrange("p a d -> p (a d)")

        with nc.Block() as block:
            @block.sync
            def _(sp):
                for n in ("ih", "hh"):
                    sp.dma_start(wraw[n][:], A["L3_gnn_w_" + n].rearrange("(k p) d -> p k d", p=P)).then_inc(S["loaded"], 16)
                sp.dma_start(rel[:], A["L3_gnn_relvectors"]).then_inc(S["loaded"], 16)
                for t, n in ((b_ih, "ih"), (b_hh, "hh")):
                    sp.dma_start(t[:], A["L3_gnn_b_" + n].rearrange("(a d) -> a d", a=1)).then_inc(S["loaded"], 16)
                sp.dma_start(b_hn[:], A["L3_gnn_b_hh"][2 * D:G].rearrange("(a d) -> a d", a=1).broadcast_to([P, D])
                             ).then_inc(S["loaded"], 16)
                sp.wait_ge(S["bias"], 1)
                sp.dma_start(relw[RELS:RW, :], b_ih[:]).then_inc(S["bias_in"], 16)

                def load(i, k, opening, g):
                    if not opening:
                        own_wait(sp, S["done"], i - TB + 1)
                    sp.dma_start(hin[:, k:k + 1, :], rows_view(env["h3_rows"], i)).then_inc(h_in[k], 16)

                in_turns(sp, BLOCKS, TB, (0, load))

            @block.gpsimd
            def _(gp):
                nc.gpsimd.memset(typT[:], 1.0).then_inc(S["ones"], 1)

                def store(i, k, opening, g, n=P):
                    own_wait(gp, S["done"], i + 1)
                    gp.dma_start(rows_view(out, i) if n == P else out[i * P:i * P + n, :], x3[0:n, blk(i), 0:D]).then_inc(stored[k], 16)

                for k in range(TB):
                    store(k, k, True, 0)
                with gp.Fori(1, BLOCKS // TB - 1) as g:
                    for k in range(TB):
                        store(g * TB + k, k, False, g)
                for k in range(TB):
                    i = BLOCKS - TB + k
                    store(i, k, False, BLOCKS // TB - 1, min(P, NODES - i * P))
                for k in range(TB):
                    gp.wait_ge(stored[k], 16 * BLOCKS // TB)

            @block.tensor
            def _(pe):
                pe.wait_ge(S["loaded"], 16 * 6)
                n = 0
                for w in ("ih", "hh"):
                    for r in range(0, G // P, 2):
                        if n >= 2:
                            pe.wait_ge(S["w_copied"], n - 1)
                        for q in range(2):
                            for j in range(DC):
                                last = nc.tensor.transpose(p_t[n % 2][:, j * 2 + q, :], wraw[w][:, r + q, j * P:(j + 1) * P], c["ident"][:])
                        last.then_inc(S["w_turned"], 1)
                        n += 1
                pe.wait_ge(S["w_copied"], n)
                for j in range(DC):
                    last = nc.tensor.transpose(p_t[0][:, j, 0:RELS], rel[:, j * P:(j + 1) * P], c["ident"][0:RELS, 0:RELS])
                last.then_inc(S["w_turned"], 1)
                pe.wait_ge(S["w_copied"], n + 1)
                for m, (t, cs) in enumerate(((p_rz[0], slice(0, 2 * D)), (p_n[0][:, 0:D], slice(2 * D, G)))):
                    for j in range(DC):
                        last = nc.tensor.matmul(t[0:RELS], relT[:, j, :], wT["ih"][:, j, cs], start=j == 0, stop=j == DC - 1)
                    last.then_inc(S["w_turned"], 1)
                pe.wait_ge(S["w_copied"], n + 3)
                pe.wait_ge(S["bias_in"], 16)

                def turn(i, k, opening, g):
                    pe.wait_ge(S["staged"], i + 1)
                    pe.wait_ge(h_in[k], g * 16 + 16)
                    if not opening or k >= 2:
                        pe.wait_ge(S["copied"], (i - before(k) + 1) * 2)
                    for j in range(DC):
                        nc.tensor.transpose(p_t[k % 2][:, j, :], staged[:, k % 2, j * P:(j + 1) * P], c["ident"][:])
                        nc.tensor.transpose(p_t[k % 2][:, DC + j, :], hin[:, k, j * P:(j + 1) * P], c["ident"][:])
                    if not opening or k >= 1:
                        pe.wait_ge(S["copied"], i * 2)
                    nc.tensor.transpose(p_y, staged[:, k % 2, D:DW], c["ident"][:]).then_inc(S["turned"], 1)

                def gates(i, k, opening, g):
                    pe.wait_ge(S["copied"], i * 2 + 2)
                    if not opening or k >= 2:
                        pe.wait_ge(S["rz_ready"], i - before(k) + 1)
                    for n, w in enumerate(("ih", "hh")):
                        for j in range(DC):
                            nc.tensor.matmul(p_rz[k % 2], turned[:, k % 2, n * DC + j, :], wT[w][:, j, 0:2 * D],
                                             start=n + j == 0, stop=False)
                    nc.tensor.matmul(p_rz[k % 2], typT[:, k % 2, :], relw[:, 0:2 * D], start=False, stop=True).then_inc(S["rz_in"], 1)
                    if not opening or k >= 2:
                        pe.wait_ge(S["cand_in"], i - before(k) + 1)
                    for j in range(DC):
                        nc.tensor.matmul(p_n[k % 2][:, 0:D], turned[:, k % 2, j, :], wT["ih"][:, j, 2 * D:G], start=j == 0, stop=False)
                    nc.tensor.matmul(p_n[k % 2][:, 0:D], typT[:, k % 2, :], relw[:, 2 * D:G], start=False, stop=True)
                    for j in range(DC):
                        last = nc.tensor.matmul(p_n[k % 2][:, D:2 * D], turned[:, k % 2, DC + j, :], wT["hh"][:, j, 2 * D:G],
                                                start=j == 0, stop=j == DC - 1)
                    last.then_inc(S["n_in"], 1)

                in_turns(pe, BLOCKS, TB, (1, gates), (0, turn))

            @block.scalar
            def _(ac):
                n = 0
                for w in ("ih", "hh"):
                    for r in range(0, G // P, 2):
                        ac.wait_ge(S["w_turned"], n + 1)
                        nc.scalar.activation(wT[w][:, :, r * P:(r + 2) * P],
                                             p_t[n % 2].rearrange("p (j q) n -> p j (q n)", j=DC), ACT.Copy).then_inc(S["w_copied"], 1)
                        n += 1
                ac.wait_ge(S["w_turned"], n + 1)
                nc.scalar.activation(relT[:], p_t[0][:, 0:DC, 0:RELS], ACT.Copy).then_inc(S["w_copied"], 1)
                ac.wait_ge(S["w_turned"], n + 3)
                nc.scalar.activation(relw[0:RELS, 0:2 * D], p_rz[0][0:RELS, :], ACT.Copy).then_inc(S["w_copied"], 1)
                nc.scalar.activation(relw[0:RELS, 2 * D:G], p_n[0][0:RELS, 0:D], ACT.Copy).then_inc(S["w_copied"], 1)
                ac.wait_ge(S["ones"], 1)

                def stage(i, k, opening, g):
                    if not opening or k >= 2:
                        ac.wait_ge(S["turned"], i - before(k) + 1)
                    nc.scalar.activation(staged[:, k % 2, :], flat(sums[:, blk(i), :]), ACT.Copy).then_inc(S["staged"], 1)

                def copy_turned(i, k, opening, g):
                    ac.wait_ge(S["turned"], i + 1)
                    if not opening or k >= 2:
                        ac.wait_ge(S["n_in"], i - before(k) + 1)
                    nc.scalar.activation(turned[:, k % 2, :, :], p_t[k % 2], ACT.Copy).then_inc(S["copied"], 1)
                    nc.scalar.activation(typT[0:RELS, k % 2, :], p_y, ACT.Copy).then_inc(S["copied"], 1)

                def sigmoids(i, k, opening, g):
                    ac.wait_ge(S["rz_in"], i + 1)
                    if not opening or k >= 2:
                        ac.wait_ge(S["done"], i - before(k) + 1)
                    nc.scalar.activation(rz[:, k % 2, :], p_rz[k % 2], ACT.Sigmoid).then_inc(S["rz_ready"], 1)

                def candidate(i, k, opening, g):
                    ac.wait_ge(S["cand_in"], i + 1)
                    nc.scalar.activation(new[:, k % 2, :], cand[:, k % 2, :], ACT.Tanh).then_inc(S["new_ready"], 1)

                in_turns(ac, BLOCKS, TB, (3, candidate), (2, sigmoids), (1, copy_turned), (0, stage))

            @block.vector
            def _(ve):
                ve.wait_ge(S["loaded"], 16 * 6)
                nc.vector.tensor_tensor(b_ih[:, 0:2 * D], b_ih[:, 0:2 * D], b_hh[:, 0:2 * D], ALU.add).then_inc(S["bias"], 1)

                def candidate_in(i, k, opening, g):
                    ct = cand[:, k % 2, :]
                    ve.wait_ge(S["n_in"], i + 1)
                    nc.vector.tensor_tensor(ct, p_n[k % 2][:, D:2 * D], b_hn[:], ALU.add).then_inc(S["cand1"], 1)
                    ve.wait_ge(S["cand1"], i + 1)
                    ve.wait_ge(S["rz_ready"], i + 1)
                    nc.vector.tensor_tensor(ct, ct, rz[:, k % 2, 0:D], ALU.mult).then_inc(S["cand2"], 1)
                    ve.wait_ge(S["cand2"], i + 1)
                    nc.vector.tensor_tensor(ct, ct, p_n[k % 2][:, 0:D], ALU.add).then_inc(S["cand_in"], 1)

                def state(i, k, opening, g):
                    r, v = step_h[:, k % 2, :], flat(x3[:, blk(i), 0:D])
                    ve.wait_ge(S["new_ready"], i + 1)
                    nc.vector.tensor_tensor(r, hin[:, k, :], new[:, k % 2, :], ALU.subtract).then_inc(S["s1"], 1)
                    ve.wait_ge(S["s1"], i + 1)
                    nc.vector.tensor_tensor(r, r, rz[:, k % 2, D:2 * D], ALU.mult).then_inc(S["s2"], 1)
                    ve.wait_ge(S["s2"], i + 1)
                    nc.vector.tensor_tensor(r, r, new[:, k % 2, :], ALU.add).then_inc(S["s3"], 1)
                    ve.wait_ge(S["s3"], i + 1)
                    nc.vector.tensor_tensor(v, r, v, ALU.add).then_inc(S["done"], 1)

                in_turns(ve, BLOCKS, TB, (1, state), (0, candidate_in))


_OUT_SHAPE = (NODES, D)


def kernel(**inputs):
    import numpy as np
    import concourse.bacc as bacc
    from concourse.bass_utils import run_bass_kernel_spmd

    nc = bacc.Bacc("TRN2", target_bir_lowering=False, num_devices=1)
    arrays, A = {}, {}
    for name, value in inputs.items():
        a = np.ascontiguousarray(value)
        arrays["in_" + name] = a
        A[name] = nc.dram_tensor("in_" + name, a.shape, mybir.dt.from_np(a.dtype), kind="ExternalInput").ap()
    out = nc.dram_tensor("out_x", _OUT_SHAPE, F32, kind="ExternalOutput").ap()
    build(nc, A, out)
    result = run_bass_kernel_spmd(nc, [arrays], core_ids=[0])
    return result.results[0]["out_x"]
```

```python
from contextlib import ExitStack

import concourse.bass as bass
from concourse import mybir

F32 = mybir.dt.float32
BF16 = mybir.dt.bfloat16
I32 = mybir.dt.int32
U16 = mybir.dt.uint16
ALU = mybir.AluOpType
ACT = mybir.ActivationFunctionType
AX = mybir.AxisListType
SP_E, PE_E, DVE_E = mybir.EngineType.SP, mybir.EngineType.PE, mybir.EngineType.DVE

P = 128
NODES, D = 6250, 256
EDGES, ED = 100000, 128
BLOCKS = -(-NODES // P)
NODES_PAD = BLOCKS * P
LAST_ROWS = NODES - (BLOCKS - 1) * P
EP = 125
STEPS = EDGES // EP
UNROLL = 8
TILES = -(-(-(-EDGES // P) + BLOCKS) // (2 * UNROLL)) * 2 * UNROLL
TURNS = TILES // UNROLL
PAD = 2 * UNROLL
CHUNKS = -(-TILES // P)
TABLE = CHUNKS * P
BANK = 2048
REC = ED + 4
ONE, SRC, DST, WGT = ED, ED + 1, ED + 2, ED + 3
NW = D + ED + 1
DW = D + 16
TURN_BLOCKS = 6
ROUNDS = [len(range(k, BLOCKS, TURN_BLOCKS)) for k in range(TURN_BLOCKS)]
RELS = 16
BLOCK_RANGE = "a tile's block is a count of blocks (1 to BLOCKS) less one, whatever the graph"
DEG_MAX = 511
EPS = 1e-5
DC = D // P


class Counter:

    def __init__(self, eng, sem, n=0):
        self.eng, self.sem, self.n = eng, sem, n

    def mark(self, ins):
        ins.then_inc(self.sem, 1)
        self.n = self.n + 1
        return ins

    def wait(self):
        self.eng.wait_ge(self.sem, self.n)

    def link(self, ins):
        self.mark(ins)
        self.wait()


def own_wait(eng, sem, value):
    eng.wait_ge(sem, value)
    eng.nop(nofuse=True)


def in_turns(eng, count, unroll, *steps, begin=None, peeled=1):
    turns = count // unroll
    assert turns > peeled
    begin = begin or (lambda i, k: None)

    def straight(positions):
        for n in positions:
            begin(n, n % unroll)
            for lag, step in steps:
                i = n - lag
                if 0 <= i < count:
                    step(i, i % unroll, i < unroll, i // unroll)

    straight(range(peeled * unroll))
    with eng.Fori(peeled, turns) as g:
        for k in range(unroll):
            begin(g * unroll + k, k)
            for lag, step in steps:
                step(g * unroll + (k - lag), (k - lag) % unroll, False, g + (k - lag) // unroll)
    straight(range(turns * unroll, count + max(lag for lag, _ in steps)))


def row_stats(nc, d, stats, t):
    s = stats
    d.mark(nc.vector.tensor_tensor(t["msum"][:], s[:, :, 1], s[:, :, 4], ALU.add))
    d.mark(nc.vector.tensor_tensor(t["mdif"][:], s[:, :, 1], s[:, :, 4], ALU.subtract))
    d.link(nc.vector.tensor_tensor(t["m2"][:], s[:, :, 2], s[:, :, 5], ALU.add))
    d.link(nc.vector.scalar_tensor_tensor(out=t["mdif"][:], in0=t["mdif"][:], scalar=0.25, in1=t["mdif"][:],
                                          op0=ALU.mult, op1=ALU.mult))
    d.link(nc.vector.scalar_tensor_tensor(out=t["m2"][:], in0=t["m2"][:], scalar=1.0 / D, in1=t["mdif"][:],
                                          op0=ALU.mult, op1=ALU.add))
    return nc.vector.tensor_scalar(t["vare"][:], t["m2"][:], EPS, None, ALU.add)


def build(nc, A, OUT):
    with ExitStack() as whole:
        def sem(name):
            return nc.alloc_semaphore(name=name)

        def sb(ctx, name, shape, dt=F32):
            return ctx.enter_context(nc.sbuf_tensor(name, shape, dt))

        def ps(ctx, name, shape, dt=F32):
            bank = ctx.enter_context(nc.psum_tensor(name, [P, BANK // mybir.dt.size(dt)], dt))
            n = 1
            for s in shape[1:]:
                n *= s
            if len(shape) == 2:
                return bank[0:shape[0], 0:n]
            return bank[0:shape[0], 0:n].rearrange("p (a b) -> p a b", a=shape[1])

        def dram(name, shape, dt=F32):
            return nc.dram_tensor(name, shape, dt, kind="Internal").ap()

        h0_rows = dram("h0_rows", (NODES_PAD, D))
        src_records = dram("src_records", (EDGES + P, REC))
        by_dst = {n: dram(f"by_dst_{n}", (EDGES + P, 1), F32 if n == "wgt" else I32)
                  for n in ("src", "dst", "wgt", "typ")}
        table_rows = {n: dram(f"table_{n}", (TABLE, 1), I32) for n in ("sb", "ss", "db")}

        c = {}
        c["iota"] = sb(whole, "iota", [P, P])
        c["pidx"] = sb(whole, "pidx", [P, 1])
        c["ident"] = sb(whole, "ident", [P, P])
        c["ones"] = sb(whole, "ones", [P, P])
        c["indeg"] = sb(whole, "indeg", [P, BLOCKS])
        c["dloc"] = sb(whole, "dloc", [P, TILES])
        c["dsrc"] = sb(whole, "dsrc", [P, TILES])
        c["dwgt"] = sb(whole, "dwgt", [P, TILES])
        c["dtyp"] = sb(whole, "dtyp", [P, TILES])
        c["dblk"] = sb(whole, "dblk", [1, TILES + 2 * PAD], I32)
        env = dict(nc=nc, A=A, OUT=OUT, c=c, sb=sb, ps=ps, sem=sem, h0_rows=h0_rows, dram=dram,
                   src_records=src_records, by_dst=by_dst, table_rows=table_rows)
        env["x_rows"] = dram("x_rows", (NODES_PAD, D))
        env["h2_rows"] = dram("h2_rows", (NODES_PAD, D))
        env["h3_rows"] = dram("h3_rows", (NODES_PAD, D))
        prepare(env)
        with ExitStack() as mid:
            env["nodes"] = sb(mid, "nodes", [P, BLOCKS, NW])
            source_sums(env)
            layers_0_and_1(env)
            env["sums"] = sb(mid, "sums", [P, BLOCKS, DW])
            attention(env)
            layer_2(env)
            relation_sums(env)
            layer_3(env)


def prepare(env):
    nc, A, c, sb, ps, sem = (env[k] for k in ("nc", "A", "c", "sb", "ps", "sem"))
    by_dst, table_rows, src_records = env["by_dst"], env["table_rows"], env["src_records"]
    HALF = 8
    SEG = STEPS // 4
    SB = TURN_BLOCKS
    PAIRS = (BLOCKS - 1) // 2
    FIRST_PAIR = 12
    REC_TURNS = STEPS // (2 * HALF)
    with nc.cleanup_on_exit(), ExitStack() as ctx:
        X = sb(ctx, "X", [P, BLOCKS, D])
        H = sb(ctx, "H0", [P, BLOCKS, D])
        key = {s: sb(ctx, f"key_{s}", [EP, STEPS], I32) for s in ("src", "dst")}
        typ = sb(ctx, "typ", [EP, STEPS], I32)
        wgt = sb(ctx, "wgt", [EP, STEPS])
        pos = {s: sb(ctx, f"pos_{s}", [EP, STEPS]) for s in ("src", "dst")}
        hi_i = sb(ctx, "hi_i", [EP, STEPS], I32)
        hi = sb(ctx, "hi", [EP, STEPS], BF16)
        hi_d = sb(ctx, "hi_d", [EP, STEPS], BF16)
        lo_d = sb(ctx, "lo_d", [EP, STEPS])
        eq = sb(ctx, "eq", [EP, SB, SEG], U16)
        cum_seg = sb(ctx, "cum_seg", [EP, SB, SEG])
        eq_f = sb(ctx, "eq_f", [EP, 2, STEPS], BF16)
        cum = sb(ctx, "cum", [EP, STEPS])
        ones_row = sb(ctx, "ones_row", [EP, SEG], BF16)
        meta = sb(ctx, "meta", [EP, STEPS, 4])
        rec = sb(ctx, "rec", [EP, 2 * HALF, REC])
        pos_slot = sb(ctx, "pos_slot", [EP, 2 * HALF], I32)
        word_slot = sb(ctx, "word_slot", [EP, 4, 4], I32)
        pos_one = sb(ctx, "pos_one", [EP, 4], I32)
        tail = sb(ctx, "tail", [P, REC])
        tail_i = sb(ctx, "tail_i", [P, 2], I32)
        iota_i = sb(ctx, "iota_i", [P, P], I32)
        pidx_i = sb(ctx, "pidx_i", [P, 1], I32)
        tile_i = sb(ctx, "tile_i", [P, CHUNKS], I32)
        tile_f = sb(ctx, "tile_f", [P, CHUNKS])
        upper = sb(ctx, "upper", [P, P])
        iota_b = sb(ctx, "iota_b", [P, P], BF16)
        cnt = sb(ctx, "cnt", [EP, BLOCKS])
        total = sb(ctx, "total", [P, BLOCKS])
        first = sb(ctx, "first", [P, BLOCKS])
        base = sb(ctx, "base", [EP, BLOCKS])
        nt_i = sb(ctx, "nt_i", [P, BLOCKS], I32)
        nt = sb(ctx, "nt", [P, BLOCKS])
        tfirst = sb(ctx, "tfirst", [P, BLOCKS])
        shift = sb(ctx, "shift", [P, BLOCKS])
        dshift = sb(ctx, "dshift", [P, BLOCKS])
        reached = sb(ctx, "reached", [P, CHUNKS, BLOCKS])
        weighed = sb(ctx, "weighed", [P, CHUNKS, BLOCKS])
        blk_f = sb(ctx, "blk_f", [P, CHUNKS])
        start_f = sb(ctx, "start_f", [P, CHUNKS])
        blk_i = {s: sb(ctx, f"blk_i_{s}", [P, CHUNKS], I32) for s in ("src", "dst")}
        start_i = {s: sb(ctx, f"start_i_{s}", [P, CHUNKS], I32) for s in ("src", "dst")}
        stats = sb(ctx, "stats", [P, BLOCKS, 6])
        rs = {n: sb(ctx, n, [P, BLOCKS]) for n in ("msum", "mdif", "m2", "vare")}
        vare = rs["vare"]
        half = sb(ctx, "half", [P, BLOCKS])
        rstd = sb(ctx, "rstd", [P, BLOCKS])
        nmr = sb(ctx, "nmr", [P, BLOCKS])
        oh_lo = sb(ctx, "oh_lo", [EP, 8, P], BF16)
        oh_hi = sb(ctx, "oh_hi", [EP, 8, BLOCKS], BF16)
        pair = sb(ctx, "pair", [EP - 1, 2], I32)
        pair_hi = sb(ctx, "pair_hi", [EP - 1, 2], I32)
        pair_f = sb(ctx, "pair_f", [EP - 1, 2])
        falls = sb(ctx, "falls", [P, 2])
        fall_sum = sb(ctx, "fall_sum", [P, 1])
        fall_i = sb(ctx, "fall_i", [1, 1], I32)
        windows = sb(ctx, "windows", [P, 4, P], I32)
        windows_f = sb(ctx, "windows_f", [P, 4, P])
        dblk_i = sb(ctx, "dblk_i", [P, TILES], I32)

        p_total = ps(ctx, "p_total", [P, BLOCKS])
        p_base = ps(ctx, "p_base", [P, BLOCKS])
        p_deg = ps(ctx, "p_deg", [P, BLOCKS])
        p_fall = ps(ctx, "p_fall", [P, 1])
        p_win = ps(ctx, "p_win", [P, 4, P])

        loaded_x, loaded_src, loaded_rest = sem("loaded_x"), sem("loaded_src"), sem("loaded_rest")
        iotas, consts = sem("iotas"), sem("consts")
        dve, stats_ready, rstd_ready = sem("prep_dve"), sem("stats_ready"), sem("rstd_ready")
        h0_ready, h0_stored = sem("h0_ready"), sem("h0_stored")
        counted, ranked = sem("counted"), sem("ranked")
        ranked_steps, meta_ready = sem("ranked_steps"), sem("meta_ready")
        rec_loaded = [sem(f"rec_loaded{h}") for h in range(2)]
        rec_ready = sem("rec_ready")
        rec_stored = [sem(f"rec_stored{h}") for h in range(2)]
        hot_ready, hot_used = sem("hot_ready"), sem("hot_used")
        tail_ready, tail_stored = sem("tail_ready"), sem("tail_stored")
        fall_ready, fall_summed, fall_known = sem("fall_ready"), sem("fall_summed"), sem("fall_known")
        dst_ordered, slots_copied = sem("dst_ordered"), sem("slots_copied")
        win_loaded, win_cast, win_turned = sem("win_loaded"), sem("win_cast"), sem("win_turned")
        win_out = sem("win_out")
        tables_ready, tables_stored, dblk_loaded = sem("tables_ready"), sem("tables_stored"), sem("dblk_loaded")
        act = sem("prep_act")
        block_counted, matched, scanned, carried, placed = (
            sem(n) for n in ("block_counted", "matched", "scanned", "carried", "placed"))
        rel_pad = sem("x_pad")

        def grid(ap):
            return ap.rearrange("(p t) -> p t", t=STEPS)

        nfull = (BLOCKS - 1) * P

        with nc.Block() as block:
            @block.sync
            def _(sp):
                sp.dma_start(key["src"][:], grid(A["src"])).then_inc(loaded_src, 16)
                sp.dma_start(key["dst"][:], grid(A["dst"])).then_inc(loaded_rest, 16)
                sp.dma_start(wgt[:], grid(A["edge_weight"])).then_inc(loaded_rest, 16)
                sp.dma_start(typ[:], grid(A["edge_type_16"])).then_inc(loaded_rest, 16)
                sp.dma_start(pair[:], A["dst"][STEPS - 1:STEPS - 1 + (EP - 1) * STEPS]
                             .rearrange("(p t) -> p t", t=STEPS)[:, 0:2]).then_inc(loaded_rest, 16)
                attr = A["edge_attr_128"].rearrange("(p t) d -> p t d", t=STEPS)

                def load(turn, h):
                    sp.dma_start(rec[:, h * HALF:(h + 1) * HALF, 0:ED],
                                 attr[:, bass.ds(turn * 2 * HALF + h * HALF, HALF), :]
                                 ).then_inc(rec_loaded[h], 16)

                for h in range(2):
                    load(0, h)
                sp.wait_ge(rel_pad, 1)
                sp.dma_start(X[:, 0:BLOCKS - 1, :],
                             A["x"][0:nfull, :].rearrange("(i p) d -> p i d", p=P)).then_inc(loaded_x, 16)
                sp.dma_start(X[0:LAST_ROWS, BLOCKS - 1, :], A["x"][nfull:NODES, :]).then_inc(loaded_x, 16)
                with sp.Fori(1, REC_TURNS) as turn:
                    for h in range(2):
                        sp.wait_ge(rec_stored[h], turn * (16 * HALF))
                        load(turn, h)
                sp.wait_ge(h0_ready, BLOCKS)
                sp.dma_start(env["h0_rows"].rearrange("(i p) d -> p i d", p=P), H[:]).then_inc(h0_stored, 16)
                sp.wait_ge(tail_ready, 2)
                sp.dma_start(src_records[EDGES:EDGES + P, :], tail[:]).then_inc(tail_stored, 16)
                for n, col in (("src", 1), ("dst", 0), ("wgt", 1), ("typ", 1)):
                    t = tail_i[:, col:col + 1]
                    if n == "wgt":
                        t = t.bitcast(F32)
                    sp.dma_start(by_dst[n][EDGES:EDGES + P, :], t).then_inc(tail_stored, 16)
                sp.wait_ge(tables_ready, 2)
                for n, t in (("sb", blk_i["src"]), ("ss", start_i["src"]), ("db", blk_i["dst"])):
                    sp.dma_start(table_rows[n].rearrange("(c p) o -> p (c o)", p=P), t[:],
                                 allow_slow_non_contiguous=True).then_inc(tables_stored, 16)
                sp.wait_ge(tables_stored, 48)
                row = table_rows["db"][0:TILES, :].rearrange("t o -> o t")
                sp.dma_start(c["dblk"][:, PAD:PAD + TILES], row).then_inc(dblk_loaded, 16)
                sp.dma_start(dblk_i[:], row.broadcast_to([P, TILES])).then_inc(dblk_loaded, 16)
                sp.wait_ge(h0_stored, 16)
                sp.wait_ge(tail_stored, 80)
                sp.wait_ge(dblk_loaded, 32)

            @block.gpsimd
            def _(gp):
                nc.gpsimd.iota(iota_i[:], [[1, P]], base=0, channel_multiplier=0).then_inc(iotas, 1)
                nc.gpsimd.iota(pidx_i[:], [[0, 1]], base=0, channel_multiplier=1).then_inc(iotas, 1)
                nc.gpsimd.iota(tile_i[:], [[P, CHUNKS]], base=0, channel_multiplier=1).then_inc(iotas, 1)
                nc.gpsimd.memset(half[:], -0.5).then_inc(iotas, 1)
                nc.gpsimd.memset(tail[:], 0.0).then_inc(iotas, 1)
                nc.gpsimd.memset(c["dblk"][:], 0)
                gp.wait_ge(iotas, 5)
                nc.gpsimd.memset(tail[:, SRC:SRC + 1], -1.0).then_inc(tail_ready, 1)
                nc.gpsimd.memset(tail_i[:, 0:1], -1).then_inc(iotas, 1)
                nc.gpsimd.memset(tail_i[:, 1:2], 0).then_inc(iotas, 1)
                gp.wait_ge(iotas, 7)
                nc.gpsimd.memset(ones_row[:], 1.0).then_inc(tail_ready, 1)
                gp.wait_ge(loaded_rest, 64)
                nc.gpsimd.memset(meta[:, :, 0], 1.0).then_inc(meta_ready, 1)
                nc.gpsimd.tensor_copy(meta[:, :, 1], key["src"][:]).then_inc(meta_ready, 1)
                nc.gpsimd.tensor_copy(meta[:, :, 2], key["dst"][:]).then_inc(meta_ready, 1)
                nc.gpsimd.tensor_copy(meta[:, :, 3], wgt[:]).then_inc(meta_ready, 1)

                def scatter(turn, h):
                    own_wait(gp, rec_ready, turn * 2 + h + 1)
                    for k in range(h * HALF, (h + 1) * HALF):
                        gp.indirect_dma_start(out=src_records,
                                              out_offset=bass.IndirectOffsetOnAxis(ap=pos_slot[:, k:k + 1], axis=0),
                                              in_=rec[:, k, :], in_offset=None).then_inc(rec_stored[h], 16)

                def scatters(turns):
                    with gp.Fori(*turns) as turn:
                        for h in range(2):
                            scatter(turn, h)

                scatters((0, FIRST_PAIR))
                gp.wait_ge(stats_ready, 1)
                nc.gpsimd.tensor_tensor(rstd[:], vare[:], half[:], ALU.pow).then_inc(rstd_ready, 1)
                scatters((FIRST_PAIR, REC_TURNS))
                for h in range(2):
                    gp.wait_ge(rec_stored[h], STEPS // (2 * HALF) * 16 * HALF)

                gp.wait_ge(fall_known, 1)
                gp.wait_ge(ranked_steps, 2 * STEPS)
                falling = gp.alloc_register("falling")
                gp.load(falling, fall_i[0:1, 0:1])
                with gp.If_ne(falling, 0):
                    with gp.Fori(0, STEPS // 4) as turn:
                        for n, field in enumerate((key["src"], key["dst"], wgt, typ)):
                            f = field[:, bass.ds(turn * 4, 4)]
                            if n == 2:
                                f = f.bitcast(I32)
                            nc.gpsimd.tensor_copy(word_slot[:, n, :], f).then_inc(slots_copied, 1)
                        nc.gpsimd.tensor_copy(pos_one[:], pos["dst"][:, bass.ds(turn * 4, 4)]).then_inc(slots_copied, 1)
                        own_wait(gp, slots_copied, turn * 5 + 5)
                        for k in range(4):
                            for n, name in enumerate(("src", "dst", "wgt", "typ")):
                                w = word_slot[:, n, k:k + 1]
                                if name == "wgt":
                                    w = w.bitcast(F32)
                                gp.indirect_dma_start(out=by_dst[name],
                                                      out_offset=bass.IndirectOffsetOnAxis(ap=pos_one[:, k:k + 1], axis=0),
                                                      in_=w, in_offset=None).then_inc(dst_ordered, 16)
                        gp.wait_ge(dst_ordered, turn * 256 + 256)
                with gp.Else():
                    for n, name in (("src", "src"), ("dst", "dst"), ("wgt", "edge_weight"), ("typ", "edge_type_16")):
                        gp.dma_start(by_dst[n][0:EDGES, :].rearrange("(a b) o -> a (b o)", a=32),
                                     A[name].rearrange("(a b) -> a b", a=32)).then_inc(dst_ordered, 16)
                    gp.wait_ge(dst_ordered, 64)
                gp.wait_ge(tail_stored, 80)
                for ch in range(CHUNKS):
                    if ch:
                        gp.wait_ge(win_cast, ch)
                    for n, name in enumerate(("src", "dst", "wgt", "typ")):
                        w = windows[:, n, :]
                        if name == "wgt":
                            w = w.bitcast(F32)
                        gp.indirect_dma_start(out=w, out_offset=None, in_=by_dst[name],
                                              in_offset=bass.IndirectOffsetOnAxis(ap=start_i["dst"][:, ch:ch + 1], axis=0)
                                              ).then_inc(win_loaded, 16)

            @block.scalar
            def _(ac):
                def complete(turn):
                    for h in range(2):
                        step = turn * 2 * HALF + h * HALF
                        ks = slice(h * HALF, (h + 1) * HALF)
                        ac.wait_ge(rec_loaded[h], turn * 16 + 16)
                        ac.wait_ge(ranked_steps, step + HALF)
                        nc.scalar.activation(pos_slot[:, ks], pos["src"][:, bass.ds(step, HALF)], ACT.Copy).then_inc(act, 1)
                        nc.scalar.activation(rec[:, ks, ED:REC], meta[:, bass.ds(step, HALF), :], ACT.Copy).then_inc(act, 1)
                        ac.wait_ge(act, turn * 4 + h * 2 + 2)
                        ac.nop().then_inc(rec_ready, 1)

                def normalise(i):
                    nc.scalar.activation(H[:, bass.ds(i, 1), :], X[:, bass.ds(i, 1), :], ACT.Relu,
                                         bias=nmr[:, bass.ds(i, 1)], scale=rstd[:, bass.ds(i, 1)]).then_inc(h0_ready, 1)

                ac.wait_ge(meta_ready, 4)
                with ac.Fori(0, FIRST_PAIR) as turn:
                    complete(turn)
                ac.wait_ge(rstd_ready, 2)
                ac.wait_ge(loaded_x, 32)
                with ac.Fori(0, PAIRS) as pair_i:
                    complete(pair_i + FIRST_PAIR)
                    normalise(pair_i * 2)
                    normalise(pair_i * 2 + 1)
                normalise(BLOCKS - 1)
                with ac.Fori(FIRST_PAIR + PAIRS, REC_TURNS) as turn:
                    complete(turn)

            @block.tensor
            def _(pe):
                for n in range(2):
                    pe.wait_ge(counted, n + 1)
                    pe.wait_ge(consts, 1)
                    nc.tensor.matmul(p_total[:], c["ones"][0:EP, :], cnt[:], start=True, stop=True)
                    nc.tensor.matmul(p_base[:], upper[0:EP, :], cnt[:], start=True, stop=True).then_inc(ranked, 1)
                pe.wait_ge(fall_ready, 1)
                nc.tensor.matmul(p_fall[:], c["ones"][:], fall_sum[:], start=True, stop=True).then_inc(fall_summed, 1)

                def degrees(turn, opening):
                    for k in range(8):
                        pe.wait_ge(hot_ready, turn * 8 + k + 1)
                        nc.tensor.matmul(p_deg[:], oh_lo[:, k, :], oh_hi[:, k, :], start=opening and k == 0,
                                         stop=True, skip_group_check=True).then_inc(hot_used, 1)

                degrees(0, True)
                with pe.Fori(1, STEPS // 8) as turn:
                    degrees(turn, False)
                for ch in range(CHUNKS):
                    pe.wait_ge(win_cast, ch + 1)
                    if ch:
                        pe.wait_ge(win_out, ch)
                    for n in range(4):
                        last = nc.tensor.transpose(p_win[:, n, :], windows_f[:, n, :], c["ident"][:])
                    last.then_inc(win_turned, 1)

            @block.vector
            def _(ve):
                d = Counter(ve, dve)
                nc.vector.memset(X[:, BLOCKS - 1, :], 0.0).then_inc(rel_pad, 1)
                d.mark(nc.vector.memset(c["ones"][:], 1.0))
                ve.wait_ge(iotas, 5)
                d.mark(nc.vector.tensor_copy(c["iota"][:], iota_i[:]))
                d.mark(nc.vector.tensor_copy(c["pidx"][:], pidx_i[:]))
                d.link(nc.vector.tensor_copy(tile_f[:], tile_i[:]))
                d.mark(nc.vector.tensor_copy(iota_b[:], c["iota"][:]))
                d.mark(nc.vector.tensor_scalar(c["ident"][:], c["iota"][:], c["pidx"][:, 0:1], None, ALU.is_equal))
                d.link(nc.vector.tensor_scalar(upper[:], c["iota"][:], c["pidx"][:, 0:1], None, ALU.is_gt))
                nc.vector.memset(fall_sum[:], 0.0).then_inc(consts, 1)

                def rank(side, hi_t):
                    if side == "dst":
                        ve.wait_ge(loaded_rest, 64)
                    else:
                        ve.wait_ge(loaded_src, 16)
                    d.link(nc.vector.tensor_scalar(hi_i[:], key[side][:], 7, None, ALU.arith_shift_right))
                    d.link(nc.vector.tensor_copy(hi_t[:], hi_i[:]))
                    nth = 0 if side == "src" else 1

                    def count_block(i, k, opening, g):
                        if not opening or k >= 2:
                            ve.wait_ge(block_counted, i - 2 + (nth * BLOCKS + 1))
                        nc.vector.tensor_scalar(eq_f[:, k % 2, :], hi_t[:], c["iota"][0:EP, bass.ds(i, 1)], None, ALU.is_equal,
                                                op1=ALU.add, accum_out=cnt[:, bass.ds(i, 1)]).then_inc(block_counted, 1)

                    in_turns(ve, BLOCKS, SB, (0, count_block))
                    ve.wait_ge(block_counted, (nth + 1) * BLOCKS)
                    ve.nop().then_inc(counted, 1)
                    ve.wait_ge(ranked, 1 if side == "src" else 2)
                    d.link(nc.vector.tensor_copy(total[:], p_total[:]))
                    d.link(nc.vector.tensor_tensor_scan(first[:], total[:], total[:], 0.0, ALU.add, ALU.bypass))
                    d.link(nc.vector.tensor_tensor(first[:], first[:], total[:], ALU.subtract))
                    d.link(nc.vector.scalar_tensor_tensor(out=base[:], in0=p_base[0:EP, :], scalar=-1.0,
                                                          in1=first[0:EP, :], op0=ALU.add, op1=ALU.add))
                    for seg in range(STEPS // SEG):
                        cols = slice(seg * SEG, (seg + 1) * SEG)
                        n = (nth * (STEPS // SEG) + seg) * BLOCKS

                        def match(i, k, opening, g):
                            nc.vector.tensor_scalar(eq[:, k, :], hi_t[:, cols], c["iota"][0:EP, bass.ds(i, 1)], None,
                                                    ALU.is_equal).then_inc(matched, 1)

                        def count_up(i, k, opening, g):
                            ve.wait_ge(matched, i + (n + 1))
                            nc.vector.tensor_tensor_scan(cum_seg[:, k, :], ones_row[:], eq[:, k, :], base[:, bass.ds(i, 1)],
                                                         ALU.mult, ALU.add).then_inc(scanned, 1)

                        def place(i, k, opening, g):
                            ve.wait_ge(scanned, i + (n + 1))
                            own_wait(ve, placed, i + n)
                            nc.vector.copy_predicated(pos[side][:, cols], eq[:, k, :], cum_seg[:, k, :]).then_inc(placed, 1)

                        def carry(i, k, opening, g):
                            nc.vector.tensor_scalar(base[:, bass.ds(i, 1)], cum_seg[:, k, SEG - 1:SEG], 0.0, None,
                                                    ALU.add).then_inc(carried, 1)

                        in_turns(ve, BLOCKS, SB, (2, place), (2, carry), (1, count_up), (0, match))
                        ve.wait_ge(placed, n + BLOCKS)
                        ve.wait_ge(carried, n + BLOCKS)
                        ve.nop().then_inc(ranked_steps, SEG)

                def table(side):
                    d.link(nc.vector.tensor_scalar(nt[:], total[:], float(P - 1), None, ALU.add))
                    d.link(nc.vector.tensor_copy(nt_i[:], nt[:]))
                    d.link(nc.vector.tensor_scalar(nt_i[:], nt_i[:], 7, None, ALU.arith_shift_right))
                    d.link(nc.vector.tensor_copy(nt[:], nt_i[:]))
                    d.link(nc.vector.tensor_tensor_scan(tfirst[:], nt[:], nt[:], 0.0, ALU.add, ALU.bypass))
                    d.link(nc.vector.tensor_tensor(tfirst[:], tfirst[:], nt[:], ALU.subtract))
                    d.link(nc.vector.scalar_tensor_tensor(out=shift[:], in0=tfirst[:], scalar=-float(P),
                                                          in1=first[:], op0=ALU.mult, op1=ALU.add))
                    d.mark(nc.vector.tensor_copy(dshift[:, 0:1], shift[:, 0:1]))
                    d.link(nc.vector.tensor_tensor(dshift[:, 1:BLOCKS], shift[:, 1:BLOCKS],
                                                   shift[:, 0:BLOCKS - 1], ALU.subtract))
                    for ch in range(CHUNKS):
                        d.mark(nc.vector.tensor_scalar(reached[:, ch, :], tfirst[:], tile_f[:, ch:ch + 1], None, ALU.is_le))
                    d.wait()
                    for ch in range(CHUNKS):
                        d.mark(nc.vector.tensor_tensor(weighed[:, ch, :], reached[:, ch, :], dshift[:], ALU.mult))
                    d.mark(nc.vector.tensor_reduce(blk_f[:], reached[:], AX.X, ALU.add))
                    d.wait()
                    d.link(nc.vector.tensor_reduce(start_f[:], weighed[:], AX.X, ALU.add))
                    d.link(nc.vector.scalar_tensor_tensor(out=start_f[:], in0=tile_f[:], scalar=float(P),
                                                          in1=start_f[:], op0=ALU.mult, op1=ALU.add))
                    d.link(nc.vector.tensor_scalar(start_f[:], start_f[:], float(EDGES), None, ALU.min))
                    d.link(nc.vector.tensor_scalar(blk_f[:], blk_f[:], -1.0, None, ALU.add))
                    d.mark(nc.vector.tensor_copy(start_i[side][:], start_f[:]))
                    d.link(nc.vector.tensor_copy(blk_i[side][:], blk_f[:]))
                    ve.nop().then_inc(tables_ready, 1)

                ve.wait_ge(tail_ready, 2)
                rank("src", hi)

                ve.wait_ge(loaded_x, 32)
                n0 = d.n
                with ve.Fori(0, BLOCKS) as i:
                    nc.vector.bn_stats(stats[:, bass.ds(i, 1), :], X[:, bass.ds(i, 1), :]).then_inc(dve, 1)
                nc.vector.memset(falls[:], 0.0).then_inc(dve, 1)
                d.n = n0 + BLOCKS + 1
                d.wait()
                row_stats(nc, d, stats, rs).then_inc(stats_ready, 1)
                ve.wait_ge(rstd_ready, 1)
                nc.vector.scalar_tensor_tensor(out=nmr[:], in0=rs["msum"][:], scalar=-0.5, in1=rstd[:],
                                               op0=ALU.mult, op1=ALU.mult).then_inc(rstd_ready, 1)

                table("src")
                rank("dst", hi_d)
                table("dst")

                d.mark(nc.vector.tensor_tensor(cum[:, 0:STEPS - 1], hi_i[:, 0:STEPS - 1], hi_i[:, 1:STEPS], ALU.is_gt))
                d.link(nc.vector.tensor_scalar(pair_hi[:], pair[:], 7, None, ALU.arith_shift_right))
                d.mark(nc.vector.tensor_reduce(falls[0:EP, 0:1], cum[:, 0:STEPS - 1], AX.X, ALU.max))
                d.link(nc.vector.tensor_copy(pair_f[:], pair_hi[:]))
                d.link(nc.vector.tensor_tensor(falls[0:EP - 1, 1:2], pair_f[:, 0:1], pair_f[:, 1:2], ALU.is_gt))
                nc.vector.tensor_tensor(fall_sum[:], falls[:, 0:1], falls[:, 1:2], ALU.add).then_inc(fall_ready, 1)
                ve.wait_ge(fall_summed, 1)
                nc.vector.tensor_copy(fall_i[:], p_fall[0:1, :]).then_inc(fall_known, 1)

                d.link(nc.vector.tensor_scalar(hi_i[:], key["dst"][:], P - 1, None, ALU.bitwise_and))
                d.link(nc.vector.tensor_copy(lo_d[:], hi_i[:]))
                d.link(nc.vector.tensor_copy(cum[:], hi_d[:]))

                def hots(turn, opening):
                    for k in range(8):
                        if not opening:
                            ve.wait_ge(hot_used, turn * 8 + (k - 7))
                        nc.vector.tensor_scalar(oh_hi[:, k, :], iota_b[0:EP, 0:BLOCKS], cum[:, bass.ds(turn * 8 + k, 1)],
                                                None, ALU.is_equal)
                        nc.vector.tensor_scalar(oh_lo[:, k, :], iota_b[0:EP, :], lo_d[:, bass.ds(turn * 8 + k, 1)],
                                                None, ALU.is_equal).then_inc(hot_ready, 1)

                hots(0, True)
                with ve.Fori(1, STEPS // 8) as turn:
                    hots(turn, False)
                ve.wait_ge(hot_used, STEPS)
                nc.vector.tensor_copy(c["indeg"][:], p_deg[:])

                for ch in range(CHUNKS):
                    ve.wait_ge(win_loaded, 64 * (ch + 1))
                    if ch:
                        ve.wait_ge(win_turned, ch)
                    for n in (0, 1, 3):
                        nc.vector.tensor_copy(windows_f[:, n, :], windows[:, n, :])
                    nc.vector.tensor_copy(windows_f[:, 2, :], windows[:, 2, :].bitcast(F32)).then_inc(win_cast, 1)
                    ve.wait_ge(win_turned, ch + 1)
                    w = min(P, TILES - ch * P)
                    ts = slice(ch * P, ch * P + w)
                    for n, t in enumerate(("dsrc", "dloc", "dwgt", "dtyp")):
                        last = nc.vector.tensor_copy(c[t][:, ts], p_win[:, n, 0:w])
                    last.then_inc(win_out, 1)
                ve.wait_ge(dblk_loaded, 32)
                ve.wait_ge(win_out, CHUNKS)
                d.link(nc.vector.tensor_copy(cum[:], cum[:]))
                nc.vector.scalar_tensor_tensor(out=c["dloc"][:], in0=dblk_i[:], scalar=-float(P), in1=c["dloc"][:],
                                               op0=ALU.mult, op1=ALU.add)


def source_sums(env):
    nc, c, sb, ps, sem = (env[k] for k in ("nc", "c", "sb", "ps", "sem"))
    acc = env["nodes"]
    R = UNROLL
    LAG = 2
    with nc.cleanup_on_exit(), ExitStack() as ctx:
        rec = sb(ctx, "s_rec", [P, R, REC])
        row = sb(ctx, "s_row", [P, R, D])
        idx = sb(ctx, "s_idx", [P, R], I32)
        loc = sb(ctx, "s_loc", [P, R])
        hot = sb(ctx, "s_hot", [P, R, P])
        hotw = sb(ctx, "s_hotw", [P, R, P])
        blk = sb(ctx, "s_blk", [1, TILES], I32)
        start = sb(ctx, "s_start", [1, TILES], I32)
        blk_all = sb(ctx, "s_blk_all", [P, TILES], I32)
        nbase = sb(ctx, "s_nbase", [P, TILES])
        sums = [ps(ctx, f"s_sums{k}", [P, 512]) for k in range(4)]

        tables, cleared = sem("s_tables"), sem("s_cleared")
        rec_in = [sem(f"s_rec_in{k}") for k in range(R)]
        row_in = [sem(f"s_row_in{k}") for k in range(R)]
        idx_ready, loc_ready, hot_ready = sem("s_idx_ready"), sem("s_loc_ready"), sem("s_hot_ready")
        summed, added = sem("s_summed"), sem("s_added")

        with nc.Block() as block:
            @block.sync
            def _(sp):
                sp.dma_start(blk[:], env["table_rows"]["sb"][0:TILES, :].rearrange("t o -> o t")).then_inc(tables, 16)
                sp.dma_start(start[:], env["table_rows"]["ss"][0:TILES, :].rearrange("t o -> o t")).then_inc(tables, 16)
                sp.dma_start(blk_all[:], env["table_rows"]["sb"][0:TILES, :].rearrange("t o -> o t")
                             .broadcast_to([P, TILES])).then_inc(tables, 16)
                sp.wait_ge(tables, 48)

                def turn(g, opening):
                    _, firsts = nc.values_load_multi_w_load_instructions(
                        start[0:1, bass.ds(g * R, R)], engines=(SP_E,), min_val=0, max_val=EDGES)
                    for k in range(R):
                        if not opening:
                            sp.wait_ge(summed, g * R + (k - R + 1))
                        sp.dma_start(rec[:, k, :], env["src_records"][bass.ds(firsts[k], P), :]).then_inc(rec_in[k], 16)

                turn(0, True)
                with sp.Fori(1, TURNS) as g:
                    turn(g, False)

            @block.scalar
            def _(ac):
                ac.wait_ge(cleared, 2)
                with ac.Fori(0, TURNS) as g:
                    for k in range(R):
                        ac.wait_ge(rec_in[k], g * 16 + 16)
                        nc.scalar.activation(idx[:, k:k + 1], rec[:, k, DST:DST + 1], ACT.Copy).then_inc(idx_ready, 1)
                        nc.scalar.activation(loc[:, k:k + 1], rec[:, k, SRC:SRC + 1], ACT.Identity,
                                             bias=nbase[:, bass.ds(g * R + k, 1)]).then_inc(loc_ready, 1)

            @block.gpsimd
            def _(gp):
                with gp.Fori(0, TURNS) as g:
                    for k in range(R):
                        own_wait(gp, idx_ready, g * R + k + 1)
                        gp.indirect_dma_start(out=row[:, k, :], out_offset=None, in_=env["h0_rows"],
                                              in_offset=bass.IndirectOffsetOnAxis(ap=idx[:, k:k + 1], axis=0)
                                              ).then_inc(row_in[k], 16)

            @block.tensor
            def _(pe):
                def turn(g, opening):
                    for k in range(R):
                        pe.wait_ge(hot_ready, g * (2 * R) + 2 * k + 2)
                        pe.wait_ge(row_in[k], g * 16 + 16)
                        if not opening or k >= 4:
                            pe.wait_ge(added, g * R + (k - 4 + 1))
                        nc.tensor.matmul(sums[k % 4][:, 0:D], hotw[:, k, :], row[:, k, :], start=True, stop=True)
                        nc.tensor.matmul(sums[k % 4][:, D:NW], hot[:, k, :], rec[:, k, 0:ED + 1],
                                         start=True, stop=True).then_inc(summed, 1)

                turn(0, True)
                with pe.Fori(1, TURNS) as g:
                    turn(g, False)

            @block.vector
            def _(ve):
                nc.vector.memset(acc[:], 0.0).then_inc(cleared, 1)
                ve.wait_ge(tables, 48)
                nc.vector.tensor_scalar(nbase[:], blk_all[:], -float(P), None, ALU.mult).then_inc(cleared, 1)
                ve.wait_ge(cleared, 2)

                def hots(g, k):
                    ve.wait_ge(loc_ready, g * R + k + 1)
                    nc.vector.tensor_scalar(hot[:, k, :], c["iota"][:], loc[:, k:k + 1], None,
                                            ALU.is_equal).then_inc(hot_ready, 1)
                    nc.vector.tensor_scalar(hotw[:, k, :], c["iota"][:], loc[:, k:k + 1], rec[:, k, WGT:WGT + 1],
                                            ALU.is_equal, ALU.mult).then_inc(hot_ready, 1)

                def add(t, k, b):
                    ve.wait_ge(summed, t + 1)
                    ve.wait_ge(added, t)
                    s = acc[:, bass.ds(b, 1), :]
                    nc.vector.tensor_tensor(s, s, sums[k % 4][:, 0:NW].rearrange("p (a b) -> p a b", a=1),
                                            ALU.add).then_inc(added, 1)

                def turn(g, opening):
                    lo = 0 if opening else g * R - LAG
                    n = R - LAG if opening else R
                    _, blocks = nc.values_load_multi_w_load_instructions(
                        blk[0:1, bass.ds(lo, n)], engines=(DVE_E,), min_val=0, max_val=BLOCKS - 1,
                            skip_runtime_bounds_check_because=BLOCK_RANGE)
                    for k in range(R):
                        hots(g, k)
                        if not opening or k >= LAG:
                            add(g * R + (k - LAG), (k - LAG) % R, blocks[k - LAG if opening else k])

                turn(0, True)
                with ve.Fori(1, TURNS) as g:
                    turn(g, False)
                _, blocks = nc.values_load_multi_w_load_instructions(
                    blk[0:1, TILES - LAG:TILES], engines=(DVE_E,), min_val=0, max_val=BLOCKS - 1,
                            skip_runtime_bounds_check_because=BLOCK_RANGE)
                for k in range(LAG):
                    add(TILES - LAG + k, R - LAG + k, blocks[k])


def rows_view(ap, i, n=1):
    return ap[bass.ds(i * P, n * P), :].rearrange("(i p) d -> p i d", p=P)


def layers_0_and_1(env):
    nc, A, c, sb, ps, sem = (env[k] for k in ("nc", "A", "c", "sb", "ps", "sem"))
    acc = env["nodes"]
    TB = TURN_BLOCKS
    SCALE = float(D) ** -0.5
    STAGE, TURN, COPY, TIMES_W, X1, SCALE1, NORM1, X2, SCALE2, H2, TURN_H, COPY_H, TIMES_QK, Q = range(14)
    GATE_ARGS, GATES, ADD_Z, ADD_GATES = X1, SCALE1, SCALE1, NORM1
    PEELED = -(-(Q + TB) // TB)
    AHEAD = 4
    with nc.cleanup_on_exit(), ExitStack() as ctx:
        w0 = sb(ctx, "w0", [P, DC, D])
        wsum = sb(ctx, "wsum", [P, D])
        wq = sb(ctx, "wq", [P, DC, D])
        wk = sb(ctx, "wk", [P, DC, D])
        wqT = sb(ctx, "wqT", [P, DC, D])
        wkT = sb(ctx, "wkT", [P, DC, D + 1])
        bq = sb(ctx, "bq", [P, DC])
        bqs = sb(ctx, "bqs", [P, DC, P])
        qk = sb(ctx, "qk", [P, DC, D + 1])
        qkb = sb(ctx, "qkb", [P, D + 1])
        b0 = sb(ctx, "b0", [P, D])
        bsum = sb(ctx, "bsum", [P, D])
        gate = sb(ctx, "gate", [2, 2, D])
        nodes = sb(ctx, "node_vecs", [2, 2, TB * P])
        deg_f = sb(ctx, "deg_f", [P, 2, BLOCKS])
        deg = sb(ctx, "deg", [P, 2, BLOCKS], I32)
        deg_slot = sb(ctx, "deg_slot", [P, 2, TB], I32)
        xin = sb(ctx, "xin", [P, TB, D])
        z = sb(ctx, "z", [P, TB, 2, D])
        turned = sb(ctx, "turned", [P, 2, DC + 1, P])
        staged = sb(ctx, "staged", [P, 2, D + ED])
        sig = sb(ctx, "sig", [P, 2, 2 * D])
        added = sb(ctx, "added_terms", [P, TB, D])
        h1 = sb(ctx, "h1", [P, 2, D])
        h2 = sb(ctx, "h2", [P, TB, D])
        turned_h = sb(ctx, "turned_h", [P, 2, DC, P])
        half = sb(ctx, "n_half", [P, 1])
        st, mv, rstd, nmr = (sb(ctx, "n_" + n, [P, 2, TB, w]) for n, w in (("st", 6), ("mv", 2), ("rstd", 1), ("nmr", 1)))
        p_t = [ps(ctx, f"p_t{k}", [P, DC + 1, P]) for k in range(2)]
        p_o = [ps(ctx, f"p_o{k}", [P, 2 * D]) for k in range(2)]
        p_g = [ps(ctx, f"p_g{k}", [P, 2 * D]) for k in range(2)]
        p_th = ps(ctx, "p_th", [P, DC, P])
        p_q = ps(ctx, "p_q", [P, D + 1])

        bq_ready = sem("bq_ready")
        loaded, prep, prep_t = sem("n_loaded"), sem("n_prep"), sem("n_prep_t")
        x_in = [sem(f"n_x_in{k}") for k in range(TB)]
        names = ("staged", "turned", "copied", "times_w", "x_biased", "x1_ready", "edge_terms", "z_added1", "z_added",
                 "gate_added1", "terms_ready", "h1_ready", "h1_added", "x2_ready", "h2_ready", "h2_turned", "h2_copied",
                 "h2_qk", "q_ready", "gates_in", "gates_ready", "vec_ones", "vec_in", "z_slot", "deg_ready", "deg_min", "half")
        S = {n: sem("n_" + n) for n in names}
        stated, averaged, with_eps, rooted, scaled = ([sem(f"n_{n}{m}") for m in range(2)]
                                                      for n in ("stated", "averaged", "with_eps", "rooted", "scaled"))
        z_in = [sem(f"z_in{k}") for k in range(TB)]
        x2_stored = [sem(f"x2_stored{k}") for k in range(TB)]
        h2_stored = [sem(f"h2_stored{k}") for k in range(TB)]
        LOADS = 12

        def row(name):
            return A[name].rearrange("(a d) -> a d", a=1)

        def kchunks(ap):
            return ap.rearrange("(k p) d -> p k d", p=P)

        def blk(i):
            return bass.ds(i, 1)

        def flat(t):
            return t.rearrange("p a d -> p (a d)")

        with nc.Block() as block:
            @block.sync
            def _(sp):
                for t, a in ((wq, kchunks(A["L2_gnn_wq"])), (wk, kchunks(A["L2_gnn_wk"])),
                             (w0, kchunks(A["L0_gnn_weight"]))):
                    sp.dma_start(t[:], a).then_inc(loaded, 16)
                sp.dma_start(wsum[:], A["L1_gnn_W_sum"]).then_inc(loaded, 16)
                sp.dma_start(bq[:], A["L2_gnn_bq"].rearrange("(k p) -> p k", p=P),
                             allow_slow_non_contiguous=True).then_inc(loaded, 16)
                sp.dma_start(wkT[:, :, D], A["L2_gnn_bk"].rearrange("(k p) -> p k", p=P),
                             allow_slow_non_contiguous=True).then_inc(loaded, 16)
                sp.dma_start(b0[:], row("L0_gnn_b").broadcast_to([P, D])).then_inc(loaded, 16)
                sp.dma_start(bsum[:], row("L1_gnn_b_sum").broadcast_to([P, D])).then_inc(loaded, 16)
                for n, (w, b) in enumerate((("L1_gnn_W_cent", "L1_gnn_b_cent"), ("L1_gnn_W_vor", "L1_gnn_b_vor"))):
                    sp.dma_start(gate[0:1, n, :], A[w]).then_inc(loaded, 16)
                    sp.dma_start(gate[1:2, n, :], row(b)).then_inc(loaded, 16)

                def load_x(i, k, opening, g):
                    if not opening:
                        own_wait(sp, S["x1_ready"], i - TB + 1)
                    if isinstance(i, int) and i == BLOCKS - 1:
                        sp.dma_start(xin[0:LAST_ROWS, k, :], A["x"][i * P:NODES, :]).then_inc(x_in[k], 16)
                    else:
                        sp.dma_start(xin[:, k:k + 1, :], rows_view(A["x"], i)).then_inc(x_in[k], 16)

                def load_vectors(i, k, opening, g):
                    if k:
                        return
                    if opening:
                        sp.wait_ge(S["vec_ones"], 1)
                    else:
                        own_wait(sp, S["gates_in"], g * TB)
                    n = NODES - i * P if isinstance(i, int) and i + TB > BLOCKS else TB * P
                    for m, name in enumerate(("node_vec1_n2", "node_vec1")):
                        sp.dma_start(nodes[0:1, m, 0:n], A[name][bass.ds(i * P, n), :].rearrange("t o -> o t")
                                     ).then_inc(S["vec_in"], 16)

                def store_x2(i, k, opening, g):
                    if not opening:
                        own_wait(sp, x2_stored[k], g * 16)
                    own_wait(sp, S["x2_ready"], i + 1)
                    sp.dma_start(rows_view(env["x_rows"], i), acc[:, blk(i), 0:D]).then_inc(x2_stored[k], 16)

                def store_h2(i, k, opening, g):
                    own_wait(sp, S["h2_ready"], i + 1)
                    sp.dma_start(rows_view(env["h2_rows"], i), h2[:, k:k + 1, :]).then_inc(h2_stored[k], 16)

                in_turns(sp, BLOCKS, TB, (GATE_ARGS + 1, load_vectors), (0, load_x), (AHEAD + X2, store_x2),
                         (AHEAD + H2, store_h2), peeled=PEELED)
                for k in range(TB):
                    sp.wait_ge(x2_stored[k], 16 * ROUNDS[k])
                    sp.wait_ge(h2_stored[k], 16 * ROUNDS[k])

            @block.gpsimd
            def _(gp):
                nc.gpsimd.memset(nodes[:], 1.0).then_inc(S["vec_ones"], 1)
                nc.gpsimd.memset(half[:], -0.5).then_inc(S["half"], 1)
                gp.wait_ge(loaded, 16 * LOADS)
                gp.wait_ge(S["half"], 1)
                gp.wait_ge(S["deg_ready"], 1)

                def gather(i, k, opening, g):
                    if not opening:
                        own_wait(gp, S["z_added"], i - TB + 1)
                    nc.gpsimd.tensor_copy(deg_slot[:, :, k:k + 1], deg[:, :, blk(i)]).then_inc(S["z_slot"], 1)
                    own_wait(gp, S["z_slot"], i + 1)
                    for n, name in enumerate(("L1_gnn_z_in", "L1_gnn_z_out")):
                        gp.indirect_dma_start(out=z[:, k, n, :], out_offset=None, in_=A[name],
                                              in_offset=bass.IndirectOffsetOnAxis(ap=deg_slot[:, n, k:k + 1], axis=0)
                                              ).then_inc(z_in[k], 16)

                def bias_x(i, k, opening, g):
                    own_wait(gp, x_in[k], g * 16 + 16)
                    nc.gpsimd.tensor_tensor(xin[:, k, :], xin[:, k, :], b0[:], ALU.add).then_inc(S["x_biased"], 1)

                def scale(m):
                    def step(i, k, opening, g):
                        own_wait(gp, averaged[m], i + 1)
                        nc.gpsimd.tensor_scalar(mv[:, m, k, 1:2], mv[:, m, k, 1:2], EPS, None, ALU.add).then_inc(with_eps[m], 1)
                        own_wait(gp, with_eps[m], i + 1)
                        nc.gpsimd.tensor_tensor(rstd[:, m, k, :], mv[:, m, k, 1:2], half[:], ALU.pow).then_inc(rooted[m], 1)
                        own_wait(gp, rooted[m], i + 1)
                        nc.gpsimd.tensor_scalar(nmr[:, m, k, :], mv[:, m, k, 0:1], rstd[:, m, k, :], -1.0,
                                                ALU.mult, ALU.mult).then_inc(scaled[m], 1)
                    return step

                in_turns(gp, BLOCKS, TB, (SCALE2, scale(1)), (SCALE1, scale(0)), (TIMES_W, bias_x), (0, gather), peeled=PEELED)

            @block.tensor
            def _(pe):
                pe.wait_ge(loaded, 16 * LOADS)
                for n, (t, k) in enumerate((t, k) for t in (wq, wk) for k in range(DC)):
                    if n >= 2:
                        pe.wait_ge(prep, n - 1)
                    for j in range(DC):
                        last = nc.tensor.transpose(p_t[n % 2][:, j, :], t[:, k, j * P:(j + 1) * P], c["ident"][:])
                    last.then_inc(prep_t, 1)
                pe.wait_ge(prep, 4)
                pe.wait_ge(bq_ready, 1)
                for k in range(DC):
                    for j in range(DC):
                        last = nc.tensor.matmul(p_o[k][:, 0:D + 1], wqT[:, j, k * P:(k + 1) * P], wkT[:, j, :],
                                                start=j == 0, stop=j == DC - 1)
                    last.then_inc(prep_t, 1)
                for j in range(DC):
                    last = nc.tensor.matmul(p_g[0][:, 0:D + 1], bqs[:, j, :], wkT[:, j, :], start=j == 0, stop=j == DC - 1)
                last.then_inc(prep_t, 1)
                pe.wait_ge(prep, 7)

                def turn_sums(i, k, opening, g):
                    pe.wait_ge(S["staged"], i + 1)
                    if not opening or k >= 2:
                        pe.wait_ge(S["copied"], i - 1)
                    for j in range(DC + 1):
                        last = nc.tensor.transpose(p_t[k % 2][:, j, :], staged[:, k % 2, j * P:(j + 1) * P], c["ident"][:])
                    last.then_inc(S["turned"], 1)

                def times_w(i, k, opening, g):
                    pe.wait_ge(S["copied"], i + 1)
                    if not opening or k >= 2:
                        pe.wait_ge(S["edge_terms"], i - 1)
                    for j in range(DC):
                        nc.tensor.matmul(p_o[k % 2][:, 0:D], turned[:, k % 2, j, :], w0[:, j, :], start=j == 0, stop=j == DC - 1)
                    nc.tensor.matmul(p_o[k % 2][:, D:2 * D], turned[:, k % 2, DC, :], wsum[:],
                                     start=True, stop=True).then_inc(S["times_w"], 1)

                def gate_arguments(i, k, opening, g):
                    if k == 0:
                        pe.wait_ge(S["vec_in"], g * 32 + 32)
                    if not opening or k >= 2:
                        pe.wait_ge(S["gates_ready"], i - 1)
                    for n in range(2):
                        last = nc.tensor.matmul(p_g[k % 2][:, n * D:(n + 1) * D], nodes[:, n, k * P:(k + 1) * P],
                                                gate[:, n, :], start=True, stop=True)
                    last.then_inc(S["gates_in"], 1)

                def turn_h2(i, k, opening, g):
                    pe.wait_ge(S["h2_ready"], i + 1)
                    if not opening or k >= 1:
                        pe.wait_ge(S["h2_copied"], i)
                    for j in range(DC):
                        last = nc.tensor.transpose(p_th[:, j, :], h2[:, k, j * P:(j + 1) * P], c["ident"][:])
                    last.then_inc(S["h2_turned"], 1)

                def h2_times_qk(i, k, opening, g):
                    pe.wait_ge(S["h2_copied"], i + 1)
                    if not opening or k >= 1:
                        pe.wait_ge(S["q_ready"], i)
                    for j in range(DC):
                        last = nc.tensor.matmul(p_q, turned_h[:, k % 2, j, :], qk[:, j, :],
                                                start=j == 0, stop=j == DC - 1)
                    last.then_inc(S["h2_qk"], 1)

                in_turns(pe, BLOCKS, TB, (TIMES_W, times_w), (GATE_ARGS, gate_arguments), (TURN, turn_sums),
                         (TIMES_QK, h2_times_qk), (TURN_H, turn_h2), peeled=PEELED)

            @block.scalar
            def _(ac):
                for n in range(2 * DC):
                    ac.wait_ge(prep_t, n + 1)
                    t, k = (wqT, wkT)[n // DC], n % DC
                    nc.scalar.activation(t[:, :, k * P:(k + 1) * P], p_t[n % 2][:, 0:DC, :], ACT.Copy).then_inc(prep, 1)
                ac.wait_ge(prep_t, 2 * DC + 3)
                for k in range(DC):
                    nc.scalar.activation(qk[:, k, :], p_o[k][:, 0:D + 1], ACT.Copy, scale=SCALE).then_inc(prep, 1)
                nc.scalar.activation(qkb[:], p_g[0][:, 0:D + 1], ACT.Copy, scale=SCALE).then_inc(prep, 1)

                def stage(i, k, opening, g):
                    if not opening or k >= 2:
                        ac.wait_ge(S["turned"], i - 1)
                    nc.scalar.activation(staged[:, k % 2, :], flat(acc[:, blk(i), 0:D + ED]), ACT.Copy).then_inc(S["staged"], 1)

                def copy_turned(i, k, opening, g):
                    ac.wait_ge(S["turned"], i + 1)
                    if not opening or k >= 2:
                        ac.wait_ge(S["times_w"], i - 1)
                    nc.scalar.activation(turned[:, k % 2, :, :], p_t[k % 2], ACT.Copy).then_inc(S["copied"], 1)

                def gates(i, k, opening, g):
                    ac.wait_ge(S["gates_in"], i + 1)
                    if not opening or k >= 2:
                        ac.wait_ge(S["terms_ready"], i - 1)
                    nc.scalar.activation(sig[:, k % 2, :], p_g[k % 2], ACT.Sigmoid).then_inc(S["gates_ready"], 1)

                def norm_x1(i, k, opening, g):
                    if not opening or k >= 2:
                        ac.wait_ge(S["h1_added"], i - 1)
                    own_wait(ac, scaled[0], i + 1)
                    nc.scalar.activation(h1[:, k % 2, :], flat(acc[:, blk(i), 0:D]), ACT.Relu, bias=nmr[:, 0, k, :],
                                         scale=rstd[:, 0, k, :]).then_inc(S["h1_ready"], 1)

                def norm_x2(i, k, opening, g):
                    if not opening:
                        ac.wait_ge(S["h2_turned"], i - TB + 1)
                        ac.wait_ge(h2_stored[k], g * 16)
                    own_wait(ac, scaled[1], i + 1)
                    nc.scalar.activation(h2[:, k, :], flat(acc[:, blk(i), 0:D]), ACT.Relu, bias=nmr[:, 1, k, :],
                                         scale=rstd[:, 1, k, :]).then_inc(S["h2_ready"], 1)

                def copy_h2(i, k, opening, g):
                    ac.wait_ge(S["h2_turned"], i + 1)
                    if not opening or k >= 2:
                        ac.wait_ge(S["h2_qk"], i - 1)
                    nc.scalar.activation(turned_h[:, k % 2, :, :], p_th, ACT.Copy).then_inc(S["h2_copied"], 1)

                in_turns(ac, BLOCKS, TB, (COPY_H, copy_h2), (COPY, copy_turned), (GATES, gates), (NORM1, norm_x1),
                         (H2, norm_x2), (STAGE, stage), peeled=PEELED)

            @block.vector
            def _(ve):
                ve.wait_ge(loaded, 16 * LOADS)
                for j in range(DC):
                    last = nc.vector.tensor_scalar(bqs[:, j, :], c["ones"][:], bq[:, j:j + 1], None, ALU.mult)
                last.then_inc(bq_ready, 1)
                for n, t in enumerate((c["indeg"][:], acc[:, :, NW - 1])):
                    nc.vector.tensor_scalar(deg_f[:, n, :], t, float(DEG_MAX), None, ALU.min).then_inc(S["deg_min"], 1)
                ve.wait_ge(S["deg_min"], 2)
                nc.vector.tensor_copy(deg[:], deg_f[:]).then_inc(S["deg_ready"], 1)

                def value(i):
                    return flat(acc[:, blk(i), 0:D])

                def make_x1(i, k, opening, g):
                    ve.wait_ge(S["x_biased"], i + 1)
                    ve.wait_ge(S["times_w"], i + 1)
                    nc.vector.tensor_tensor(value(i), p_o[k % 2][:, 0:D], xin[:, k, :], ALU.add).then_inc(S["x1_ready"], 1)

                def edge_terms(i, k, opening, g):
                    nc.vector.scalar_tensor_tensor(out=added[:, k, :], in0=bsum[:], scalar=flat(acc[:, blk(i), NW - 1:NW]),
                                                   in1=p_o[k % 2][:, D:2 * D], op0=ALU.mult, op1=ALU.add
                                                   ).then_inc(S["edge_terms"], 1)

                def add_z(n, before, after):
                    def step(i, k, opening, g):
                        ve.wait_ge(S[before], i + 1)
                        ve.wait_ge(z_in[k], g * 32 + 32)
                        nc.vector.tensor_tensor(added[:, k, :], added[:, k, :], z[:, k, n, :], ALU.add).then_inc(S[after], 1)
                    return step

                def add_gate(n, before, after):
                    def step(i, k, opening, g):
                        ve.wait_ge(S[before], i + 1)
                        ve.wait_ge(S["gates_ready"], i + 1)
                        nc.vector.tensor_tensor(added[:, k, :], added[:, k, :], sig[:, k % 2, n * D:(n + 1) * D],
                                                ALU.add).then_inc(S[after], 1)
                    return step

                def add_h1(i, k, opening, g):
                    ve.wait_ge(S["h1_ready"], i + 1)
                    nc.vector.tensor_tensor(value(i), value(i), h1[:, k % 2, :], ALU.add).then_inc(S["h1_added"], 1)

                def make_x2(i, k, opening, g):
                    ve.wait_ge(S["h1_added"], i + 1)
                    ve.wait_ge(S["terms_ready"], i + 1)
                    nc.vector.tensor_tensor(value(i), value(i), added[:, k, :], ALU.add).then_inc(S["x2_ready"], 1)

                def statistics(m, ready):
                    def step(i, k, opening, g):
                        own_wait(ve, S[ready], i + 1)
                        nc.vector.bn_stats(st[:, m, k, :], value(i)).then_inc(stated[m], 1)
                    return step

                def average(m):
                    def step(i, k, opening, g):
                        own_wait(ve, stated[m], i + 1)
                        nc.vector.bn_aggr(mv[:, m, k, :], st[:, m, k, :]).then_inc(averaged[m], 1)
                    return step

                def make_q(i, k, opening, g):
                    ve.wait_ge(S["h2_qk"], i + 1)
                    ve.wait_ge(x2_stored[k], g * 16 + 16)
                    nc.vector.tensor_tensor(flat(acc[:, blk(i), 0:D + 1]), p_q, qkb[:], ALU.add).then_inc(S["q_ready"], 1)

                in_turns(ve, BLOCKS, TB, (Q, make_q), (X1, make_x1), (ADD_Z, add_z(0, "edge_terms", "z_added1")),
                         (X2, add_h1), (ADD_GATES, add_gate(0, "z_added", "gate_added1")), (X1, edge_terms),
                         (X2, make_x2), (X1, statistics(0, "x1_ready")), (ADD_Z, add_z(1, "z_added1", "z_added")),
                         (ADD_GATES, add_gate(1, "gate_added1", "terms_ready")), (X1, average(0)),
                         (X2, statistics(1, "x2_ready")), (X2, average(1)), peeled=PEELED)


def attention(env):
    nc, A, c, sb, ps, sem = (env[k] for k in ("nc", "A", "c", "sb", "ps", "sem"))
    query, acc = env["nodes"], env["sums"]
    R = 2 * UNROLL
    H = UNROLL
    FAR = 2.0 ** 101
    LOWEST = -1e30
    FAR_T, HOT_T, ASK, DOT, MASK, MASK_T, MAX, LOOK, EXP, SUM, ADD = range(1, 12)
    AHEAD = 4
    with nc.cleanup_on_exit(), ExitStack() as ctx:
        idx = sb(ctx, "a_idx", [P, R], I32)
        row = sb(ctx, "a_row", [P, R, D + 1])
        far = sb(ctx, "a_far", [P, H, P])
        hotT = sb(ctx, "a_hotT", [P, H, P])
        prod = sb(ctx, "a_prod", [P, 2, D + 1])
        dot = sb(ctx, "a_dot", [P, H])
        score = sb(ctx, "a_score", [P, H])
        masked = sb(ctx, "a_masked", [P, H, P])
        part = sb(ctx, "a_part", [P, H, P])
        tmax = sb(ctx, "a_tmax", [P, H])
        mnew = sb(ctx, "a_mnew", [P, H])
        drop = sb(ctx, "a_drop", [P, H])
        fade = sb(ctx, "a_fade", [P, H])
        mneg = sb(ctx, "a_mneg", [P, H])
        m = sb(ctx, "a_m", [P, BLOCKS])
        ew = sb(ctx, "a_ew", [P, TILES])
        web = sb(ctx, "a_web", [P, 2])
        p_hot = ps(ctx, "a_p_hot", [P, P])
        p_q = [ps(ctx, f"a_p_q{k}", [P, D + 1]) for k in range(2)]
        p_m = [ps(ctx, f"a_p_m{k}", [P, P]) for k in range(2)]
        p_l = ps(ctx, "a_p_l", [P, 1])
        p_s = [ps(ctx, f"a_p_s{k}", [P, D + 1]) for k in range(2)]

        names = ("loaded", "ones", "begun", "idx_ready", "far_ready", "odd_far_ready", "hot_turned", "hotT_ready", "asked",
                 "dotted", "scored", "masked", "mask_turned", "maxed", "mnew", "dropped", "m_kept", "faded",
                 "looked_up", "m_negated", "part_ready", "summed", "added")
        S = {n: sem("a_" + n) for n in names}
        row_in = [sem(f"a_row_in{k}") for k in range(R)]

        with nc.Block() as block:
            @block.sync
            def _(sp):
                sp.dma_start(web[:, 0:1], A["L2_gnn_we"].broadcast_to([P, 1])).then_inc(S["loaded"], 16)
                sp.dma_start(web[:, 1:2], A["L2_gnn_be"].rearrange("(a b) -> a b", a=1).broadcast_to([P, 1])
                             ).then_inc(S["loaded"], 16)
                sp.wait_ge(S["loaded"], 32)

            @block.gpsimd
            def _(gp):
                nc.gpsimd.memset(row[:], 1.0).then_inc(S["ones"], 1)
                gp.wait_ge(S["ones"], 1)

                def gather(i, k, opening, g):
                    if k % 4 == 0:
                        own_wait(gp, S["idx_ready"], g * (R // 4) + (k // 4 + 1))
                    if not opening:
                        own_wait(gp, S["summed"], i - R + 1)
                    gp.indirect_dma_start(out=row[:, k, 0:D], out_offset=None, in_=env["h2_rows"],
                                          in_offset=bass.IndirectOffsetOnAxis(ap=idx[:, k:k + 1], axis=0)
                                          ).then_inc(row_in[k], 16)

                in_turns(gp, TILES, R, (0, gather))

            @block.scalar
            def _(ac):
                def indices(i, k, opening, g):
                    if k % 4:
                        return
                    if not opening:
                        for j in range(k, k + 4):
                            ac.wait_ge(row_in[j], g * 16)
                    nc.scalar.activation(idx[:, k:k + 4], c["dsrc"][:, bass.ds(i, 4)], ACT.Copy).then_inc(S["idx_ready"], 1)

                def make_far(i, k, opening, g):
                    if k % 2 == 0:
                        return
                    nc.scalar.activation(far[:, k % H, :], c["iota"][:], ACT.Square, bias=c["dloc"][:, bass.ds(i, 1)],
                                         scale=-1.0).then_inc(S["odd_far_ready"], 1)

                def copy_hot(i, k, opening, g):
                    ac.wait_ge(S["hot_turned"], i + 1)
                    nc.scalar.activation(hotT[:, k % H, :], p_hot, ACT.Relu, bias=c["ones"][:, 0:1], scale=-1.0).then_inc(S["hotT_ready"], 1)

                def mask(i, k, opening, g):
                    ac.wait_ge(S["scored"], i + 1)
                    nc.scalar.activation(masked[:, k % H, :], far[:, k % H, :], ACT.Identity, scale=-FAR,
                                         bias=score[:, k % H:k % H + 1]).then_inc(S["masked"], 1)

                def exponents(i, k, opening, g):
                    ac.wait_ge(S["dropped"], i + 1)
                    nc.scalar.activation(fade[:, k % H:k % H + 1], drop[:, k % H:k % H + 1], ACT.Exp).then_inc(S["faded"], 1)
                    ac.wait_ge(S["looked_up"], i + 1)
                    nc.scalar.activation(mneg[:, k % H:k % H + 1], p_l, ACT.Copy, scale=-1.0).then_inc(S["m_negated"], 1)
                    ac.wait_ge(S["m_negated"], i + 1)
                    ac.wait_ge(S["masked"], i + 1)
                    nc.scalar.activation(part[:, k % H, :], masked[:, k % H, :], ACT.Exp,
                                         bias=mneg[:, k % H:k % H + 1]).then_inc(S["part_ready"], 1)

                in_turns(ac, TILES, R, (AHEAD + HOT_T, copy_hot), (AHEAD + EXP, exponents), (AHEAD + MASK, mask),
                         (AHEAD, make_far), (0, indices))

            @block.tensor
            def _(pe):
                blocks = []

                def load_blocks(i, k):
                    if k == 0:
                        _, blocks[:] = nc.values_load_multi_w_load_instructions(
                            c["dblk"][0:1, bass.ds(i + (PAD - ASK), R)],
                            engines=(PE_E,), min_val=0, max_val=BLOCKS - 1,
                            skip_runtime_bounds_check_because=BLOCK_RANGE)

                def turn_far(i, k, opening, g):
                    pe.wait_ge(S["odd_far_ready" if k % 2 else "far_ready"], g * (R // 2) + (k // 2 + 1))
                    if not opening or k >= 1:
                        pe.wait_ge(S["hotT_ready"], i)
                    nc.tensor.transpose(p_hot, far[:, k % H, :], c["ident"][:]).then_inc(S["hot_turned"], 1)

                def ask(i, k, opening, g):
                    pe.wait_ge(S["hotT_ready"], i + 1)
                    if not opening or k >= 2:
                        pe.wait_ge(S["dotted"], i - 1)
                    b = blocks[(k + ASK) % R]
                    nc.tensor.matmul(p_q[k % 2], hotT[:, k % H, :], query[:, bass.ds(b, 1), 0:D + 1].rearrange("p a d -> p (a d)"),
                                     start=True, stop=True).then_inc(S["asked"], 1)

                def turn_masked(i, k, opening, g):
                    pe.wait_ge(S["masked"], i + 1)
                    if not opening or k >= 2:
                        pe.wait_ge(S["maxed"], i - 1)
                    nc.tensor.transpose(p_m[k % 2], masked[:, k % H, :], c["ident"][:]).then_inc(S["mask_turned"], 1)

                def look_up(i, k, opening, g):
                    pe.wait_ge(S["mnew"], i + 1)
                    if not opening or k >= 1:
                        pe.wait_ge(S["m_negated"], i)
                    nc.tensor.matmul(p_l, hotT[:, k % H, :], mnew[:, k % H:k % H + 1], start=True, stop=True).then_inc(S["looked_up"], 1)

                def sum_rows(i, k, opening, g):
                    pe.wait_ge(S["part_ready"], i + 1)
                    pe.wait_ge(row_in[k], g * 16 + 16)
                    if not opening or k >= 2:
                        pe.wait_ge(S["added"], i - 1)
                    nc.tensor.matmul(p_s[k % 2], part[:, k % H, :], row[:, k, :], start=True, stop=True).then_inc(S["summed"], 1)

                in_turns(pe, TILES, R, (SUM, sum_rows), (ASK, ask), (MASK_T, turn_masked),
                         (LOOK, look_up), (FAR_T, turn_far), begin=load_blocks)

            @block.vector
            def _(ve):
                nc.vector.memset(acc[:], 0.0).then_inc(S["begun"], 1)
                nc.vector.memset(m[:], LOWEST).then_inc(S["begun"], 1)
                ve.wait_ge(S["loaded"], 32)
                nc.vector.tensor_scalar(ew[:], c["dwgt"][:], web[:, 0:1], web[:, 1:2], ALU.mult, ALU.add).then_inc(S["begun"], 1)
                ve.wait_ge(S["begun"], 3)
                blocks = []

                def load_blocks(i, k):
                    if k == 0:
                        _, blocks[:] = nc.values_load_multi_w_load_instructions(
                            c["dblk"][0:1, bass.ds(i + (PAD - ADD), R + ADD - MAX)],
                            engines=(DVE_E,), min_val=0, max_val=BLOCKS - 1,
                            skip_runtime_bounds_check_because=BLOCK_RANGE)

                def make_far(i, k, opening, g):
                    if k % 2 == 0:
                        nc.vector.tensor_scalar(far[:, k % H, :], c["iota"][:], c["dloc"][:, bass.ds(i, 1)], None,
                                                ALU.not_equal).then_inc(S["far_ready"], 1)

                def dots(i, k, opening, g):
                    ve.wait_ge(S["asked"], i + 1)
                    ve.wait_ge(row_in[k], g * 16 + 16)
                    nc.vector.tensor_tensor_reduce(out=prod[:, k % 2, :], in0=p_q[k % 2], in1=row[:, k, :], scale=1.0,
                                                   scalar=0.0, op0=ALU.mult, op1=ALU.add,
                                                   accum_out=dot[:, k % H:k % H + 1]).then_inc(S["dotted"], 1)

                def scores(i, k, opening, g):
                    ve.wait_ge(S["dotted"], i + 1)
                    nc.vector.tensor_tensor(score[:, k % H:k % H + 1], dot[:, k % H:k % H + 1], ew[:, bass.ds(i, 1)], ALU.add).then_inc(S["scored"], 1)

                def tile_maximum(i, k, opening, g):
                    ve.wait_ge(S["mask_turned"], i + 1)
                    nc.vector.reduce_max(tmax[:, k % H:k % H + 1], p_m[k % 2], AX.X).then_inc(S["maxed"], 1)

                def new_maximum(i, k, opening, g):
                    b = bass.ds(blocks[(k + MAX) % R + ADD - MAX], 1)
                    ve.wait_ge(S["maxed"], i + 1)
                    ve.wait_ge(S["m_kept"], i)
                    nc.vector.tensor_tensor(mnew[:, k % H:k % H + 1], m[:, b], tmax[:, k % H:k % H + 1], ALU.max).then_inc(S["mnew"], 1)

                def maximum_drop(i, k, opening, g):
                    b = bass.ds(blocks[(k + MAX) % R + ADD - MAX], 1)
                    ve.wait_ge(S["mnew"], i + 1)
                    nc.vector.tensor_tensor(drop[:, k % H:k % H + 1], m[:, b], mnew[:, k % H:k % H + 1], ALU.subtract).then_inc(S["dropped"], 1)

                def keep_maximum(i, k, opening, g):
                    b = bass.ds(blocks[(k + MAX) % R + ADD - MAX], 1)
                    ve.wait_ge(S["dropped"], i + 1)
                    nc.vector.tensor_tensor(m[:, b], m[:, b], tmax[:, k % H:k % H + 1], ALU.max).then_inc(S["m_kept"], 1)

                def add(i, k, opening, g):
                    b = blocks[(k + ADD) % R]
                    ve.wait_ge(S["summed"], i + 1)
                    ve.wait_ge(S["faded"], i + 1)
                    ve.wait_ge(S["added"], i)
                    s = acc[:, bass.ds(b, 1), 0:D + 1].rearrange("p a d -> p (a d)")
                    nc.vector.scalar_tensor_tensor(out=s, in0=s, scalar=fade[:, k % H:k % H + 1], in1=p_s[k % 2],
                                                   op0=ALU.mult, op1=ALU.add).then_inc(S["added"], 1)

                in_turns(ve, TILES, R, (MAX, tile_maximum), (ADD, add), (MAX, new_maximum),
                         (DOT, dots), (MAX, maximum_drop), (0, make_far), (DOT, scores), (MAX, keep_maximum),
                         begin=load_blocks)


def relation_sums(env):
    nc, c, sb, ps, sem = (env[k] for k in ("nc", "c", "sb", "ps", "sem"))
    acc = env["sums"]
    R = UNROLL
    LAG = 2
    with nc.cleanup_on_exit(), ExitStack() as ctx:
        idx = sb(ctx, "r_idx", [P, R], I32)
        row = sb(ctx, "r_row", [P, R, DW])
        hot = sb(ctx, "r_hot", [P, R, P])
        p_s = [ps(ctx, f"r_p_s{k}", [P, DW]) for k in range(4)]
        idx_ready, hot_ready, summed, added, cleared = (sem("r_" + n) for n in ("idx_ready", "hot_ready", "summed", "added", "cleared"))
        row_in = [sem(f"r_row_in{k}") for k in range(R)]

        with nc.Block() as block:
            @block.gpsimd
            def _(gp):
                def gather(i, k, opening, g):
                    if k % 4 == 0:
                        own_wait(gp, idx_ready, g * (R // 4) + (k // 4 + 1))
                    if not opening:
                        own_wait(gp, summed, i - R + 1)
                    gp.indirect_dma_start(out=row[:, k, 0:D], out_offset=None, in_=env["h3_rows"],
                                          in_offset=bass.IndirectOffsetOnAxis(ap=idx[:, k:k + 1], axis=0)
                                          ).then_inc(row_in[k], 16)

                in_turns(gp, TILES, R, (0, gather))

            @block.scalar
            def _(ac):
                def indices(i, k, opening, g):
                    if k % 4:
                        return
                    if not opening:
                        for j in range(k, k + 4):
                            ac.wait_ge(row_in[j], g * 16)
                    nc.scalar.activation(idx[:, k:k + 4], c["dsrc"][:, bass.ds(i, 4)], ACT.Copy).then_inc(idx_ready, 1)

                in_turns(ac, TILES, R, (0, indices))

            @block.tensor
            def _(pe):
                def sum_rows(i, k, opening, g):
                    pe.wait_ge(hot_ready, i * 2 + 2)
                    pe.wait_ge(row_in[k], g * 16 + 16)
                    if not opening or k >= 4:
                        pe.wait_ge(added, i - 3)
                    nc.tensor.matmul(p_s[k % 4], hot[:, k, :], row[:, k, :], start=True, stop=True).then_inc(summed, 1)

                in_turns(pe, TILES, R, (0, sum_rows))

            @block.vector
            def _(ve):
                nc.vector.memset(acc[:], 0.0).then_inc(cleared, 1)
                ve.wait_ge(cleared, 1)
                blocks = []

                def load_blocks(i, k):
                    if k == 0:
                        _, blocks[:] = nc.values_load_multi_w_load_instructions(
                            c["dblk"][0:1, bass.ds(i + (PAD - LAG), R + LAG)], engines=(DVE_E,), min_val=0, max_val=BLOCKS - 1,
                            skip_runtime_bounds_check_because=BLOCK_RANGE)

                def hots(i, k, opening, g):
                    if not opening:
                        ve.wait_ge(summed, i - R + 1)
                    nc.vector.tensor_scalar(hot[:, k, :], c["iota"][:], c["dloc"][:, bass.ds(i, 1)], None,
                                            ALU.is_equal).then_inc(hot_ready, 1)
                    nc.vector.tensor_scalar(row[:, k, D:DW], c["iota"][:, 0:RELS], c["dtyp"][:, bass.ds(i, 1)], None,
                                            ALU.is_equal).then_inc(hot_ready, 1)

                def add(i, k, opening, g):
                    b = blocks[LAG + (k + LAG) % R - LAG]
                    ve.wait_ge(summed, i + 1)
                    ve.wait_ge(added, i)
                    s = acc[:, bass.ds(b, 1), :].rearrange("p a d -> p (a d)")
                    nc.vector.tensor_tensor(s, s, p_s[k % 4], ALU.add).then_inc(added, 1)

                in_turns(ve, TILES, R, (LAG, add), (0, hots), begin=load_blocks)


def layer_2(env):
    nc, A, c, sb, ps, sem = (env[k] for k in ("nc", "A", "c", "sb", "ps", "sem"))
    sums = env["sums"]
    val = env["nodes"]
    TB = TURN_BLOCKS
    F = 2 * D
    FC = F // P
    STAGE, TURN, COPY, PROJECT, RES1, SCALE1, NORM1, Y, TURN_Y, COPY_Y, FF_IN, HIDDEN, FF_OUT, RES2, SCALE2, NORM2, \
        X3, SCALE3, H3 = range(19)
    PEELED = -(-(H3 + TB) // TB)
    AHEAD = 3
    with nc.cleanup_on_exit(), ExitStack() as ctx:
        wv = sb(ctx, "e_wv", [P, DC, D])
        ws = sb(ctx, "e_ws", [P, DC, D])
        w1 = sb(ctx, "e_w1", [P, DC, F])
        w2 = sb(ctx, "e_w2", [P, FC, D])
        b_ff1 = sb(ctx, "b_ff1_cols", [P, FC])
        vec = {n: sb(ctx, "e_" + n, [P, D]) for n in ("bv", "bs", "g1", "b1", "g2", "b2", "b_ff2")}
        hin = sb(ctx, "e_hin", [P, TB, D])
        xin = sb(ctx, "e_xin", [P, TB, D])
        staged = sb(ctx, "e_staged", [P, 2, D])
        turned = sb(ctx, "e_turned", [P, 2, 2 * DC, P])
        biased = sb(ctx, "e_biased", [P, 2, D])
        norm1 = sb(ctx, "e_norm1", [P, 2, D])
        y = sb(ctx, "e_y", [P, 2, D])
        turned_y = sb(ctx, "e_turned_y", [P, 2, DC, P])
        hid = sb(ctx, "e_hid", [P, 2, FC, P])
        norm2 = sb(ctx, "e_norm2", [P, 2, D])
        h3 = sb(ctx, "e_h3", [P, TB, D])
        half = sb(ctx, "e_half", [P, 1])
        inv, coef = (sb(ctx, "e_" + n, [P, BLOCKS]) for n in ("inv", "coef"))
        st, mv, rstd, nmr = (sb(ctx, "e_" + n, [P, 3, TB, w]) for n, w in (("st", 6), ("mv", 2), ("rstd", 1), ("nmr", 1)))
        p_t = ps(ctx, "e_p_t", [P, 2 * DC, P])
        p_ty = ps(ctx, "e_p_ty", [P, DC, P])
        p_o = [ps(ctx, f"e_p_o{k}", [P, D]) for k in range(2)]
        p_f = [ps(ctx, f"e_p_f{k}", [P, FC, P]) for k in range(2)]
        p_y = [ps(ctx, f"e_p_y{k}", [P, D]) for k in range(2)]

        names = ("loaded", "half", "inv_ready", "staged", "turned", "copied", "projected", "biased", "res1", "res1_done",
                 "norm1", "y_scaled", "y_ready", "y_biased", "y_turned", "y_copied", "hid_in", "hid_ready",
                 "ffn", "res2", "norm2", "x3_scaled", "x3_biased", "x3_ready", "h3_ready", "coef1")
        S = {n: sem("e_" + n) for n in names}
        stated, averaged, with_eps, rooted, scaled = ([sem(f"e_{n}{m}") for m in range(3)]
                                                      for n in ("stated", "averaged", "with_eps", "rooted", "scaled"))
        h2_in = [sem(f"e_h2_in{k}") for k in range(TB)]
        x2_in = [sem(f"e_x2_in{k}") for k in range(TB)]
        h3_stored = [sem(f"e_h3_stored{k}") for k in range(TB)]
        LOADS = 5 + len(vec)

        def row(name):
            return A[name].rearrange("(a d) -> a d", a=1)

        def kchunks(ap):
            return ap.rearrange("(k p) d -> p k d", p=P)

        def blk(i):
            return bass.ds(i, 1)

        def flat(t):
            return t.rearrange("p a d -> p (a d)")

        with nc.Block() as block:
            @block.sync
            def _(sp):
                for t, n in ((wv, "L2_gnn_wv"), (ws, "L2_gnn_ws"), (w1, "L2_gnn_w_ff1"), (w2, "L2_gnn_w_ff2")):
                    sp.dma_start(t[:], kchunks(A[n])).then_inc(S["loaded"], 16)
                sp.dma_start(b_ff1[:], A["L2_gnn_b_ff1"].rearrange("(k p) -> p k", p=P),
                             allow_slow_non_contiguous=True).then_inc(S["loaded"], 16)
                for n, t in vec.items():
                    sp.dma_start(t[:], row("L2_gnn_" + n).broadcast_to([P, D])).then_inc(S["loaded"], 16)

                def load_h2(i, k, opening, g):
                    if not opening:
                        own_wait(sp, S["res1_done"], i - TB + 1)
                    sp.dma_start(hin[:, k:k + 1, :], rows_view(env["h2_rows"], i)).then_inc(h2_in[k], 16)

                def load_x2(i, k, opening, g):
                    if not opening:
                        own_wait(sp, S["x3_ready"], i - TB + 1)
                    sp.dma_start(xin[:, k:k + 1, :], rows_view(env["x_rows"], i)).then_inc(x2_in[k], 16)

                def store_h3(i, k, opening, g):
                    own_wait(sp, S["h3_ready"], i + 1)
                    sp.dma_start(rows_view(env["h3_rows"], i), h3[:, k:k + 1, :]).then_inc(h3_stored[k], 16)

                in_turns(sp, BLOCKS, TB, (0, load_h2), (RES2, load_x2), (AHEAD + H3 + 1, store_h3), peeled=PEELED)
                for k in range(TB):
                    sp.wait_ge(h3_stored[k], 16 * ROUNDS[k])

            @block.gpsimd
            def _(gp):
                nc.gpsimd.memset(half[:], -0.5).then_inc(S["half"], 1)
                gp.wait_ge(S["half"], 1)
                gp.wait_ge(S["loaded"], 16 * LOADS)

                def add_bs(i, k, opening, g):
                    own_wait(gp, h2_in[k], g * 16 + 16)
                    if not opening or k >= 2:
                        own_wait(gp, S["res1_done"], i - 1)
                    nc.gpsimd.tensor_tensor(biased[:, k % 2, :], hin[:, k, :], vec["bs"][:], ALU.add).then_inc(S["biased"], 1)

                def scale(m):
                    def step(i, k, opening, g):
                        own_wait(gp, averaged[m], i + 1)
                        nc.gpsimd.tensor_scalar(mv[:, m, k, 1:2], mv[:, m, k, 1:2], EPS, None, ALU.add).then_inc(with_eps[m], 1)
                        own_wait(gp, with_eps[m], i + 1)
                        nc.gpsimd.tensor_tensor(rstd[:, m, k, :], mv[:, m, k, 1:2], half[:], ALU.pow).then_inc(rooted[m], 1)
                        own_wait(gp, rooted[m], i + 1)
                        nc.gpsimd.tensor_scalar(nmr[:, m, k, :], mv[:, m, k, 0:1], rstd[:, m, k, :], -1.0,
                                                ALU.mult, ALU.mult).then_inc(scaled[m], 1)
                    return step

                in_turns(gp, BLOCKS, TB, (SCALE3, scale(2)), (SCALE2, scale(1)), (SCALE1, scale(0)), (PROJECT, add_bs),
                         peeled=PEELED)

            @block.tensor
            def _(pe):
                pe.wait_ge(S["loaded"], 16 * LOADS)

                def turn_rows(i, k, opening, g):
                    pe.wait_ge(S["staged"], i + 1)
                    pe.wait_ge(h2_in[k], g * 16 + 16)
                    if not opening or k >= 1:
                        pe.wait_ge(S["copied"], i)
                    for j in range(DC):
                        nc.tensor.transpose(p_t[:, j, :], staged[:, k % 2, j * P:(j + 1) * P], c["ident"][:])
                        last = nc.tensor.transpose(p_t[:, DC + j, :], hin[:, k, j * P:(j + 1) * P], c["ident"][:])
                    last.then_inc(S["turned"], 1)

                def project(i, k, opening, g):
                    pe.wait_ge(S["copied"], i + 1)
                    if not opening or k >= 2:
                        pe.wait_ge(S["res1"], i - 1)
                    for n, w in enumerate((wv, ws)):
                        for j in range(DC):
                            last = nc.tensor.matmul(p_o[k % 2], turned[:, k % 2, n * DC + j, :], w[:, j, :],
                                                    start=n + j == 0, stop=n + j == DC)
                    last.then_inc(S["projected"], 1)

                def turn_y(i, k, opening, g):
                    pe.wait_ge(S["y_ready"], i + 1)
                    if not opening or k >= 1:
                        pe.wait_ge(S["y_copied"], i)
                    for j in range(DC):
                        last = nc.tensor.transpose(p_ty[:, j, :], y[:, k % 2, j * P:(j + 1) * P], c["ident"][:])
                    last.then_inc(S["y_turned"], 1)

                def ffn_in(i, k, opening, g):
                    pe.wait_ge(S["y_copied"], i + 1)
                    if not opening or k >= 2:
                        pe.wait_ge(S["hid_ready"], (i - 1) * FC)
                    for f in range(FC):
                        for j in range(DC):
                            last = nc.tensor.matmul(p_f[k % 2][:, f, :], w1[:, j, f * P:(f + 1) * P],
                                                    turned_y[:, k % 2, j, :], start=j == 0, stop=j == DC - 1)
                    last.then_inc(S["hid_in"], 1)

                def ffn_out(i, k, opening, g):
                    pe.wait_ge(S["hid_ready"], (i + 1) * FC)
                    if not opening or k >= 2:
                        pe.wait_ge(S["res2"], i - 1)
                    for f in range(FC):
                        last = nc.tensor.matmul(p_y[k % 2], hid[:, k % 2, f, :], w2[:, f, :], start=f == 0, stop=f == FC - 1)
                    last.then_inc(S["ffn"], 1)

                in_turns(pe, BLOCKS, TB, (FF_OUT, ffn_out), (FF_IN, ffn_in), (PROJECT, project), (TURN_Y, turn_y),
                         (TURN, turn_rows), peeled=PEELED)

            @block.scalar
            def _(ac):
                ac.wait_ge(S["inv_ready"], 2)

                def stage(i, k, opening, g):
                    if not opening or k >= 2:
                        ac.wait_ge(S["turned"], i - 1)
                    nc.scalar.activation(staged[:, k % 2, :], flat(sums[:, blk(i), 0:D]), ACT.Copy,
                                         scale=inv[:, blk(i)]).then_inc(S["staged"], 1)

                def copy_rows(i, k, opening, g):
                    ac.wait_ge(S["turned"], i + 1)
                    if not opening or k >= 2:
                        ac.wait_ge(S["projected"], i - 1)
                    nc.scalar.activation(turned[:, k % 2, :, :], p_t, ACT.Copy).then_inc(S["copied"], 1)

                def normalise(m, slots, used, out):
                    def step(i, k, opening, g):
                        if not opening or k >= 2:
                            ac.wait_ge(S[used], i - 1)
                        own_wait(ac, scaled[m], i + 1)
                        nc.scalar.activation(slots[:, k % 2, :], flat(val[:, blk(i), 0:D]), ACT.Identity,
                                             bias=nmr[:, m, k, :], scale=rstd[:, m, k, :]).then_inc(S[out], 1)
                    return step

                def copy_y(i, k, opening, g):
                    ac.wait_ge(S["y_turned"], i + 1)
                    if not opening or k >= 2:
                        ac.wait_ge(S["hid_in"], i - 1)
                    nc.scalar.activation(turned_y[:, k % 2, :, :], p_ty, ACT.Copy).then_inc(S["y_copied"], 1)

                def hidden(i, k, opening, g):
                    ac.wait_ge(S["hid_in"], i + 1)
                    if not opening or k >= 2:
                        ac.wait_ge(S["ffn"], i - 1)
                    for f in range(FC):
                        nc.scalar.activation(hid[:, k % 2, f, :], p_f[k % 2][:, f, :], ACT.Gelu_apprx_tanh,
                                             bias=b_ff1[:, f:f + 1]).then_inc(S["hid_ready"], 1)

                def norm_x3(i, k, opening, g):
                    if not opening:
                        ac.wait_ge(h3_stored[k], g * 16)
                    own_wait(ac, scaled[2], i + 1)
                    nc.scalar.activation(h3[:, k, :], flat(val[:, blk(i), 0:D]), ACT.Relu, bias=nmr[:, 2, k, :],
                                         scale=rstd[:, 2, k, :]).then_inc(S["h3_ready"], 1)

                in_turns(ac, BLOCKS, TB, (COPY_Y, copy_y), (COPY, copy_rows), (HIDDEN, hidden),
                         (NORM1, normalise(0, norm1, "y_scaled", "norm1")), (NORM2, normalise(1, norm2, "x3_scaled", "norm2")),
                         (H3, norm_x3), (STAGE, stage), peeled=PEELED)

            @block.vector
            def _(ve):
                nc.vector.tensor_scalar(coef[:], sums[:, :, D], 1e-12, None, ALU.max).then_inc(S["coef1"], 1)
                ve.wait_ge(S["coef1"], 1)
                nc.vector.reciprocal(inv[:], coef[:]).then_inc(S["inv_ready"], 1)
                ve.wait_ge(S["inv_ready"], 1)
                nc.vector.tensor_tensor(coef[:], sums[:, :, D], inv[:], ALU.mult).then_inc(S["inv_ready"], 1)
                ve.wait_ge(S["inv_ready"], 2)
                ve.wait_ge(S["loaded"], 16 * LOADS)

                def value(i):
                    return flat(val[:, blk(i), 0:D])

                def residual(i, k, opening, g):
                    ve.wait_ge(S["projected"], i + 1)
                    ve.wait_ge(S["biased"], i + 1)
                    nc.vector.tensor_tensor(value(i), p_o[k % 2], biased[:, k % 2, :], ALU.add).then_inc(S["res1"], 1)

                def residual_bv(i, k, opening, g):
                    ve.wait_ge(S["res1"], i + 1)
                    nc.vector.scalar_tensor_tensor(out=value(i), in0=vec["bv"][:], scalar=coef[:, blk(i)], in1=value(i),
                                                   op0=ALU.mult, op1=ALU.add).then_inc(S["res1_done"], 1)

                def statistics(m, ready):
                    def step(i, k, opening, g):
                        own_wait(ve, S[ready], i + 1)
                        nc.vector.bn_stats(st[:, m, k, :], value(i)).then_inc(stated[m], 1)
                    return step

                def average(m):
                    def step(i, k, opening, g):
                        own_wait(ve, stated[m], i + 1)
                        nc.vector.bn_aggr(mv[:, m, k, :], st[:, m, k, :]).then_inc(averaged[m], 1)
                    return step

                def scale_y(i, k, opening, g):
                    ve.wait_ge(S["norm1"], i + 1)
                    if not opening or k >= 2:
                        ve.wait_ge(S["y_turned"], i - 1)
                    nc.vector.tensor_tensor(y[:, k % 2, :], norm1[:, k % 2, :], vec["g1"][:], ALU.mult).then_inc(S["y_scaled"], 1)

                def make_y(i, k, opening, g):
                    ve.wait_ge(S["y_scaled"], i + 1)
                    nc.vector.tensor_tensor(y[:, k % 2, :], y[:, k % 2, :], vec["b1"][:], ALU.add).then_inc(S["y_ready"], 1)

                def bias_y(i, k, opening, g):
                    ve.wait_ge(S["y_ready"], i + 1)
                    nc.vector.tensor_tensor(value(i), y[:, k % 2, :], vec["b_ff2"][:], ALU.add).then_inc(S["y_biased"], 1)

                def residual2(i, k, opening, g):
                    ve.wait_ge(S["y_biased"], i + 1)
                    ve.wait_ge(S["ffn"], i + 1)
                    nc.vector.tensor_tensor(value(i), value(i), p_y[k % 2], ALU.add).then_inc(S["res2"], 1)

                def scale_x3(i, k, opening, g):
                    ve.wait_ge(S["norm2"], i + 1)
                    nc.vector.tensor_tensor(value(i), norm2[:, k % 2, :], vec["g2"][:], ALU.mult).then_inc(S["x3_scaled"], 1)

                def bias_x3(i, k, opening, g):
                    ve.wait_ge(S["x3_scaled"], i + 1)
                    nc.vector.tensor_tensor(value(i), value(i), vec["b2"][:], ALU.add).then_inc(S["x3_biased"], 1)

                def make_x3(i, k, opening, g):
                    ve.wait_ge(S["x3_biased"], i + 1)
                    ve.wait_ge(x2_in[k], g * 16 + 16)
                    nc.vector.tensor_tensor(value(i), value(i), xin[:, k, :], ALU.add).then_inc(S["x3_ready"], 1)

                in_turns(ve, BLOCKS, TB, (X3, scale_x3), (RES2, residual2), (RES1, residual), (X3, bias_x3), (Y, scale_y),
                         (RES1, residual_bv), (X3, make_x3), (Y, make_y), (RES2, statistics(1, "res2")),
                         (RES1, statistics(0, "res1_done")), (Y, bias_y), (X3, statistics(2, "x3_ready")),
                         (RES2, average(1)), (RES1, average(0)), (X3, average(2)), peeled=PEELED)


def layer_3(env):
    nc, A, c, sb, ps, sem = (env[k] for k in ("nc", "A", "c", "sb", "ps", "sem"))
    sums, x3, out = env["sums"], env["nodes"], env["OUT"]
    TB = TURN_BLOCKS
    G = 3 * D
    RW = RELS + 1
    with nc.cleanup_on_exit(), ExitStack() as ctx:
        wraw = {n: sb(ctx, f"g_w_{n}_raw", [P, G // P, D]) for n in ("ih", "hh")}
        wT = {n: sb(ctx, f"g_w_{n}", [P, DC, G]) for n in ("ih", "hh")}
        rel = sb(ctx, "g_rel", [RELS, D])
        relT = sb(ctx, "g_relT", [P, DC, RELS])
        relw = sb(ctx, "g_relw", [RW, G])
        b_ih, b_hh = sb(ctx, "g_b_ih", [1, G]), sb(ctx, "g_b_hh", [1, G])
        b_hn = sb(ctx, "g_b_hn", [P, D])
        hin = sb(ctx, "g_hin", [P, TB, D])
        staged = sb(ctx, "g_staged", [P, 2, DW])
        turned = sb(ctx, "g_turned", [P, 2, 2 * DC, P])
        typT = sb(ctx, "g_typT", [RW, 2, P])
        rz = sb(ctx, "g_rz", [P, 2, 2 * D])
        cand = sb(ctx, "g_cand", [P, 2, D])
        new = sb(ctx, "g_new", [P, 2, D])
        step_h = sb(ctx, "g_step", [P, 2, D])
        p_t = [ps(ctx, f"g_p_t{k}", [P, 2 * DC, P]) for k in range(2)]
        p_y = ps(ctx, "g_p_y", [RELS, P])
        p_rz = [ps(ctx, f"g_p_rz{k}", [P, 2 * D]) for k in range(2)]
        p_n = [ps(ctx, f"g_p_n{k}", [P, 2 * D]) for k in range(2)]

        names = ("loaded", "ones", "w_turned", "w_copied", "bias", "bias_in", "staged", "turned", "copied",
                 "rz_in", "n_in", "rz_ready", "cand1", "cand2", "cand_in", "new_ready", "s1", "s2", "s3", "done")
        S = {n: sem("g_" + n) for n in names}
        h_in = [sem(f"g_h_in{k}") for k in range(TB)]
        stored = [sem(f"g_stored{k}") for k in range(TB)]

        def blk(i):
            return bass.ds(i, 1)

        def flat(t):
            return t.rearrange("p a d -> p (a d)")

        with nc.Block() as block:
            @block.sync
            def _(sp):
                for n in ("ih", "hh"):
                    sp.dma_start(wraw[n][:], A["L3_gnn_w_" + n].rearrange("(k p) d -> p k d", p=P)).then_inc(S["loaded"], 16)
                sp.dma_start(rel[:], A["L3_gnn_relvectors"]).then_inc(S["loaded"], 16)
                for t, n in ((b_ih, "ih"), (b_hh, "hh")):
                    sp.dma_start(t[:], A["L3_gnn_b_" + n].rearrange("(a d) -> a d", a=1)).then_inc(S["loaded"], 16)
                sp.dma_start(b_hn[:], A["L3_gnn_b_hh"][2 * D:G].rearrange("(a d) -> a d", a=1).broadcast_to([P, D])
                             ).then_inc(S["loaded"], 16)
                sp.wait_ge(S["bias"], 1)
                sp.dma_start(relw[RELS:RW, :], b_ih[:]).then_inc(S["bias_in"], 16)

                def load(i, k, opening, g):
                    if not opening:
                        own_wait(sp, S["done"], i - TB + 1)
                    sp.dma_start(hin[:, k:k + 1, :], rows_view(env["h3_rows"], i)).then_inc(h_in[k], 16)

                in_turns(sp, BLOCKS, TB, (0, load))

            @block.gpsimd
            def _(gp):
                nc.gpsimd.memset(typT[:], 1.0).then_inc(S["ones"], 1)

                def store(i, k, opening, g):
                    n = LAST_ROWS if isinstance(i, int) and i == BLOCKS - 1 else P
                    own_wait(gp, S["done"], i + 1)
                    gp.dma_start(rows_view(out, i) if n == P else out[i * P:i * P + n, :], x3[0:n, blk(i), 0:D]).then_inc(stored[k], 16)

                in_turns(gp, BLOCKS, TB, (0, store))
                for k in range(TB):
                    gp.wait_ge(stored[k], 16 * ROUNDS[k])

            @block.tensor
            def _(pe):
                pe.wait_ge(S["loaded"], 16 * 6)
                n = 0
                for w in ("ih", "hh"):
                    for r in range(0, G // P, 2):
                        if n >= 2:
                            pe.wait_ge(S["w_copied"], n - 1)
                        for q in range(2):
                            for j in range(DC):
                                last = nc.tensor.transpose(p_t[n % 2][:, j * 2 + q, :], wraw[w][:, r + q, j * P:(j + 1) * P], c["ident"][:])
                        last.then_inc(S["w_turned"], 1)
                        n += 1
                pe.wait_ge(S["w_copied"], n)
                for j in range(DC):
                    last = nc.tensor.transpose(p_t[0][:, j, 0:RELS], rel[:, j * P:(j + 1) * P], c["ident"][0:RELS, 0:RELS])
                last.then_inc(S["w_turned"], 1)
                pe.wait_ge(S["w_copied"], n + 1)
                for m, (t, cs) in enumerate(((p_rz[0], slice(0, 2 * D)), (p_n[0][:, 0:D], slice(2 * D, G)))):
                    for j in range(DC):
                        last = nc.tensor.matmul(t[0:RELS], relT[:, j, :], wT["ih"][:, j, cs], start=j == 0, stop=j == DC - 1)
                    last.then_inc(S["w_turned"], 1)
                pe.wait_ge(S["w_copied"], n + 3)
                pe.wait_ge(S["bias_in"], 16)

                def turn(i, k, opening, g):
                    pe.wait_ge(S["staged"], i + 1)
                    pe.wait_ge(h_in[k], g * 16 + 16)
                    if not opening or k >= 2:
                        pe.wait_ge(S["copied"], (i - 1) * 2)
                    for j in range(DC):
                        nc.tensor.transpose(p_t[k % 2][:, j, :], staged[:, k % 2, j * P:(j + 1) * P], c["ident"][:])
                        nc.tensor.transpose(p_t[k % 2][:, DC + j, :], hin[:, k, j * P:(j + 1) * P], c["ident"][:])
                    if not opening or k >= 1:
                        pe.wait_ge(S["copied"], i * 2)
                    nc.tensor.transpose(p_y, staged[:, k % 2, D:DW], c["ident"][:]).then_inc(S["turned"], 1)

                def gates(i, k, opening, g):
                    pe.wait_ge(S["copied"], i * 2 + 2)
                    if not opening or k >= 2:
                        pe.wait_ge(S["rz_ready"], i - 1)
                    for n, w in enumerate(("ih", "hh")):
                        for j in range(DC):
                            nc.tensor.matmul(p_rz[k % 2], turned[:, k % 2, n * DC + j, :], wT[w][:, j, 0:2 * D],
                                             start=n + j == 0, stop=False)
                    nc.tensor.matmul(p_rz[k % 2], typT[:, k % 2, :], relw[:, 0:2 * D], start=False, stop=True).then_inc(S["rz_in"], 1)
                    if not opening or k >= 2:
                        pe.wait_ge(S["cand_in"], i - 1)
                    for j in range(DC):
                        nc.tensor.matmul(p_n[k % 2][:, 0:D], turned[:, k % 2, j, :], wT["ih"][:, j, 2 * D:G], start=j == 0, stop=False)
                    nc.tensor.matmul(p_n[k % 2][:, 0:D], typT[:, k % 2, :], relw[:, 2 * D:G], start=False, stop=True)
                    for j in range(DC):
                        last = nc.tensor.matmul(p_n[k % 2][:, D:2 * D], turned[:, k % 2, DC + j, :], wT["hh"][:, j, 2 * D:G],
                                                start=j == 0, stop=j == DC - 1)
                    last.then_inc(S["n_in"], 1)

                in_turns(pe, BLOCKS, TB, (3, gates), (1, turn), peeled=2)

            @block.scalar
            def _(ac):
                n = 0
                for w in ("ih", "hh"):
                    for r in range(0, G // P, 2):
                        ac.wait_ge(S["w_turned"], n + 1)
                        nc.scalar.activation(wT[w][:, :, r * P:(r + 2) * P],
                                             p_t[n % 2].rearrange("p (j q) n -> p j (q n)", j=DC), ACT.Copy).then_inc(S["w_copied"], 1)
                        n += 1
                ac.wait_ge(S["w_turned"], n + 1)
                nc.scalar.activation(relT[:], p_t[0][:, 0:DC, 0:RELS], ACT.Copy).then_inc(S["w_copied"], 1)
                ac.wait_ge(S["w_turned"], n + 3)
                nc.scalar.activation(relw[0:RELS, 0:2 * D], p_rz[0][0:RELS, :], ACT.Copy).then_inc(S["w_copied"], 1)
                nc.scalar.activation(relw[0:RELS, 2 * D:G], p_n[0][0:RELS, 0:D], ACT.Copy).then_inc(S["w_copied"], 1)
                ac.wait_ge(S["ones"], 1)

                def stage(i, k, opening, g):
                    if not opening or k >= 2:
                        ac.wait_ge(S["turned"], i - 1)
                    nc.scalar.activation(staged[:, k % 2, :], flat(sums[:, blk(i), :]), ACT.Copy).then_inc(S["staged"], 1)

                def copy_turned(i, k, opening, g):
                    ac.wait_ge(S["turned"], i + 1)
                    if not opening or k >= 2:
                        ac.wait_ge(S["n_in"], i - 1)
                    nc.scalar.activation(turned[:, k % 2, :, :], p_t[k % 2], ACT.Copy).then_inc(S["copied"], 1)
                    nc.scalar.activation(typT[0:RELS, k % 2, :], p_y, ACT.Copy).then_inc(S["copied"], 1)

                def sigmoids(i, k, opening, g):
                    ac.wait_ge(S["rz_in"], i + 1)
                    if not opening or k >= 2:
                        ac.wait_ge(S["done"], i - 1)
                    nc.scalar.activation(rz[:, k % 2, :], p_rz[k % 2], ACT.Sigmoid).then_inc(S["rz_ready"], 1)

                def candidate(i, k, opening, g):
                    ac.wait_ge(S["cand_in"], i + 1)
                    nc.scalar.activation(new[:, k % 2, :], cand[:, k % 2, :], ACT.Tanh).then_inc(S["new_ready"], 1)

                in_turns(ac, BLOCKS, TB, (6, candidate), (4, sigmoids), (2, copy_turned), (0, stage), peeled=2)

            @block.vector
            def _(ve):
                ve.wait_ge(S["loaded"], 16 * 6)
                nc.vector.tensor_tensor(b_ih[:, 0:2 * D], b_ih[:, 0:2 * D], b_hh[:, 0:2 * D], ALU.add).then_inc(S["bias"], 1)

                def candidate_in(i, k, opening, g):
                    ct = cand[:, k % 2, :]
                    ve.wait_ge(S["n_in"], i + 1)
                    nc.vector.tensor_tensor(ct, p_n[k % 2][:, D:2 * D], b_hn[:], ALU.add).then_inc(S["cand1"], 1)
                    ve.wait_ge(S["cand1"], i + 1)
                    ve.wait_ge(S["rz_ready"], i + 1)
                    nc.vector.tensor_tensor(ct, ct, rz[:, k % 2, 0:D], ALU.mult).then_inc(S["cand2"], 1)
                    ve.wait_ge(S["cand2"], i + 1)
                    nc.vector.tensor_tensor(ct, ct, p_n[k % 2][:, 0:D], ALU.add).then_inc(S["cand_in"], 1)

                def state(i, k, opening, g):
                    r, v = step_h[:, k % 2, :], flat(x3[:, blk(i), 0:D])
                    ve.wait_ge(S["new_ready"], i + 1)
                    nc.vector.tensor_tensor(r, hin[:, k, :], new[:, k % 2, :], ALU.subtract).then_inc(S["s1"], 1)
                    ve.wait_ge(S["s1"], i + 1)
                    nc.vector.tensor_tensor(r, r, rz[:, k % 2, D:2 * D], ALU.mult).then_inc(S["s2"], 1)
                    ve.wait_ge(S["s2"], i + 1)
                    nc.vector.tensor_tensor(r, r, new[:, k % 2, :], ALU.add).then_inc(S["s3"], 1)
                    ve.wait_ge(S["s3"], i + 1)
                    nc.vector.tensor_tensor(v, r, v, ALU.add).then_inc(S["done"], 1)

                in_turns(ve, BLOCKS, TB, (6, state), (5, candidate_in), peeled=2)


_OUT_SHAPE = (NODES, D)


def kernel(**inputs):
    import numpy as np
    import concourse.bacc as bacc
    from concourse.bass_utils import run_bass_kernel_spmd

    nc = bacc.Bacc("TRN2", target_bir_lowering=False, num_devices=1)
    arrays, A = {}, {}
    for name, value in inputs.items():
        a = np.ascontiguousarray(value)
        arrays["in_" + name] = a
        A[name] = nc.dram_tensor("in_" + name, a.shape, mybir.dt.from_np(a.dtype), kind="ExternalInput").ap()
    out = nc.dram_tensor("out_x", _OUT_SHAPE, F32, kind="ExternalOutput").ap()
    build(nc, A, out)
    result = run_bass_kernel_spmd(nc, [arrays], core_ids=[0])
    return result.results[0]["out_x"]
```
